# Optimizing a Trainium2 kernel written in Bass

```python
import numpy as np
import jax
import jax.numpy as jnp

def _softmax(x, axis=-1):
    return jax.nn.softmax(x, axis=axis)

def _gelu(x):
    return jax.nn.gelu(x, approximate=True)

def _silu(x):
    return jax.nn.silu(x)

def _sigmoid(x):
    return jax.nn.sigmoid(x)

def _layernorm(x, axis=-1, eps=1e-05):
    m = jnp.mean(x, axis=axis, keepdims=True)
    v = jnp.var(x, axis=axis, keepdims=True)
    return (x - m) / jnp.sqrt(v + eps)

def _scatter_add(tgt, idx, src, axis=0):
    return tgt.at[idx].add(src)

def _segment_sum(src, seg, n):
    return jax.ops.segment_sum(src, seg, n)
kernel_name = 'mk_pixart_seq_d4_seqx_r8_956edc'

def setup_inputs(seed: int=0):
    np.random.seed(seed)
    _w = jnp.asarray

    def _rec_inputs():
        import jax
        import jax.numpy as jnp
        _rk = jax.random.key(seed)
        x = 7.22e-05 + 1 * jax.random.normal(jax.random.fold_in(_rk, 1), (8, 128, 128), jnp.float32)
        _lenS = 128 - jax.random.randint(jax.random.fold_in(_rk, 7), (8,), 0, max(1, 128 // 4) + 1, jnp.int32)
        _lenS2 = 120 - jax.random.randint(jax.random.fold_in(_rk, 8), (8,), 0, max(1, 120 // 4) + 1, jnp.int32)
        cond_1024 = 0.000887014 + 1.03683 * jax.random.normal(jax.random.fold_in(_rk, 11), (8, 128), jnp.float32)
        _ctx_1024P = jax.random.normal(jax.random.fold_in(_rk, 12), (8, 16, 128), jnp.float32)
        _ctx_1024c = jax.random.dirichlet(jax.random.fold_in(_rk, 512), 0.3 * jnp.ones((16,), jnp.float32), (8, 120))
        _ctx_1024t = jnp.einsum('bsk,bkd->bsd', _ctx_1024c, _ctx_1024P)
        _ctx_1024t = _ctx_1024t * jax.lax.rsqrt(jnp.mean(jnp.square(_ctx_1024t)) + 1e-12) * 0.953939
        ctx_1024 = 0.00086875 + 0.999764 * (_ctx_1024t + 0.3 * jax.random.normal(jax.random.fold_in(_rk, 612), (8, 120, 128), jnp.float32))
        return (x, cond_1024, ctx_1024)
    x, cond_1024, ctx_1024 = _rec_inputs()

    def _L0_xcond_setup():
        import jax, jax.numpy as jnp
        import numpy as np
        C = 128
        H = 16
        D = C // H
        WIN = 64
        SHIFT = 32
        TOPK = 16
        HID = 512
        EPS = 1e-06

        def _ln(x):
            x32 = x.astype(jnp.float32)
            m = x32.mean(-1, keepdims=True)
            v = jnp.mean((x32 - m) ** 2, axis=-1, keepdims=True)
            return ((x32 - m) * jax.lax.rsqrt(v + EPS)).astype(x.dtype)

        def _self_attn(h, w_qkv, b_qkv, w_so, b_so):
            B, L, _ = h.shape
            qkv = h @ w_qkv + b_qkv
            qkv = jnp.roll(qkv, -SHIFT, axis=1)
            nw = L // WIN
            qkv = qkv.reshape(B, nw, WIN, 3, H, D)
            q, k, v = (qkv[:, :, :, 0], qkv[:, :, :, 1], qkv[:, :, :, 2])
            scores = jnp.einsum('bnqhd,bnkhd->bnhqk', q, k) / jnp.sqrt(jnp.float32(D)).astype(h.dtype)
            attn = jax.nn.softmax(scores, axis=-1)
            o = jnp.einsum('bnhqk,bnkhd->bnqhd', attn, v).reshape(B, L, C)
            o = jnp.roll(o, SHIFT, axis=1)
            return o @ w_so + b_so

        def _topk_cross_attn(h, ctx, w_q, b_q, w_kv, b_kv, w_co, b_co):
            B, L, _ = h.shape
            Lc = ctx.shape[1]
            q = (h @ w_q + b_q).reshape(B, L, H, D)
            kv = (ctx @ w_kv + b_kv).reshape(B, Lc, 2, H, D)
            k, v = (kv[:, :, 0], kv[:, :, 1])
            scores = jnp.einsum('bqhd,bkhd->bhqk', q, k) / jnp.sqrt(jnp.float32(D)).astype(h.dtype)
            top_s, top_i = jax.lax.top_k(scores, TOPK)
            attn = jax.nn.softmax(top_s, axis=-1)
            v_bh = jnp.transpose(v, (0, 2, 1, 3))
            vg = jnp.take_along_axis(v_bh[:, :, None, :, :], top_i[..., None], axis=3)
            o = jnp.einsum('bhqk,bhqkd->bqhd', attn, vg).reshape(B, L, C)
            return o @ w_co + b_co

        def _swiglu(h, w_m1, b_m1, w_m2, b_m2):
            u = h @ w_m1 + b_m1
            a, b = (u[..., :HID], u[..., HID:])
            return jax.nn.silu(a) * b @ w_m2 + b_m2
        key = jax.random.key(seed)
        ks = jax.random.split(key, 24)
        s = 0.02
        inp = {'x': jax.random.normal(ks[0], (2, 512, C), jnp.float32), 'mod': jax.random.normal(ks[1], (2, C), jnp.float32), 'context': jax.random.normal(ks[2], (2, 128, C), jnp.float32), 'w_ada': jax.random.normal(ks[3], (C, 9 * C), jnp.float32) * s, 'b_ada': jnp.zeros((9 * C,), jnp.float32), 'w_qkv': jax.random.normal(ks[4], (C, 3 * C), jnp.float32) * s, 'b_qkv': jnp.zeros((3 * C,), jnp.float32), 'w_so': jax.random.normal(ks[5], (C, C), jnp.float32) * s, 'b_so': jnp.zeros((C,), jnp.float32), 'w_q': jax.random.normal(ks[6], (C, C), jnp.float32) * s, 'b_q': jnp.zeros((C,), jnp.float32), 'w_kv': jax.random.normal(ks[7], (C, 2 * C), jnp.float32) * s, 'b_kv': jnp.zeros((2 * C,), jnp.float32), 'w_co': jax.random.normal(ks[8], (C, C), jnp.float32) * s, 'b_co': jnp.zeros((C,), jnp.float32), 'w_m1': jax.random.normal(ks[9], (C, 2 * HID), jnp.float32) * s, 'b_m1': jnp.zeros((2 * HID,), jnp.float32), 'w_m2': jax.random.normal(ks[10], (HID, C), jnp.float32) * s, 'b_m2': jnp.zeros((C,), jnp.float32)}
        return inp
    _L0_xcond_all = _L0_xcond_setup()
    _L0_xcond_in = {k: v for k, v in _L0_xcond_all.items() if k in ('w_ada', 'b_ada', 'w_qkv', 'b_qkv', 'w_so', 'b_so', 'w_q', 'b_q', 'w_kv', 'b_kv', 'w_co', 'b_co', 'w_m1', 'b_m1', 'w_m2', 'b_m2')}
    del _L0_xcond_all

    def _L1_xcond_setup():
        import jax, jax.numpy as jnp
        import numpy as np
        LN_EPS = 1e-06

        def _ln(x):
            mu = jnp.mean(x, axis=-1, keepdims=True)
            var = jnp.var(x, axis=-1, keepdims=True)
            return (x - mu) * jax.lax.rsqrt(var + LN_EPS)
        key = jax.random.key(seed)
        H, NH = (128, 16)
        B, N, S = (4, 128, 77)
        MLP = int(H * 4.0)
        ks = jax.random.split(key, 20)
        s = 1.0 / np.sqrt(H)
        return {'x': jax.random.normal(ks[0], (B, N, H), jnp.float32), 'c': jax.random.normal(ks[1], (B, H), jnp.float32), 'context': jax.random.normal(ks[2], (B, S, H), jnp.float32), 'W_mod': jax.random.normal(ks[3], (H, 6 * H), jnp.float32) * s, 'b_mod': jnp.zeros((6 * H,), jnp.float32), 'W_qkv': jax.random.normal(ks[4], (H, 3 * H), jnp.float32) * s, 'b_qkv': jnp.zeros((3 * H,), jnp.float32), 'W_proj': jax.random.normal(ks[5], (H, H), jnp.float32) * s, 'b_proj': jnp.zeros((H,), jnp.float32), 'W_qc': jax.random.normal(ks[6], (H, H), jnp.float32) * s, 'b_qc': jnp.zeros((H,), jnp.float32), 'W_kvc': jax.random.normal(ks[7], (H, 2 * H), jnp.float32) * s, 'b_kvc': jnp.zeros((2 * H,), jnp.float32), 'W_cproj': jax.random.normal(ks[8], (H, H), jnp.float32) * s, 'b_cproj': jnp.zeros((H,), jnp.float32), 'W_mlp1': jax.random.normal(ks[9], (H, MLP), jnp.float32) * s, 'b_mlp1': jnp.zeros((MLP,), jnp.float32), 'W_mlp2': jax.random.normal(ks[10], (MLP, H), jnp.float32) * (1.0 / np.sqrt(MLP)), 'b_mlp2': jnp.zeros((H,), jnp.float32)}
    _L1_xcond_all = _L1_xcond_setup()
    _L1_xcond_in = {k: v for k, v in _L1_xcond_all.items() if k in ('W_mod', 'b_mod', 'W_qkv', 'b_qkv', 'W_proj', 'b_proj', 'W_qc', 'b_qc', 'W_kvc', 'b_kvc', 'W_cproj', 'b_cproj', 'W_mlp1', 'b_mlp1', 'W_mlp2', 'b_mlp2')}
    del _L1_xcond_all

    def _L2_xcond_setup():
        import jax, jax.numpy as jnp
        import numpy as np
        EPS = 1e-05

        def _ada_ln(x, c, W_ss, b_ss):
            mu = jnp.mean(x, axis=-1, keepdims=True)
            var = jnp.mean((x - mu) ** 2, axis=-1, keepdims=True)
            h = (x - mu) / jnp.sqrt(var + EPS)
            ss = jax.nn.silu(c) @ W_ss + b_ss
            scale, bias = jnp.split(ss, 2, axis=-1)
            return (1.0 + scale)[:, None, :] * h + bias[:, None, :]
        key = jax.random.key(seed)
        ks = jax.random.split(key, 12)
        B, Lq, Lkv, H = (8, 256, 64, 128)
        s = 0.02
        return {'x_q': jax.random.normal(ks[0], (B, Lq, H), jnp.float32), 'x_kv': jax.random.normal(ks[1], (B, Lkv, H), jnp.float32), 't_vec': jax.random.normal(ks[2], (B, H), jnp.float32), 'Wq': jax.random.normal(ks[3], (H, H), jnp.float32) * s, 'bq': jnp.zeros((H,), jnp.float32), 'Wkv': jax.random.normal(ks[4], (H, 2 * H), jnp.float32) * s, 'bkv': jnp.zeros((2 * H,), jnp.float32), 'Wp': jax.random.normal(ks[5], (H, H), jnp.float32) * s, 'bp': jnp.zeros((H,), jnp.float32), 'Wss_q': jax.random.normal(ks[6], (H, 2 * H), jnp.float32) * s, 'bss_q': jnp.zeros((2 * H,), jnp.float32), 'Wss_kv': jax.random.normal(ks[7], (H, 2 * H), jnp.float32) * s, 'bss_kv': jnp.zeros((2 * H,), jnp.float32)}
    _L2_xcond_all = _L2_xcond_setup()
    _L2_xcond_in = {k: v for k, v in _L2_xcond_all.items() if k in ('Wq', 'bq', 'Wkv', 'bkv', 'Wp', 'bp', 'Wss_q', 'bss_q', 'Wss_kv', 'bss_kv')}
    del _L2_xcond_all

    def _L3_xcond_setup():
        import jax, jax.numpy as jnp
        import numpy as np
        import math
        D_MODEL = 128
        N_HEADS = 16
        HEAD_DIM = D_MODEL // N_HEADS
        D_FF = 512
        EPS = 1e-05
        ROPE_BASE = 10000.0

        def _rope(t):
            L, Dh = (t.shape[1], t.shape[-1])
            half = Dh // 2
            inv_freq = 1.0 / ROPE_BASE ** (jnp.arange(half, dtype=t.dtype) / half)
            ang = jnp.arange(L, dtype=t.dtype)[:, None] * inv_freq[None, :]
            cos = jnp.cos(ang)[None, :, None, :]
            sin = jnp.sin(ang)[None, :, None, :]
            t1, t2 = (t[..., :half], t[..., half:])
            return jnp.concatenate([t1 * cos - t2 * sin, t2 * cos + t1 * sin], axis=-1)

        def _adaln(x, emb, w, b):
            e = emb[:, 0, :]
            gb = e @ w.T + b
            gamma, beta = jnp.split(gb, 2, axis=-1)
            mu = x.mean(-1, keepdims=True)
            var = x.var(-1, keepdims=True)
            xn = (x - mu) * jax.lax.rsqrt(var + EPS)
            return xn * (1.0 + gamma[:, None, :]) + beta[:, None, :]

        def _attn(q, k, v):
            scale = 1.0 / math.sqrt(HEAD_DIM)
            scores = jnp.einsum('bqhd,bkhd->bhqk', q, k) * scale
            w = jax.nn.softmax(scores, axis=-1)
            out = jnp.einsum('bhqk,bkhd->bqhd', w, v)
            B, Lq = (out.shape[0], out.shape[1])
            return out.reshape(B, Lq, D_MODEL)
        key = jax.random.key(seed)
        ks = jax.random.split(key, 24)
        s = 0.02
        inp = {'x': jax.random.normal(ks[0], (2, 256, D_MODEL), jnp.float32), 'noise_emb': jax.random.normal(ks[1], (2, 1, D_MODEL), jnp.float32), 'context': jax.random.normal(ks[2], (2, 128, D_MODEL), jnp.float32), 'ln1_w': jax.random.normal(ks[3], (2 * D_MODEL, D_MODEL), jnp.float32) * s, 'ln1_b': jax.random.normal(ks[4], (2 * D_MODEL,), jnp.float32) * s, 'ln2_w': jax.random.normal(ks[5], (2 * D_MODEL, D_MODEL), jnp.float32) * s, 'ln2_b': jax.random.normal(ks[6], (2 * D_MODEL,), jnp.float32) * s, 'ln3_w': jax.random.normal(ks[7], (2 * D_MODEL, D_MODEL), jnp.float32) * s, 'ln3_b': jax.random.normal(ks[8], (2 * D_MODEL,), jnp.float32) * s, 'qkv_w': jax.random.normal(ks[9], (3 * D_MODEL, D_MODEL), jnp.float32) * s, 'sa_out_w': jax.random.normal(ks[10], (D_MODEL, D_MODEL), jnp.float32) * s, 'q_w': jax.random.normal(ks[11], (D_MODEL, D_MODEL), jnp.float32) * s, 'k_w': jax.random.normal(ks[12], (D_MODEL, D_MODEL), jnp.float32) * s, 'v_w': jax.random.normal(ks[13], (D_MODEL, D_MODEL), jnp.float32) * s, 'ca_out_w': jax.random.normal(ks[14], (D_MODEL, D_MODEL), jnp.float32) * s, 'ffn_w1': jax.random.normal(ks[15], (D_FF, D_MODEL), jnp.float32) * s, 'ffn_b1': jax.random.normal(ks[16], (D_FF,), jnp.float32) * s, 'ffn_w2': jax.random.normal(ks[17], (D_MODEL, D_FF), jnp.float32) * s, 'ffn_b2': jax.random.normal(ks[18], (D_MODEL,), jnp.float32) * s}
        return inp
    _L3_xcond_all = _L3_xcond_setup()
    _L3_xcond_in = {k: v for k, v in _L3_xcond_all.items() if k in ('ln1_w', 'ln1_b', 'ln2_w', 'ln2_b', 'ln3_w', 'ln3_b', 'qkv_w', 'sa_out_w', 'q_w', 'k_w', 'v_w', 'ca_out_w', 'ffn_w1', 'ffn_b1', 'ffn_w2', 'ffn_b2')}
    del _L3_xcond_all
    return {'x': x, 'cond_1024': cond_1024, 'ctx_1024': ctx_1024, 'L0_xcond_w_ada': _L0_xcond_in['w_ada'], 'L0_xcond_b_ada': _L0_xcond_in['b_ada'], 'L0_xcond_w_qkv': _L0_xcond_in['w_qkv'], 'L0_xcond_b_qkv': _L0_xcond_in['b_qkv'], 'L0_xcond_w_so': _L0_xcond_in['w_so'], 'L0_xcond_b_so': _L0_xcond_in['b_so'], 'L0_xcond_w_q': _L0_xcond_in['w_q'], 'L0_xcond_b_q': _L0_xcond_in['b_q'], 'L0_xcond_w_kv': _L0_xcond_in['w_kv'], 'L0_xcond_b_kv': _L0_xcond_in['b_kv'], 'L0_xcond_w_co': _L0_xcond_in['w_co'], 'L0_xcond_b_co': _L0_xcond_in['b_co'], 'L0_xcond_w_m1': _L0_xcond_in['w_m1'], 'L0_xcond_b_m1': _L0_xcond_in['b_m1'], 'L0_xcond_w_m2': _L0_xcond_in['w_m2'], 'L0_xcond_b_m2': _L0_xcond_in['b_m2'], 'L1_xcond_W_mod': _L1_xcond_in['W_mod'], 'L1_xcond_b_mod': _L1_xcond_in['b_mod'], 'L1_xcond_W_qkv': _L1_xcond_in['W_qkv'], 'L1_xcond_b_qkv': _L1_xcond_in['b_qkv'], 'L1_xcond_W_proj': _L1_xcond_in['W_proj'], 'L1_xcond_b_proj': _L1_xcond_in['b_proj'], 'L1_xcond_W_qc': _L1_xcond_in['W_qc'], 'L1_xcond_b_qc': _L1_xcond_in['b_qc'], 'L1_xcond_W_kvc': _L1_xcond_in['W_kvc'], 'L1_xcond_b_kvc': _L1_xcond_in['b_kvc'], 'L1_xcond_W_cproj': _L1_xcond_in['W_cproj'], 'L1_xcond_b_cproj': _L1_xcond_in['b_cproj'], 'L1_xcond_W_mlp1': _L1_xcond_in['W_mlp1'], 'L1_xcond_b_mlp1': _L1_xcond_in['b_mlp1'], 'L1_xcond_W_mlp2': _L1_xcond_in['W_mlp2'], 'L1_xcond_b_mlp2': _L1_xcond_in['b_mlp2'], 'L2_xcond_Wq': _L2_xcond_in['Wq'], 'L2_xcond_bq': _L2_xcond_in['bq'], 'L2_xcond_Wkv': _L2_xcond_in['Wkv'], 'L2_xcond_bkv': _L2_xcond_in['bkv'], 'L2_xcond_Wp': _L2_xcond_in['Wp'], 'L2_xcond_bp': _L2_xcond_in['bp'], 'L2_xcond_Wss_q': _L2_xcond_in['Wss_q'], 'L2_xcond_bss_q': _L2_xcond_in['bss_q'], 'L2_xcond_Wss_kv': _L2_xcond_in['Wss_kv'], 'L2_xcond_bss_kv': _L2_xcond_in['bss_kv'], 'L3_xcond_ln1_w': _L3_xcond_in['ln1_w'], 'L3_xcond_ln1_b': _L3_xcond_in['ln1_b'], 'L3_xcond_ln2_w': _L3_xcond_in['ln2_w'], 'L3_xcond_ln2_b': _L3_xcond_in['ln2_b'], 'L3_xcond_ln3_w': _L3_xcond_in['ln3_w'], 'L3_xcond_ln3_b': _L3_xcond_in['ln3_b'], 'L3_xcond_qkv_w': _L3_xcond_in['qkv_w'], 'L3_xcond_sa_out_w': _L3_xcond_in['sa_out_w'], 'L3_xcond_q_w': _L3_xcond_in['q_w'], 'L3_xcond_k_w': _L3_xcond_in['k_w'], 'L3_xcond_v_w': _L3_xcond_in['v_w'], 'L3_xcond_ca_out_w': _L3_xcond_in['ca_out_w'], 'L3_xcond_ffn_w1': _L3_xcond_in['ffn_w1'], 'L3_xcond_ffn_b1': _L3_xcond_in['ffn_b1'], 'L3_xcond_ffn_w2': _L3_xcond_in['ffn_w2'], 'L3_xcond_ffn_b2': _L3_xcond_in['ffn_b2']}

def reference(x, cond_1024, ctx_1024, L0_xcond_w_ada, L0_xcond_b_ada, L0_xcond_w_qkv, L0_xcond_b_qkv, L0_xcond_w_so, L0_xcond_b_so, L0_xcond_w_q, L0_xcond_b_q, L0_xcond_w_kv, L0_xcond_b_kv, L0_xcond_w_co, L0_xcond_b_co, L0_xcond_w_m1, L0_xcond_b_m1, L0_xcond_w_m2, L0_xcond_b_m2, L1_xcond_W_mod, L1_xcond_b_mod, L1_xcond_W_qkv, L1_xcond_b_qkv, L1_xcond_W_proj, L1_xcond_b_proj, L1_xcond_W_qc, L1_xcond_b_qc, L1_xcond_W_kvc, L1_xcond_b_kvc, L1_xcond_W_cproj, L1_xcond_b_cproj, L1_xcond_W_mlp1, L1_xcond_b_mlp1, L1_xcond_W_mlp2, L1_xcond_b_mlp2, L2_xcond_Wq, L2_xcond_bq, L2_xcond_Wkv, L2_xcond_bkv, L2_xcond_Wp, L2_xcond_bp, L2_xcond_Wss_q, L2_xcond_bss_q, L2_xcond_Wss_kv, L2_xcond_bss_kv, L3_xcond_ln1_w, L3_xcond_ln1_b, L3_xcond_ln2_w, L3_xcond_ln2_b, L3_xcond_ln3_w, L3_xcond_ln3_b, L3_xcond_qkv_w, L3_xcond_sa_out_w, L3_xcond_q_w, L3_xcond_k_w, L3_xcond_v_w, L3_xcond_ca_out_w, L3_xcond_ffn_w1, L3_xcond_ffn_b1, L3_xcond_ffn_w2, L3_xcond_ffn_b2):
    import jax
    import jax.numpy as jnp

    def _L0_xcond_ref(x, mod, context, w_ada, b_ada, w_qkv, b_qkv, w_so, b_so, w_q, b_q, w_kv, b_kv, w_co, b_co, w_m1, b_m1, w_m2, b_m2):
        import jax, jax.numpy as jnp
        import numpy as np
        C = 128
        H = 16
        D = C // H
        WIN = 64
        SHIFT = 32
        TOPK = 16
        HID = 512
        EPS = 1e-06

        def _ln(x):
            x32 = x.astype(jnp.float32)
            m = x32.mean(-1, keepdims=True)
            v = jnp.mean((x32 - m) ** 2, axis=-1, keepdims=True)
            return ((x32 - m) * jax.lax.rsqrt(v + EPS)).astype(x.dtype)

        def _self_attn(h, w_qkv, b_qkv, w_so, b_so):
            B, L, _ = h.shape
            qkv = h @ w_qkv + b_qkv
            qkv = jnp.roll(qkv, -SHIFT, axis=1)
            nw = L // WIN
            qkv = qkv.reshape(B, nw, WIN, 3, H, D)
            q, k, v = (qkv[:, :, :, 0], qkv[:, :, :, 1], qkv[:, :, :, 2])
            scores = jnp.einsum('bnqhd,bnkhd->bnhqk', q, k) / jnp.sqrt(jnp.float32(D)).astype(h.dtype)
            attn = jax.nn.softmax(scores, axis=-1)
            o = jnp.einsum('bnhqk,bnkhd->bnqhd', attn, v).reshape(B, L, C)
            o = jnp.roll(o, SHIFT, axis=1)
            return o @ w_so + b_so

        def _topk_cross_attn(h, ctx, w_q, b_q, w_kv, b_kv, w_co, b_co):
            B, L, _ = h.shape
            Lc = ctx.shape[1]
            q = (h @ w_q + b_q).reshape(B, L, H, D)
            kv = (ctx @ w_kv + b_kv).reshape(B, Lc, 2, H, D)
            k, v = (kv[:, :, 0], kv[:, :, 1])
            scores = jnp.einsum('bqhd,bkhd->bhqk', q, k) / jnp.sqrt(jnp.float32(D)).astype(h.dtype)
            top_s, top_i = jax.lax.top_k(scores, TOPK)
            attn = jax.nn.softmax(top_s, axis=-1)
            v_bh = jnp.transpose(v, (0, 2, 1, 3))
            vg = jnp.take_along_axis(v_bh[:, :, None, :, :], top_i[..., None], axis=3)
            o = jnp.einsum('bhqk,bhqkd->bqhd', attn, vg).reshape(B, L, C)
            return o @ w_co + b_co

        def _swiglu(h, w_m1, b_m1, w_m2, b_m2):
            u = h @ w_m1 + b_m1
            a, b = (u[..., :HID], u[..., HID:])
            return jax.nn.silu(a) * b @ w_m2 + b_m2
        m = jax.nn.silu(mod) @ w_ada + b_ada
        sh_msa, sc_msa, g_msa, sh_mca, sc_mca, g_mca, sh_mlp, sc_mlp, g_mlp = [m[:, i * C:(i + 1) * C][:, None, :] for i in range(9)]
        h = _ln(x) * (1 + sc_msa) + sh_msa
        h = _self_attn(h, w_qkv, b_qkv, w_so, b_so)
        x = x + h * g_msa
        h = _ln(x) * (1 + sc_mca) + sh_mca
        h = _topk_cross_attn(h, context, w_q, b_q, w_kv, b_kv, w_co, b_co)
        x = x + h * g_mca
        h = _ln(x) * (1 + sc_mlp) + sh_mlp
        h = _swiglu(h, w_m1, b_m1, w_m2, b_m2)
        x = x + h * g_mlp
        return x

    def _L1_xcond_ref(x, c, context, W_mod, b_mod, W_qkv, b_qkv, W_proj, b_proj, W_qc, b_qc, W_kvc, b_kvc, W_cproj, b_cproj, W_mlp1, b_mlp1, W_mlp2, b_mlp2):
        import jax, jax.numpy as jnp
        import numpy as np
        LN_EPS = 1e-06

        def _ln(x):
            mu = jnp.mean(x, axis=-1, keepdims=True)
            var = jnp.var(x, axis=-1, keepdims=True)
            return (x - mu) * jax.lax.rsqrt(var + LN_EPS)
        B, N, H = x.shape
        NH = 16
        hd = H // NH
        scale = hd ** (-0.5)
        c_proj = jax.nn.silu(c) @ W_mod + b_mod
        shift_a, scale_a, gate_a, shift_m, scale_m, gate_m = jnp.split(c_proj, 6, axis=-1)

        def modulate(t, shift, sc):
            return t * (1 + sc[:, None]) + shift[:, None]
        x_norm = modulate(_ln(x), shift_a, scale_a)
        qkv = x_norm @ W_qkv + b_qkv
        q, k, v = jnp.split(qkv, 3, axis=-1)
        q = q.reshape(B, N, NH, hd).transpose(0, 2, 1, 3)
        k = k.reshape(B, N, NH, hd).transpose(0, 2, 1, 3)
        v = v.reshape(B, N, NH, hd).transpose(0, 2, 1, 3)
        attn_w = jax.nn.softmax(jnp.einsum('bhqd,bhkd->bhqk', q, k) * scale, axis=-1)
        attn_out = jnp.einsum('bhqk,bhkd->bhqd', attn_w, v)
        attn_out = attn_out.transpose(0, 2, 1, 3).reshape(B, N, H)
        attn_out = attn_out @ W_proj + b_proj
        x = x + gate_a[:, None] * attn_out
        S = context.shape[1]
        q_c = _ln(x) @ W_qc + b_qc
        kv_c = _ln(context) @ W_kvc + b_kvc
        k_c, v_c = jnp.split(kv_c, 2, axis=-1)
        q_c = q_c.reshape(B, N, NH, hd).transpose(0, 2, 1, 3)
        k_c = k_c.reshape(B, S, NH, hd).transpose(0, 2, 1, 3)
        v_c = v_c.reshape(B, S, NH, hd).transpose(0, 2, 1, 3)
        c_attn_w = jax.nn.softmax(jnp.einsum('bhqd,bhsd->bhqs', q_c, k_c) * scale, axis=-1)
        c_attn_out = jnp.einsum('bhqs,bhsd->bhqd', c_attn_w, v_c)
        c_attn_out = c_attn_out.transpose(0, 2, 1, 3).reshape(B, N, H)
        c_attn_out = c_attn_out @ W_cproj + b_cproj
        x = x + c_attn_out
        x_norm2 = modulate(_ln(x), shift_m, scale_m)
        h = jax.nn.gelu(x_norm2 @ W_mlp1 + b_mlp1)
        h = h @ W_mlp2 + b_mlp2
        x = x + gate_m[:, None] * h
        return x

    def _L2_xcond_ref(x_q, x_kv, t_vec, Wq, bq, Wkv, bkv, Wp, bp, Wss_q, bss_q, Wss_kv, bss_kv):
        import jax, jax.numpy as jnp
        import numpy as np
        EPS = 1e-05

        def _ada_ln(x, c, W_ss, b_ss):
            mu = jnp.mean(x, axis=-1, keepdims=True)
            var = jnp.mean((x - mu) ** 2, axis=-1, keepdims=True)
            h = (x - mu) / jnp.sqrt(var + EPS)
            ss = jax.nn.silu(c) @ W_ss + b_ss
            scale, bias = jnp.split(ss, 2, axis=-1)
            return (1.0 + scale)[:, None, :] * h + bias[:, None, :]
        B, Lq, H = x_q.shape
        Lkv = x_kv.shape[1]
        nh = 16
        dh = H // nh
        xq = _ada_ln(x_q, t_vec, Wss_q, bss_q)
        xkv = _ada_ln(x_kv, t_vec, Wss_kv, bss_kv)
        q = (xq @ Wq + bq).reshape(B, Lq, nh, dh)
        kv = (xkv @ Wkv + bkv).reshape(B, Lkv, 2, nh, dh)
        k = kv[:, :, 0]
        v = kv[:, :, 1]
        scores = jnp.einsum('bqhd,bkhd->bhqk', q, k) / jnp.sqrt(jnp.float32(dh))
        attn = jax.nn.softmax(scores, axis=-1)
        out = jnp.einsum('bhqk,bkhd->bqhd', attn, v).reshape(B, Lq, H)
        return x_q + (out @ Wp + bp)

    def _L3_xcond_ref(x, noise_emb, context, ln1_w, ln1_b, ln2_w, ln2_b, ln3_w, ln3_b, qkv_w, sa_out_w, q_w, k_w, v_w, ca_out_w, ffn_w1, ffn_b1, ffn_w2, ffn_b2):
        import jax, jax.numpy as jnp
        import numpy as np
        import math
        D_MODEL = 128
        N_HEADS = 16
        HEAD_DIM = D_MODEL // N_HEADS
        D_FF = 512
        EPS = 1e-05
        ROPE_BASE = 10000.0

        def _rope(t):
            L, Dh = (t.shape[1], t.shape[-1])
            half = Dh // 2
            inv_freq = 1.0 / ROPE_BASE ** (jnp.arange(half, dtype=t.dtype) / half)
            ang = jnp.arange(L, dtype=t.dtype)[:, None] * inv_freq[None, :]
            cos = jnp.cos(ang)[None, :, None, :]
            sin = jnp.sin(ang)[None, :, None, :]
            t1, t2 = (t[..., :half], t[..., half:])
            return jnp.concatenate([t1 * cos - t2 * sin, t2 * cos + t1 * sin], axis=-1)

        def _adaln(x, emb, w, b):
            e = emb[:, 0, :]
            gb = e @ w.T + b
            gamma, beta = jnp.split(gb, 2, axis=-1)
            mu = x.mean(-1, keepdims=True)
            var = x.var(-1, keepdims=True)
            xn = (x - mu) * jax.lax.rsqrt(var + EPS)
            return xn * (1.0 + gamma[:, None, :]) + beta[:, None, :]

        def _attn(q, k, v):
            scale = 1.0 / math.sqrt(HEAD_DIM)
            scores = jnp.einsum('bqhd,bkhd->bhqk', q, k) * scale
            w = jax.nn.softmax(scores, axis=-1)
            out = jnp.einsum('bhqk,bkhd->bqhd', w, v)
            B, Lq = (out.shape[0], out.shape[1])
            return out.reshape(B, Lq, D_MODEL)
        B, L, D = x.shape
        L_ctx = context.shape[1]
        res = x
        xn = _adaln(x, noise_emb, ln1_w, ln1_b)
        qkv = xn @ qkv_w.T
        q, k, v = jnp.split(qkv, 3, axis=-1)
        q = _rope(q.reshape(B, L, N_HEADS, HEAD_DIM))
        k = _rope(k.reshape(B, L, N_HEADS, HEAD_DIM))
        v = v.reshape(B, L, N_HEADS, HEAD_DIM)
        sa = _attn(q, k, v) @ sa_out_w.T
        x = res + sa
        res = x
        xn = _adaln(x, noise_emb, ln2_w, ln2_b)
        q = _rope((xn @ q_w.T).reshape(B, L, N_HEADS, HEAD_DIM))
        k = _rope((context @ k_w.T).reshape(B, L_ctx, N_HEADS, HEAD_DIM))
        v = (context @ v_w.T).reshape(B, L_ctx, N_HEADS, HEAD_DIM)
        ca = _attn(q, k, v) @ ca_out_w.T
        x = res + ca
        res = x
        xn = _adaln(x, noise_emb, ln3_w, ln3_b)
        h = jax.nn.gelu(xn @ ffn_w1.T + ffn_b1, approximate=False)
        x = res + (h @ ffn_w2.T + ffn_b2)
        return x
    x = _L0_xcond_ref(x, cond_1024, ctx_1024, L0_xcond_w_ada, L0_xcond_b_ada, L0_xcond_w_qkv, L0_xcond_b_qkv, L0_xcond_w_so, L0_xcond_b_so, L0_xcond_w_q, L0_xcond_b_q, L0_xcond_w_kv, L0_xcond_b_kv, L0_xcond_w_co, L0_xcond_b_co, L0_xcond_w_m1, L0_xcond_b_m1, L0_xcond_w_m2, L0_xcond_b_m2)
    x = _L1_xcond_ref(x, cond_1024, ctx_1024, L1_xcond_W_mod, L1_xcond_b_mod, L1_xcond_W_qkv, L1_xcond_b_qkv, L1_xcond_W_proj, L1_xcond_b_proj, L1_xcond_W_qc, L1_xcond_b_qc, L1_xcond_W_kvc, L1_xcond_b_kvc, L1_xcond_W_cproj, L1_xcond_b_cproj, L1_xcond_W_mlp1, L1_xcond_b_mlp1, L1_xcond_W_mlp2, L1_xcond_b_mlp2)
    x = _L2_xcond_ref(x, ctx_1024, cond_1024, L2_xcond_Wq, L2_xcond_bq, L2_xcond_Wkv, L2_xcond_bkv, L2_xcond_Wp, L2_xcond_bp, L2_xcond_Wss_q, L2_xcond_bss_q, L2_xcond_Wss_kv, L2_xcond_bss_kv)
    x = _L3_xcond_ref(x, cond_1024[:, None, :], ctx_1024, L3_xcond_ln1_w, L3_xcond_ln1_b, L3_xcond_ln2_w, L3_xcond_ln2_b, L3_xcond_ln3_w, L3_xcond_ln3_b, L3_xcond_qkv_w, L3_xcond_sa_out_w, L3_xcond_q_w, L3_xcond_k_w, L3_xcond_v_w, L3_xcond_ca_out_w, L3_xcond_ffn_w1, L3_xcond_ffn_b1, L3_xcond_ffn_w2, L3_xcond_ffn_b2)
    return x

_drawn_inputs = setup_inputs


def setup_inputs(seed=0):
    import zlib

    import numpy as np

    out = dict(_drawn_inputs(seed))
    spreads = {'L0_xcond_b_ada': (0.0, 0.411),
     'L0_xcond_b_qkv': (0.0, 0.8),
     'L0_xcond_b_so': (0.0, 0.478),
     'L0_xcond_b_q': (0.0, 0.8),
     'L0_xcond_b_kv': (0.0, 0.8),
     'L0_xcond_b_co': (0.0, 0.459),
     'L0_xcond_b_m1': (0.0, 0.8),
     'L0_xcond_b_m2': (0.0, 1.107),
     'L1_xcond_b_mod': (0.0, 0.319),
     'L1_xcond_b_qkv': (0.0, 0.79),
     'L1_xcond_b_proj': (0.0, 0.8),
     'L1_xcond_b_qc': (0.0, 2.0),
     'L1_xcond_b_kvc': (0.0, 0.493),
     'L1_xcond_b_cproj': (0.0, 0.551),
     'L1_xcond_b_mlp1': (0.0, 0.8),
     'L1_xcond_b_mlp2': (0.0, 0.8),
     'L2_xcond_bq': (0.0, 2.0),
     'L2_xcond_bkv': (0.0, 2.0),
     'L2_xcond_bp': (0.0, 0.52),
     'L2_xcond_bss_q': (0.0, 2.0),
     'L2_xcond_bss_kv': (0.0, 2.0)}
    factors = {'L0_xcond_w_qkv': 8.0,
     'L0_xcond_w_so': 8.0,
     'L0_xcond_w_q': 8.0,
     'L0_xcond_w_kv': 8.0,
     'L0_xcond_w_co': 7.903,
     'L0_xcond_w_m1': 8.0,
     'L0_xcond_w_m2': 8.0,
     'L2_xcond_Wq': 64.0,
     'L2_xcond_Wss_q': 64.0,
     'L2_xcond_Wss_kv': 44.813,
     'L3_xcond_ln1_w': 26.576,
     'L3_xcond_ln1_b': 64.0,
     'L3_xcond_ln2_w': 8.0,
     'L3_xcond_ln2_b': 105.69,
     'L3_xcond_ln3_w': 19.922,
     'L3_xcond_ln3_b': 64.0,
     'L3_xcond_q_w': 8.0,
     'L3_xcond_k_w': 8.0,
     'L3_xcond_v_w': 2.9,
     'L3_xcond_ca_out_w': 2.956,
     'L3_xcond_ffn_b1': 64.0,
     'L3_xcond_ffn_b2': 19.901,
     'L2_xcond_Wkv': 4.168,
     'L2_xcond_Wp': 2.745,
     'L3_xcond_qkv_w': 4.581,
     'L3_xcond_sa_out_w': 4.625,
     'L3_xcond_ffn_w1': 3.903,
     'L3_xcond_ffn_w2': 3.561}
    for name, (base, spread) in spreads.items():
        noise = np.random.default_rng([zlib.crc32(name.encode()), seed]).standard_normal(out[name].shape)
        drawn = base * np.exp(spread * noise) if base else spread * noise
        out[name] = jnp.asarray(drawn.astype(out[name].dtype))
    for name, factor in factors.items():
        out[name] = (out[name] * factor).astype(out[name].dtype)
    return out
```

```python
from contextlib import ExitStack

import numpy as np

import concourse.bass as bass
from concourse import mybir

F32 = mybir.dt.float32
BF16 = mybir.dt.bfloat16
ALU = mybir.AluOpType
ACT = mybir.ActivationFunctionType
AX = mybir.AxisListType.X

B, L, C, LC = 8, 128, 128, 120
H = 16
D = C // H
G = 4
J = H // G
SHIFT = 32
HID = 512
CH = HID // C
SCALE = float(D) ** -0.5
TAKEN = -3.0e38

MODS = ["L0a", "L0c", "L0m", "L1a", "L1m", "L2q", "L2kv", "L31", "L32", "L33"]
GATED = 5
NMOD = len(MODS)
NVEC = 2 * NMOD + GATED


class Blk:
    def __init__(self, kind, name, mod=None, eps=1e-6, windows=1, ctx=None, rope=False, bias=True, gate=None, act=None):
        self.kind, self.name, self.mod, self.eps, self.windows = kind, name, mod, eps, windows
        self.ctx, self.rope, self.bias, self.gate, self.act = ctx, rope, bias, gate, act
        self.attn = kind != "mlp"
        self.keys = LC if ctx is not None else L


BLOCKS = [
    Blk("soft", "sa0", mod=0, windows=2, gate=0),
    Blk("topk", "xa0", mod=1, ctx=0, gate=1),
    Blk("mlp", "ml0", mod=2, gate=2, act=ACT.Silu),
    Blk("soft", "sa1", mod=3, gate=3),
    Blk("soft", "xa1", ctx=1),
    Blk("mlp", "ml1", mod=4, gate=4, act=ACT.Gelu_apprx_tanh),
    Blk("soft", "xa2", mod=5, eps=1e-5, ctx=2),
    Blk("soft", "sa3", mod=7, eps=1e-5, rope=True, bias=False),
    Blk("soft", "xa3", mod=8, eps=1e-5, ctx=0, rope=True, bias=False),
    Blk("mlp", "ml3", mod=9, eps=1e-5, act=ACT.Gelu),
]
NBLK = len(BLOCKS)
BIASED = [n for n, k in enumerate(BLOCKS) if k.bias and k.attn]

WCOL = {}
_at = 0
for _k in BLOCKS:
    for _w, _n in ((("q", C), ("k", C), ("qr", C * _k.rope), ("kr", C * _k.rope), ("v", C), ("o", C)) if _k.attn
                   else (("w1", HID * (2 if _k.act == ACT.Silu else 1)), ("w2", HID))):
        if _n:
            WCOL[_k.name, _w] = _at
            _at += _n
WTOT = _at
WSPLIT = [WCOL["xa0", "q"], WCOL["ml0", "w1"], WCOL["sa1", "q"], WCOL["xa2", "q"], WTOT]

BCOL = {}
_at = 0
for _k in BLOCKS:
    for _w, _n in ((("q", 1), ("k", 1), ("v", 1), ("o", 1)) if _k.attn
                   else (("b1", CH * (2 if _k.act == ACT.Silu else 1)), ("b2", 1))):
        if _k.bias:
            BCOL[_k.name, _w] = _at
            _at += _n
BTOT = _at

CCOL = {"ident": 0, "headmask": 128, "sel": 132, "cos": 148, "sin": 276, "cosc": 404, "sinc": 524, "groupmask": 644}
CTOT = CCOL["groupmask"] + G


def build(nc, x, cond_t, ctx_n, ctx_t, wmod, bmod, wts, bias, consts, out):
    with ExitStack() as ctx:
        def sb(name, shape, dt=F32):
            return ctx.enter_context(nc.sbuf_tensor(name, shape, dt))

        def sem(name):
            return ctx.enter_context(nc.semaphore(name))

        def sems(name, n=G):
            return [sem(f"{name}{i}") for i in range(n)]

        bank_a = [ctx.enter_context(nc.psum_tensor(f"bank_a{i}", [128, 512], F32)) for i in range(2)]
        bank_b = [ctx.enter_context(nc.psum_tensor(f"bank_b{i}", [128, 512], F32)) for i in range(2)]
        bank_o = ctx.enter_context(nc.psum_tensor("bank_o", [128, 512], F32))
        bank_p = ctx.enter_context(nc.psum_tensor("bank_p", [128, 512], F32))
        bank_f = ctx.enter_context(nc.psum_tensor("bank_f", [128, 512], F32))
        bank_m = ctx.enter_context(nc.psum_tensor("bank_m", [128, 512], F32))

        x_sb = sb("x_sb", [128, B * C])
        w_sb = sb("w_sb", [128, WTOT])
        b_sb = sb("b_sb", [128, BTOT])
        c_sb = sb("c_sb", [128, CTOT])
        wmod_sb = sb("wmod_sb", [128, NVEC * C])
        bmod_sb = sb("bmod_sb", [128, NVEC])
        cond_sb = sb("cond_sb", [128, B])
        scond_sb = sb("scond_sb", [128, B])
        mods = sb("mods", [128, NVEC * B])
        bprime = sb("bprime", [128, NBLK])
        gbias = sb("gbias", [128, GATED * B])
        ctxn_sb = sb("ctxn_sb", [LC, B * C])
        ctx_sb = [sb(f"ctx_sb{i}", [128, B * LC]) for i in range(3)]
        cstat = sb("cstat", [LC, B * 6])
        cmv = sb("cmv", [LC, B * 2])
        ceps = sb("ceps", [LC, 2 * B])
        crstd = sb("crstd", [LC, 2 * B])
        cnorm = sb("cnorm", [LC, 2 * B * C])
        half_neg = sb("half_neg", [128, 2 * B])
        ident = c_sb[:, 0:128]
        identb = sb("identb", [128, 128], BF16)
        selcol = c_sb[:, CCOL["sel"]:CCOL["sel"] + H]
        sel = sb("sel", [128, H * 128], BF16)
        headmask = c_sb[:, CCOL["headmask"]:CCOL["headmask"] + J]
        groupmask = c_sb[:, CCOL["groupmask"]:CCOL["groupmask"] + G]

        stat = sb("stat", [128, 2 * 6])
        mv = sb("mv", [128, 2 * 2])
        vareps = sb("vareps", [128, 2])
        rstd = sb("rstd", [128, 2])
        xn = [sb(f"xn{i}", [128, C]) for i in range(2)]
        ht = [sb(f"ht{i}", [128, L]) for i in range(2)]
        cslot = [sb(f"cslot{i}", [128, LC]) for i in range(2)]
        qk = [sb(f"qk{i}", [128, 2 * L]) for i in range(2)]
        ropec = sb("ropec", [128, 2 * L])
        ropes = sb("ropes", [128, 2 * L])
        qbd = [sb(f"qbd{i}", [128, J * L]) for i in range(2)]
        kbd = [sb(f"kbd{i}", [128, J * L]) for i in range(2)]
        qgr = [sb(f"qgr{i}", [128, G * L]) for i in range(2)]
        kgr = [sb(f"kgr{i}", [128, G * L]) for i in range(2)]
        vpad = [sb(f"vpad{i}", [128, H * 64]) for i in range(2)]
        vwin = [[sb(f"vwin{w}_{i}", [128, H * 64]) for i in range(2)] for w in range(2)]
        nmax = sb("nmax", [128, H])
        mres = sb("mres", [128, H])
        mparts = sb("mparts", [128, 3 * H], BF16)
        mt = sb("mt", [128, L], BF16)
        pt = [sb(f"pt{i}", [128, 512]) for i in range(2)]
        ot = sb("ot", [128, 2 * L])
        rec = sb("rec", [128, H])
        on = sb("on", [128, C])
        ont = sb("ont", [128, L])
        yt = sb("yt", [128, L])
        top = sb("top", [128, H * 16])
        nbias = sb("nbias", [128, H])
        s3 = sb("s3", [128, H * LC])
        ex = sb("ex", [128, H * LC])
        pn = sb("pn", [128, H * LC])
        act = [sb(f"act{i}", [128, HID]) for i in range(2)]
        hid = [sb(f"hid{i}", [128, HID]) for i in range(2)]

        x_in, w_in, small_in, wmod_in, ctx_in = sem("x_in"), sems("w_in", 5), sem("small_in"), sem("wmod_in"), sem("ctx_in")
        silu_c, consts_made, pads_zero, pads_made = sem("silu_c"), sem("consts_made"), sem("pads_zero"), sem("pads_made")
        mods_mm, mods_add, mods_made, bp_mm, bp_made = (
            sem("mods_mm"), sem("mods_add"), sem("mods_made"), sem("bp_mm"), sem("bp_made"))
        gb_made = sem("gb_made")
        c_stat, c_aggr, c_eps, c_rstd, c_norm, c_tr, c_out = (
            sem("c_stat"), sem("c_aggr"), sem("c_eps"), sem("c_rstd"), sem("c_norm"), sem("c_tr"), sem("c_out"))
        st_done, aggr_done, eps_done, rstd_done, xn_done = (
            sem("st_done"), sem("aggr_done"), sem("eps_done"), sem("rstd_done"), sem("xn_done"))
        xnt_done, ht_done, proj_done = sem("xnt_done"), sem("ht_done"), sem("proj_done")
        ctx_copied, ropec_done, ropes_done = sem("ctx_copied"), sem("ropec_done"), sem("ropes_done")
        qk_done, v_done, kbd_done, qbd_done = sem("qk_done"), sem("v_done"), sem("kbd_done"), sem("qbd_done")
        a_done, a_free = sems("a_done"), sems("a_free")
        m1_done, r1_done, m2_done, mparts_done = sem("m1_done"), sem("r1_done"), sem("m2_done"), sem("mparts_done")
        mpt_done, mt_done = sem("mpt_done"), sem("mt_done")
        t8_done, tmr_done, t16_done, s3_done, mask_done, p_done = (
            sems("t8_done"), sems("tmr_done"), sems("t16_done"), sems("s3_done"), sems("mask_done"), sems("p_done"))
        b_done, pt_done, pv_done = sems("b_done"), sems("pt_done"), sems("pv_done", G - 1)
        o_done, o_free = sem("o_done"), sem("o_free")
        otn_done, rec_done, on_done, ont_done, ontc_done = (
            sem("otn_done"), sem("rec_done"), sem("on_done"), sem("ont_done"), sem("ontc_done"))
        y_done, yt_done, yb_done, xadd_done = sem("y_done"), sem("yt_done"), sem("yb_done"), sem("xadd_done")
        act_done, hid_done = sem("act_done"), sem("hid_done")
        stored = sem("stored")

        def before(n, *kinds):
            return B * sum(k.kind in kinds for k in BLOCKS[:n])

        def all_(n):
            return B * n

        def attn_(n):
            return before(n, "soft", "topk")

        def soft_(n):
            return before(n, "soft")

        def topk_(n):
            return before(n, "topk")

        def mlp_(n):
            return before(n, "mlp")

        def cross_(n):
            return B * sum(k.ctx is not None for k in BLOCKS[:n])

        def rope_(n):
            return B * sum(k.rope for k in BLOCKS[:n])

        class At:

            def __init__(self, eng, n, c, i=None, held=None):
                self.eng, self.n, self.c, self.i, self.held = eng, n, c, i, held
                self.k, self.u = BLOCKS[n], c % 2

            def value(self, scale, add):
                if self.i is None:
                    return scale * self.c + add
                key = (scale, scale * self.c + add)
                if key not in self.held:
                    self.held[key] = self.eng.snap(self.i * (2 * scale) + key[1])
                    self.eng.compute_val(self.held[key])
                return self.held[key]

            def span(self, width, at=0):
                return bass.ds(self.value(width, at), width)

            def one(self, at):
                return bass.ds(self.value(1, at), 1)

            def wait(self, semaphore, base, back=0, carry=None):
                if self.i is None and base + self.c + 1 - back <= 0:
                    return
                value = self.value(1, base + 1 - back)
                if carry and self.i is not None:
                    self.eng.wait_ge(*carry)
                self.eng.wait_ge(semaphore, value)

            @property
            def first(self):
                return self.i is None and self.c == 0

        def pipeline(eng, step):
            def fixed(n, c):
                n, c = n + c // B, c % B
                return At(eng, n, c) if 0 <= n < NBLK else None

            step(None, None, fixed(0, 0), fixed(0, 1))
            for n in range(NBLK):
                for c in (0, 1):
                    step(*(fixed(n, c + d) for d in (-1, 0, 1, 2)))
                with eng.Fori(0, 2) as i:
                    for c in (2, 3):
                        held = {}
                        step(*(At(eng, n, c + d, i, held) for d in (-1, 0, 1, 2)))
                for c in (6, 7):
                    step(*(fixed(n, c + d) for d in (-1, 0, 1, 2)))
            step(fixed(NBLK, -1), None, None, None)

        def w(k, what, n=C, at=0):
            c = WCOL[k.name, what] + at
            return w_sb[:, c:c + n]

        def bcol(k, what, at=0):
            c = BCOL[k.name, what] + at
            return b_sb[:, c:c + 1]

        def heads4(ap, n):
            return ap.rearrange("p (j n) -> p j n", n=n)

        def vspots(t, rows):
            base = t[rows, :]
            v = base.rearrange("p (g r) -> p g r", g=G)
            return v

        block = ctx.enter_context(nc.Block())

        @block.sync
        def _(sp):
            sp.dma_start(cond_sb[:], cond_t).then_inc(small_in, 16)
            sp.dma_start(bmod_sb[:], bmod).then_inc(small_in, 16)
            sp.dma_start(b_sb[:], bias).then_inc(small_in, 16)
            sp.dma_start(c_sb[:], consts).then_inc(small_in, 16)
            sp.dma_start(wmod_sb[:], wmod).then_inc(wmod_in, 16)
            sp.dma_start(ctx_sb[0][:], ctx_t).then_inc(ctx_in, 16)
            sp.dma_start(ctxn_sb[:].rearrange("p (b c) -> p b c", b=B), ctx_n.rearrange("b s c -> s b c")).then_inc(ctx_in, 16)
            lo = 0
            for s, hi in zip(w_in[1:], WSPLIT[1:]):
                lo = WSPLIT[w_in.index(s) - 1]
                sp.dma_start(w_sb[:, lo:hi], wts[:, lo:hi]).then_inc(s, 16)
            for b in range(B):
                sp.wait_ge(xadd_done, all_(NBLK - 1) + b + 1)
                sp.dma_start(out[b, SHIFT:L, :], x_sb[0:L - SHIFT, b * C:(b + 1) * C]).then_inc(stored, 16)
                sp.dma_start(out[b, 0:SHIFT, :], x_sb[L - SHIFT:L, b * C:(b + 1) * C]).then_inc(stored, 16)
            sp.wait_ge(stored, 2 * 16 * B)

        @block.gpsimd
        def _(pool):
            for t in vpad + vwin[0] + vwin[1]:
                nc.gpsimd.memset(t[:], 0.0)
            nc.gpsimd.memset(mt[:], 0.0)
            nc.gpsimd.memset(half_neg[:], -0.5).then_inc(pads_zero, 1)
            pool.wait_ge(pads_zero, 1)
            for j in range(J):
                for t in vpad:
                    last = nc.gpsimd.memset(t[:].rearrange("p (g r) -> p g r", g=G)[:, :, 64 * j + 32 + j:64 * j + 33 + j], 1.0)
            last.then_inc(pads_zero, 1)
            pool.wait_ge(pads_zero, 2)
            for wd in range(2):
                for j in range(J):
                    for t in vwin[wd]:
                        last = nc.gpsimd.memset(
                            t[64 * wd:64 * wd + 64, :].rearrange("p (g r) -> p g r", g=G)[:, :, 64 * j + 32 + j:64 * j + 33 + j], 1.0)
            last.then_inc(pads_made, 1)
            pool.wait_ge(pads_made, 1)
            pool.wait_ge(c_aggr, 1)
            var = cmv[:].rearrange("p (b t) -> p b t", t=2)[:, :, 1]
            for e, eps in enumerate((1e-6, 1e-5)):
                last = nc.gpsimd.tensor_scalar(ceps[:, e * B:(e + 1) * B], var, eps, None, ALU.add)
            last.then_inc(c_eps, 1)
            pool.wait_ge(c_eps, 1)
            nc.gpsimd.tensor_tensor(crstd[:], ceps[:], half_neg[0:LC, :], ALU.pow).then_inc(c_rstd, 1)

            def rstd_of(a):
                u = a.u
                a.wait(aggr_done, all_(a.n), carry=(pads_made, 1))
                a.wait(xn_done, all_(a.n), 2, carry=(pads_made, 1))
                nc.gpsimd.tensor_scalar(vareps[:, u:u + 1], mv[:, 2 * u + 1:2 * u + 2], a.k.eps, None, ALU.add).then_inc(eps_done, 1)
                a.wait(eps_done, all_(a.n))
                nc.gpsimd.tensor_tensor(rstd[:, u:u + 1], vareps[:, u:u + 1], half_neg[:, 0:1], ALU.pow).then_inc(rstd_done, 1)

            def context_of(a):
                if a.k.ctx is None:
                    return
                if a.k.ctx and a.first:
                    pool.wait_ge(c_out, 10)
                if a.k.ctx == 0 and a.first:
                    pool.wait_ge(ctx_in, 32)
                a.wait(proj_done, all_(a.n), 2)
                nc.gpsimd.tensor_copy(cslot[a.u][:], ctx_sb[a.k.ctx][:, a.span(LC)]).then_inc(ctx_copied, 1)

            def head_blocks(a):
                if not a.k.attn:
                    return
                u, n = a.u, a.k.keys
                a.wait(qk_done, attn_(a.n))
                a.wait(o_done, all_(a.n), 2)

                def spread(dst, at, m, mask):
                    return nc.gpsimd.tensor_tensor(
                        heads4(dst[:, 0:4 * m], m), qk[u][:, None, at:at + m].broadcast_to([128, 4, m]),
                        mask[:, :, None].broadcast_to([128, 4, m]), ALU.mult)

                spread(qgr[u], 0, L, groupmask)
                spread(kbd[u], L, n, headmask).then_inc(kbd_done, 1)
                if a.k.kind == "soft":
                    spread(kgr[u], L, n, groupmask)
                    spread(qbd[u], 0, L, headmask).then_inc(qbd_done, 1)

            def keep_top(a):
                if a.k.kind != "topk":
                    return
                for g in range(G):
                    cols = slice(g * J * LC, (g + 1) * J * LC)
                    a.wait(s3_done[g], topk_(a.n), carry=(pads_made, 1))
                    nc.gpsimd.tensor_scalar(s3[:, cols], s3[:, cols], TAKEN, None, ALU.is_le).then_inc(mask_done[g], 1)
                    a.wait(mask_done[g], topk_(a.n))
                    a.wait(a_free[g], attn_(a.n))
                    a.wait(b_done[g], attn_(a.n), 1)
                    nc.gpsimd.tensor_tensor(pn[:, cols], ex[:, cols], s3[:, cols], ALU.mult).then_inc(p_done[g], 1)

            def step(done, now, nxt, aft):
                if now is None and nxt is not None:
                    rstd_of(nxt)
                    context_of(nxt)
                if aft is not None:
                    rstd_of(aft)
                if nxt is not None:
                    head_blocks(nxt)
                if aft is not None:
                    context_of(aft)
                if nxt is not None:
                    keep_top(nxt)

            pipeline(pool, step)

        @block.scalar
        def _(sc):
            sc.dma_start(x_sb[0:L - SHIFT, :].rearrange("p (b c) -> p b c", b=B), x[:, SHIFT:L, :].rearrange("b t c -> t b c")).then_inc(x_in, 16)
            sc.dma_start(x_sb[L - SHIFT:L, :].rearrange("p (b c) -> p b c", b=B), x[:, 0:SHIFT, :].rearrange("b t c -> t b c")).then_inc(x_in, 16)
            sc.dma_start(w_sb[:, 0:WSPLIT[0]], wts[:, 0:WSPLIT[0]]).then_inc(w_in[0], 16)
            sc.wait_ge(small_in, 64)
            nc.scalar.activation(scond_sb[:], cond_sb[:], ACT.Silu).then_inc(silu_c, 1)
            for i in range(2):
                sc.wait_ge(c_tr, i + 1)
                nc.scalar.activation(ctx_sb[1][:, i * 4 * LC:(i + 1) * 4 * LC], bank_b[i][:, 0:4 * LC], ACT.Copy).then_inc(c_out, 1)
            sc.wait_ge(mods_made, 1)
            kv = MODS.index("L2kv")
            for b in range(B):
                if b % 4 == 0:
                    sc.wait_ge(c_tr, 3 + b // 4)
                nc.scalar.activation(
                    ctx_sb[2][:, b * LC:(b + 1) * LC], (bank_o, bank_f)[b // 4][:, b % 4 * LC:(b % 4 + 1) * LC], ACT.Identity,
                    bias=mods[:, (NMOD + kv) * B + b:(NMOD + kv) * B + b + 1],
                    scale=mods[:, kv * B + b:kv * B + b + 1]).then_inc(c_out, 1)
            sc.preload_act_table(ACT.Exp)

            def modulate(a):
                a.wait(xnt_done, all_(a.n))
                a.wait(proj_done, all_(a.n), 2)
                if a.k.mod is None:
                    nc.scalar.activation(ht[a.u][:], bank_p[:, 0:L], ACT.Copy).then_inc(ht_done, 1)
                else:
                    nc.scalar.activation(ht[a.u][:], bank_p[:, 0:L], ACT.Identity, bias=mods[:, a.one((NMOD + a.k.mod) * B)],
                                         scale=mods[:, a.one(a.k.mod * B)]).then_inc(ht_done, 1)

            def qkv_out(a):
                if not a.k.attn:
                    return
                u, n, k = a.u, a.k.keys, a.k
                a.wait(proj_done, all_(a.n))
                a.wait(o_done, all_(a.n), 2)
                if a.first and a.n == 0:
                    sc.wait_ge(pads_made, 1)
                if not k.rope:
                    nc.scalar.activation(qk[u][:, 0:L], bank_p[:, 0:L], ACT.Identity, bias=bcol(k, "q"))
                    nc.scalar.activation(qk[u][:, L:L + n], bank_p[:, L:L + n], ACT.Identity, bias=bcol(k, "k")).then_inc(qk_done, 1)
                for wd in range(k.windows):
                    rows = slice(64 * wd, 64 * wd + 64) if k.windows == 2 else slice(0, n)
                    dst = vwin[wd][u] if k.windows == 2 else vpad[u]
                    for j in range(J):
                        last = nc.scalar.activation(
                            dst[rows, :].rearrange("p (g r) -> p g r", g=G)[:, :, 72 * j:72 * j + D],
                            bank_m[rows, 128:256].rearrange("p (g j d) -> p g j d", g=G, j=J)[:, :, j, :], ACT.Copy)
                last.then_inc(v_done, 1)

            def maxima_out(a):
                if a.k.kind != "soft":
                    return
                a.wait(mpt_done, soft_(a.n))
                a.wait(b_done[G - 1], attn_(a.n), 1)
                nc.scalar.activation(mt[0:3 * H, :], bank_m[0:3 * H, 0:L // 2].bitcast(BF16), ACT.Copy).then_inc(mt_done, 1)

            def weights_out(a, g):
                a.wait(b_done[g], attn_(a.n))
                if g == 1:
                    a.wait(o_done, all_(a.n), 1)
                else:
                    a.wait(pv_done[g - 2 if g else 2], attn_(a.n), 0 if g else 1)
                if a.k.kind == "soft":
                    n, q = (128, 64) if a.k.windows == 2 else (a.k.keys, L)
                    nc.scalar.activation(pt[g % 2][0:n, 0:J * q], bank_b[g % 2][0:n, 0:J * q], ACT.Exp, scale=SCALE).then_inc(pt_done[g], 1)
                else:
                    nc.scalar.activation(pt[g % 2][0:LC, :], bank_b[g % 2][0:LC, :], ACT.Copy).then_inc(pt_done[g], 1)

            def top_exp(a):
                if a.k.kind != "topk":
                    return
                for g in range(G):
                    a.wait(tmr_done[g], topk_(a.n))
                    a.wait(p_done[g], topk_(a.n), 1)
                    for j in range(J):
                        h = g * J + j
                        last = nc.scalar.activation(ex[:, h * LC:(h + 1) * LC], bank_a[g % 2][:, j * LC:(j + 1) * LC], ACT.Exp,
                                                    bias=nbias[:, h:h + 1], scale=SCALE)
                    last.then_inc(a_free[g], 1)

            def hidden_out(a):
                if a.k.attn:
                    return
                u, k = a.u, a.k
                a.wait(proj_done, all_(a.n))
                a.wait(o_done, all_(a.n), 2)
                for c in range(CH):
                    last = nc.scalar.activation(act[u][:, c * L:(c + 1) * L], bank_b[u][:, c * L:(c + 1) * L], k.act, bias=bcol(k, "b1", c))
                last.then_inc(act_done, 1)

            def gated(a, dst, src):
                k = a.k
                if k.gate is not None:
                    return nc.scalar.activation(dst, src, ACT.Identity, bias=gbias[:, a.one(k.gate * B)],
                                                scale=mods[:, a.one((2 * NMOD + k.gate) * B)])
                if k.bias:
                    return nc.scalar.activation(dst, src, ACT.Identity, bias=bprime[:, a.n:a.n + 1])
                return nc.scalar.activation(dst, src, ACT.Copy)

            def result_out(a):
                a.wait(o_done, all_(a.n))
                if a.k.attn:
                    a.wait(otn_done, attn_(a.n), 1)
                    nc.scalar.activation(ot[:], bank_o[:, 0:2 * L], ACT.Copy).then_inc(o_free, 1)
                else:
                    a.wait(yb_done, all_(a.n), 1)
                    gated(a, yt[:], bank_o[:, 0:L]).then_inc(o_free, 1)

            def heads_out(a):
                if not a.k.attn:
                    return
                a.wait(ont_done, attn_(a.n))
                nc.scalar.activation(ont[:], bank_f[:, 0:L], ACT.Copy).then_inc(ontc_done, 1)

            def branch_out(a):
                if not a.k.attn:
                    return
                a.wait(y_done, attn_(a.n))
                gated(a, yt[:], bank_f[:, 0:L]).then_inc(yt_done, 1)

            def step(done, now, nxt, aft):
                attn = now is not None and now.k.attn
                if nxt is not None:
                    modulate(nxt)
                if attn:
                    maxima_out(now)
                    weights_out(now, 0)
                if nxt is not None:
                    qkv_out(nxt)
                if attn:
                    weights_out(now, 1)
                if done is not None:
                    if done.first and done.n == 0:
                        sc.wait_ge(gb_made, 1)
                    heads_out(done)
                if attn:
                    weights_out(now, 2)
                if done is not None:
                    branch_out(done)
                if attn:
                    weights_out(now, 3)
                if now is not None:
                    result_out(now)
                if nxt is not None:
                    top_exp(nxt)
                    hidden_out(nxt)

            pipeline(sc, step)

        @block.vector
        def _(ve):
            ve.wait_ge(small_in, 64)
            nc.vector.tensor_copy(identb[:], ident)
            nc.vector.tensor_copy(sel[:].rearrange("p (h n) -> p h n", h=H), selcol[:, :, None].broadcast_to([128, H, 128])).then_inc(consts_made, 1)
            ve.wait_ge(ctx_in, 32)
            for b in range(B):
                last = nc.vector.bn_stats(cstat[:, 6 * b:6 * b + 6], ctxn_sb[:, b * C:(b + 1) * C])
            last.then_inc(c_stat, 1)
            ve.wait_ge(c_stat, 1)
            for b in range(B):
                last = nc.vector.bn_aggr(cmv[:, 2 * b:2 * b + 2], cstat[:, 6 * b:6 * b + 6])
            last.then_inc(c_aggr, 1)
            ve.wait_ge(mods_mm, 1)
            nc.vector.tensor_tensor(mods[:].rearrange("p (v b) -> p v b", b=B), bank_p[:, 0:NVEC * B].rearrange("p (v b) -> p v b", b=B),
                                    bmod_sb[:, :, None].broadcast_to([128, NVEC, B]), ALU.add).then_inc(mods_add, 1)
            ve.wait_ge(mods_add, 1)
            nc.vector.tensor_scalar(mods[:, 0:NMOD * B], mods[:, 0:NMOD * B], 1.0, None, ALU.add).then_inc(mods_made, 1)
            ve.wait_ge(c_rstd, 1)
            for e in range(2):
                for b in range(B):
                    last = nc.vector.tensor_scalar(
                        cnorm[:, (e * B + b) * C:(e * B + b + 1) * C], ctxn_sb[:, b * C:(b + 1) * C], cmv[:, 2 * b:2 * b + 1],
                        crstd[:, e * B + b:e * B + b + 1], ALU.subtract, ALU.mult)
                last.then_inc(c_norm, 1)
            ve.wait_ge(x_in, 32)

            def stats(a):
                u = a.u
                if a.n:
                    a.wait(xadd_done, all_(a.n - 1))
                a.wait(rstd_done, all_(a.n), 2)
                nc.vector.bn_stats(stat[:, 6 * u:6 * u + 6], x_sb[:, a.span(C)]).then_inc(st_done, 1)
                a.wait(st_done, all_(a.n), carry=(x_in, 32))
                nc.vector.bn_aggr(mv[:, 2 * u:2 * u + 2], stat[:, 6 * u:6 * u + 6]).then_inc(aggr_done, 1)

            def normalise(a):
                u = a.u
                a.wait(rstd_done, all_(a.n))
                a.wait(xnt_done, all_(a.n), 2)
                nc.vector.tensor_scalar(xn[u][:], x_sb[:, a.span(C)], mv[:, 2 * u:2 * u + 1], rstd[:, u:u + 1],
                                        ALU.subtract, ALU.mult).then_inc(xn_done, 1)

            def rotate(a):
                if not (a.k.attn and a.k.rope):
                    return
                u, n, base = a.u, a.k.keys, rope_(a.n)
                parts = [(0, L, "cos", "sin")]
                parts.append((L, n, "cosc", "sinc") if a.k.ctx is not None else (L, n, "cos", "sin"))
                a.wait(proj_done, all_(a.n))
                a.wait(qk_done, attn_(a.n), 1)
                for at, m, c, s in parts:
                    last = nc.vector.tensor_tensor(ropec[:, at:at + m], bank_p[:, at:at + m], c_sb[:, CCOL[c]:CCOL[c] + m], ALU.mult)
                last.then_inc(ropec_done, 1)
                for at, m, c, s in parts:
                    last = nc.vector.tensor_tensor(ropes[:, at:at + m], bank_p[:, 256 + at:256 + at + m], c_sb[:, CCOL[s]:CCOL[s] + m], ALU.mult)
                last.then_inc(ropes_done, 1)
                a.wait(ropec_done, base)
                a.wait(ropes_done, base)
                a.wait(o_done, all_(a.n), 2)
                nc.vector.tensor_tensor(qk[u][:, 0:L + n], ropec[:, 0:L + n], ropes[:, 0:L + n], ALU.add).then_inc(qk_done, 1)

            def maximum(a, g):
                n = L // a.k.windows if a.k.ctx is None else LC
                a.wait(a_done[g], attn_(a.n))
                a.wait(mparts_done, soft_(a.n), 1)
                nc.vector.tensor_reduce(nmax[:, g * J:(g + 1) * J], heads4(bank_a[g % 2][:, 0:J * n], n), AX, ALU.max,
                                        negate=True).then_inc(a_free[g], 1)

            def split(a):
                base = soft_(a.n)
                for g in range(G):
                    a.wait(a_free[g], attn_(a.n))
                a.wait(mpt_done, base, 1)
                nc.vector.tensor_copy(mparts[:, 0:H], nmax[:]).then_inc(m1_done, 1)
                a.wait(m1_done, base)
                nc.vector.tensor_tensor(mres[:], nmax[:], mparts[:, 0:H], ALU.subtract).then_inc(r1_done, 1)
                a.wait(r1_done, base)
                nc.vector.tensor_copy(mparts[:, H:2 * H], mres[:]).then_inc(m2_done, 1)
                a.wait(m2_done, base)
                nc.vector.tensor_tensor(mparts[:, 2 * H:3 * H], mres[:], mparts[:, H:2 * H], ALU.subtract).then_inc(mparts_done, 1)

            def take_top(a, g):
                base = topk_(a.n)
                heads = range(g * J, (g + 1) * J)
                a.wait(a_done[g], attn_(a.n), carry=(x_in, 32))
                a.wait(p_done[g], base, 1, carry=(x_in, 32))
                for h in heads:
                    last = nc.vector.max(top[:, 16 * h:16 * h + 8], bank_a[g % 2][:, h % J * LC:(h % J + 1) * LC])
                last.then_inc(t8_done[g], 1)
                a.wait(t8_done[g], base)
                nc.vector.tensor_scalar(nbias[:, g * J:(g + 1) * J], top[:].rearrange("p (h e) -> p h e", e=16)[:, g * J:(g + 1) * J, 0],
                                        -SCALE, None, ALU.mult)
                for h in heads:
                    last = nc.vector.match_replace(s3[:, h * LC:(h + 1) * LC], top[:, 16 * h:16 * h + 8],
                                                   bank_a[g % 2][:, h % J * LC:(h % J + 1) * LC], TAKEN)
                last.then_inc(tmr_done[g], 1)
                a.wait(tmr_done[g], base, carry=(x_in, 32))
                for h in heads:
                    last = nc.vector.max(top[:, 16 * h + 8:16 * h + 16], s3[:, h * LC:(h + 1) * LC])
                last.then_inc(t16_done[g], 1)
                a.wait(t16_done[g], base, carry=(x_in, 32))
                for h in heads:
                    last = nc.vector.match_replace(s3[:, h * LC:(h + 1) * LC], top[:, 16 * h + 8:16 * h + 16],
                                                   s3[:, h * LC:(h + 1) * LC], TAKEN)
                last.then_inc(s3_done[g], 1)

            def row_stage(a, g):
                if a.k.kind == "soft":
                    maximum(a, g)
                elif a.k.kind == "topk":
                    take_top(a, g)

            def divide(a):
                if not a.k.attn:
                    return
                a.wait(otn_done, attn_(a.n))
                f = bank_f[:, 0:4 * 64].rearrange("p (g r) -> p g r", g=G)
                nc.vector.reciprocal(rec[:].rearrange("p (g j) -> p g j", g=G), f[:, :, 32:36]).then_inc(rec_done, 1)
                a.wait(rec_done, attn_(a.n))
                a.wait(ont_done, attn_(a.n), 1)
                nc.vector.tensor_tensor(
                    on[:].rearrange("p (g j d) -> p g j d", g=G, j=J), f[:, :, 0:32].rearrange("p g (j d) -> p g j d", d=D),
                    rec[:].rearrange("p (g j) -> p g j", g=G)[:, :, :, None].broadcast_to([128, G, J, D]), ALU.mult).then_inc(on_done, 1)

            def add(a):
                a.wait(yb_done, all_(a.n))
                nc.vector.tensor_tensor(x_sb[:, a.span(C)], x_sb[:, a.span(C)], bank_f[:, 0:C], ALU.add).then_inc(xadd_done, 1)

            def hidden_gate(a):
                if a.k.attn or a.k.act != ACT.Silu:
                    return
                u = a.u
                a.wait(act_done, mlp_(a.n))
                for c in range(CH):
                    last = nc.vector.scalar_tensor_tensor(
                        out=hid[u][:, c * L:(c + 1) * L], in0=bank_a[u][:, c * L:(c + 1) * L], scalar=bcol(a.k, "b1", CH + c),
                        in1=act[u][:, c * L:(c + 1) * L], op0=ALU.add, op1=ALU.mult)
                last.then_inc(hid_done, 1)

            def step(done, now, nxt, aft):
                if done is not None:
                    divide(done)
                if now is None and nxt is not None:
                    stats(nxt)
                    normalise(nxt)
                if aft is not None:
                    stats(aft)
                if nxt is not None:
                    rotate(nxt)
                if aft is not None:
                    normalise(aft)
                if nxt is not None:
                    row_stage(nxt, 0)
                if done is not None:
                    add(done)
                if nxt is not None:
                    for g in range(1, G):
                        row_stage(nxt, g)
                    if nxt.k.kind == "soft":
                        split(nxt)
                    hidden_gate(nxt)
                if now is None and nxt is not None:
                    ve.wait_ge(bp_mm, 1)
                    for i, n in enumerate(BIASED):
                        nc.vector.tensor_tensor(bprime[:, n:n + 1], bank_f[:, i:i + 1], bcol(BLOCKS[n], "o"), ALU.add)
                    for n, k in enumerate(BLOCKS):
                        if not k.attn:
                            last = nc.vector.tensor_copy(bprime[:, n:n + 1], bcol(k, "b2"))
                    last.then_inc(bp_made, 1)
                    ve.wait_ge(bp_made, 1)
                    for n, k in enumerate(BLOCKS):
                        if k.gate is not None:
                            gate = mods[:, (2 * NMOD + k.gate) * B:(2 * NMOD + k.gate + 1) * B]
                            last = nc.vector.tensor_scalar(gbias[:, k.gate * B:(k.gate + 1) * B], gate, bprime[:, n:n + 1], None, ALU.mult)
                    last.then_inc(gb_made, 1)

            pipeline(ve, step)

        @block.tensor
        def _(pe):
            pe.wait_ge(wmod_in, 16)
            pe.wait_ge(silu_c, 1)
            for v in range(NVEC):
                m = v % NMOD if v < 2 * NMOD else v - 2 * NMOD
                src = cond_sb if MODS[m].startswith("L3") else scond_sb
                last = nc.tensor.matmul(bank_p[:, v * B:(v + 1) * B], wmod_sb[:, v * C:(v + 1) * C], src[:], start=True, stop=True)
            last.then_inc(mods_mm, 1)
            for i in range(4):
                if i % 2 == 0:
                    pe.wait_ge(c_norm, i // 2 + 1)
                bank = (bank_b[0], bank_b[1], bank_o, bank_f)[i]
                for r in range(4):
                    at = (4 * i + r) * C
                    last = nc.tensor.transpose(bank[:, r * LC:(r + 1) * LC], cnorm[:, at:at + C], c_sb[0:LC, 0:LC])
                last.then_inc(c_tr, 1)
            for s in w_in:
                pe.wait_ge(s, 16)
            pe.wait_ge(c_out, 10)
            for i, n in enumerate(BIASED):
                last = nc.tensor.matmul(bank_f[:, i:i + 1], w(BLOCKS[n], "o"), bcol(BLOCKS[n], "v"), start=True, stop=True)
            last.then_inc(bp_mm, 1)
            pe.wait_ge(mods_made, 1)
            pe.wait_ge(consts_made, 1)

            def transpose_x(a):
                a.wait(xn_done, all_(a.n))
                a.wait(ht_done, all_(a.n), 1)
                if a.first:
                    if a.n and BLOCKS[a.n - 1].attn:
                        pe.wait_ge(qk_done, attn_(a.n))
                elif a.k.attn:
                    a.wait(qk_done, attn_(a.n), 1)
                nc.tensor.transpose(bank_p[:, 0:L], xn[a.u][:], ident).then_inc(xnt_done, 1)

            def project(a):
                if not a.k.attn:
                    return
                u, k, n = a.u, a.k, a.k.keys
                a.wait(ht_done, all_(a.n))
                if k.ctx is not None:
                    a.wait(ctx_copied, cross_(a.n))
                src = cslot[u][:, 0:n] if k.ctx is not None else ht[u][:]
                nc.tensor.matmul(bank_p[:, 0:L], w(k, "q"), ht[u][:], start=True, stop=True)
                nc.tensor.matmul(bank_p[:, L:L + n], w(k, "k"), src, start=True, stop=True)
                if k.rope:
                    nc.tensor.matmul(bank_p[:, 256:256 + L], w(k, "qr"), ht[u][:], start=True, stop=True)
                    nc.tensor.matmul(bank_p[:, 384:384 + n], w(k, "kr"), src, start=True, stop=True)
                a.wait(v_done, attn_(a.n), 1)
                if a.first:
                    if a.n:
                        pe.wait_ge(mt_done, soft_(a.n))
                elif k.kind == "soft":
                    a.wait(mt_done, soft_(a.n), 1)
                nc.tensor.matmul(bank_m[0:n, 128:256], src, w(k, "v"), start=True, stop=True).then_inc(proj_done, 1)

            def scores_by_row(a, g):
                u, k = a.u, a.k
                nw = k.windows
                n = L // nw if k.ctx is None else LC
                if g == 0:
                    a.wait(kbd_done, attn_(a.n))
                if a.first and g == 0 and a.n and BLOCKS[a.n - 1].act == ACT.Silu:
                    pe.wait_ge(hid_done, mlp_(a.n))
                a.wait(a_free[g - 2], attn_(a.n), 0 if g >= 2 else 1)
                for wd in range(nw):
                    out_rows = slice(64 * wd, 64 * wd + 64) if nw == 2 else slice(0, L)
                    rhs = heads4(kbd[u][:, 0:J * k.keys], k.keys)[:, :, wd * n:(wd + 1) * n]
                    queries = qgr[u][:, g * L + out_rows.start:g * L + out_rows.stop]
                    last = nc.tensor.matmul(bank_a[g % 2][out_rows, 0:J * n], queries, rhs, start=True, stop=True)
                last.then_inc(a_done[g], 1)

            def maxima_in(a):
                if a.k.kind != "soft":
                    return
                a.wait(mparts_done, soft_(a.n), carry=(consts_made, 1))
                a.wait(v_done, attn_(a.n), carry=(consts_made, 1))
                nc.tensor.transpose(bank_m[0:3 * H, 0:L // 2].bitcast(BF16), mparts[:], identb[:]).then_inc(mpt_done, 1)

            def scores_by_key(a, g):
                u, k = a.u, a.k
                bank = bank_b[g % 2]
                if a.first and g < 2 and a.n and not BLOCKS[a.n - 1].attn:
                    pe.wait_ge(act_done, mlp_(a.n))
                a.wait(pt_done[g - 2], attn_(a.n), 0 if g >= 2 else 1)
                if k.kind == "topk":
                    a.wait(p_done[g], topk_(a.n))
                    for j in range(J):
                        h = g * J + j
                        last = nc.tensor.transpose(bank[0:LC, j * L:(j + 1) * L], pn[:, h * LC:(h + 1) * LC], ident)
                    last.then_inc(b_done[g], 1)
                    return
                nw = k.windows
                n, q = (L // nw if k.ctx is None else LC), L // nw
                if g == 0:
                    a.wait(qbd_done, soft_(a.n))
                for wd in range(nw):
                    out_rows = slice(n * wd, n * wd + n)
                    rhs = heads4(qbd[u][:], L)[:, :, wd * q:(wd + 1) * q]
                    nc.tensor.matmul(bank[out_rows, 0:J * q], kgr[u][:, g * k.keys + n * wd:g * k.keys + n * wd + n], rhs,
                                     start=True, stop=False, skip_group_check=True)
                if g == 0:
                    a.wait(mt_done, soft_(a.n), carry=(consts_made, 1))
                for wd in range(nw):
                    out_rows = slice(n * wd, n * wd + n)
                    for j in range(J):
                        h = g * J + j
                        last = nc.tensor.matmul(bank[out_rows, j * q:(j + 1) * q], sel[:, h * 128:h * 128 + n], mt[:, wd * q:(wd + 1) * q],
                                                start=False, stop=True, skip_group_check=True)
                last.then_inc(b_done[g], 1)

            def weigh(a, g):
                u, k = a.u, a.k
                n = k.keys
                q = L // k.windows
                a.wait(pt_done[g], attn_(a.n))
                if g == 0:
                    a.wait(v_done, attn_(a.n))
                    a.wait(o_free, all_(a.n), 1)
                out_rows = slice(64 * (g % 2), 64 * (g % 2) + 64)
                for wd in range(k.windows):
                    at = g // 2 * L + wd * q
                    v = vwin[wd][u] if k.windows == 2 else vpad[u]
                    for j in range(J):
                        h = g * J + j
                        last = nc.tensor.matmul(bank_o[out_rows, at:at + q], v[0:n, h * 64:(h + 1) * 64], pt[g % 2][0:n, j * q:(j + 1) * q],
                                                start=(j == 0), stop=(j == J - 1), skip_group_check=True)
                last.then_inc(pv_done[g] if g < G - 1 else o_done, 1)

            def sums_back(a):
                if not a.k.attn:
                    return
                a.wait(o_free, all_(a.n))
                a.wait(xadd_done, all_(a.n), 1)
                if a.first and a.n == 0:
                    pe.wait_ge(bp_made, 1)
                for i in range(2):
                    last = nc.tensor.transpose(bank_f[:, i * L:(i + 1) * L], ot[:, i * L:(i + 1) * L], ident)
                last.then_inc(otn_done, 1)

            def heads_back(a):
                if not a.k.attn:
                    return
                a.wait(on_done, attn_(a.n))
                nc.tensor.transpose(bank_f[:, 0:L], on[:], ident).then_inc(ont_done, 1)

            def project_out(a):
                if not a.k.attn:
                    return
                a.wait(ontc_done, attn_(a.n))
                nc.tensor.matmul(bank_f[:, 0:L], w(a.k, "o"), ont[:], start=True, stop=True).then_inc(y_done, 1)

            def branch_back(a):
                if a.k.attn:
                    a.wait(yt_done, attn_(a.n))
                else:
                    a.wait(o_free, all_(a.n))
                    a.wait(xadd_done, all_(a.n), 1)
                nc.tensor.transpose(bank_f[:, 0:C], yt[:], ident).then_inc(yb_done, 1)

            def hidden(a):
                if a.k.attn:
                    return
                u, k = a.u, a.k
                a.wait(ht_done, all_(a.n))
                a.wait(act_done, mlp_(a.n), 2)
                if k.act == ACT.Silu:
                    a.wait(hid_done, mlp_(a.n), 2)
                if a.i is None and a.c < 2 and BLOCKS[a.n - 1].attn:
                    pe.wait_ge(pt_done[2 + u], attn_(a.n))
                    pe.wait_ge(a_free[2 + u], attn_(a.n))
                if k.act == ACT.Silu:
                    for c in range(CH):
                        nc.tensor.matmul(bank_a[u][:, c * L:(c + 1) * L], w(k, "w1", C, HID + c * C), ht[u][:], start=True, stop=True)
                for c in range(CH):
                    last = nc.tensor.matmul(bank_b[u][:, c * L:(c + 1) * L], w(k, "w1", C, c * C), ht[u][:], start=True, stop=True)
                last.then_inc(proj_done, 1)

            def down(a):
                u, k = a.u, a.k
                if k.act == ACT.Silu:
                    a.wait(hid_done, mlp_(a.n))
                else:
                    a.wait(act_done, mlp_(a.n))
                src = hid[u] if k.act == ACT.Silu else act[u]
                a.wait(o_free, all_(a.n), 1)
                for c in range(CH):
                    last = nc.tensor.matmul(bank_o[:, 0:L], w(k, "w2", C, c * C), src[:, c * L:(c + 1) * L], start=(c == 0), stop=(c == CH - 1))
                last.then_inc(o_done, 1)

            def step(done, now, nxt, aft):
                attn = now is not None and now.k.attn
                rows = nxt is not None and nxt.k.attn
                if nxt is not None:
                    transpose_x(nxt)
                if done is not None:
                    sums_back(done)
                if attn:
                    maxima_in(now)
                    scores_by_key(now, 0)
                if nxt is not None:
                    project(nxt)
                if attn:
                    scores_by_key(now, 1)
                    weigh(now, 0)
                elif now is not None:
                    down(now)
                if done is not None:
                    heads_back(done)
                if attn:
                    scores_by_key(now, 2)
                    weigh(now, 1)
                if done is not None:
                    project_out(done)
                if attn:
                    scores_by_key(now, 3)
                if rows:
                    scores_by_row(nxt, 0)
                if attn:
                    weigh(now, 2)
                if done is not None:
                    branch_back(done)
                if rows:
                    scores_by_row(nxt, 1)
                if attn:
                    weigh(now, 3)
                if rows:
                    scores_by_row(nxt, 2)
                    scores_by_row(nxt, 3)
                elif nxt is not None:
                    hidden(nxt)

            pipeline(pe, step)


def shape_constants():
    c = np.zeros((128, CTOT), np.float32)
    p = np.arange(128)
    c[:, 0:128] = np.eye(128)
    c[p, CCOL["headmask"] + p // D % J] = 1.0
    c[p, CCOL["groupmask"] + p // (D * J)] = 1.0
    r = np.arange(3 * H)
    c[r, CCOL["sel"] + r % H] = 1.0
    half = D // 2
    inv = (1.0 / np.float32(10000.0) ** (np.arange(half, dtype=np.float32) / np.float32(half))).astype(np.float32)
    sign = np.where(p % D < half, -1.0, 1.0).astype(np.float32)[:, None]
    for cs, sn, pos in (("cos", "sin", (np.arange(L) + SHIFT) % L), ("cosc", "sinc", np.arange(LC))):
        ang = pos.astype(np.float32)[None, :] * inv[p % half][:, None]
        c[:, CCOL[cs]:CCOL[cs] + len(pos)] = np.cos(ang)
        c[:, CCOL[sn]:CCOL[sn] + len(pos)] = np.sin(ang) * sign
    return c


def kernel(**inputs):
    import concourse.bacc as bacc
    from concourse.bass_utils import run_bass_kernel_spmd

    a = {k: np.asarray(v) for k, v in inputs.items()}

    def l0(s): return a["L0_xcond_" + s]
    def l1(s): return a["L1_xcond_" + s]
    def l2(s): return a["L2_xcond_" + s]
    def l3(s): return a["L3_xcond_" + s]

    def cut(m, i): return m[..., i * C:(i + 1) * C]

    ada, mod, l2q, l2k = (l0("w_ada"), l0("b_ada")), (l1("W_mod"), l1("b_mod")), (l2("Wss_q"), l2("bss_q")), (l2("Wss_kv"), l2("bss_kv"))
    l3n = [(l3(f"ln{i}_w").T, l3(f"ln{i}_b")) for i in (1, 2, 3)]
    scales = [(ada, 1), (ada, 4), (ada, 7), (mod, 1), (mod, 4), (l2q, 0), (l2k, 0)] + [(m, 0) for m in l3n]
    shifts = [(ada, 0), (ada, 3), (ada, 6), (mod, 0), (mod, 3), (l2q, 1), (l2k, 1)] + [(m, 1) for m in l3n]
    gates = [(ada, 2), (ada, 5), (ada, 8), (mod, 2), (mod, 5)]
    wmod = np.concatenate([cut(m[0], i) for m, i in scales + shifts + gates], axis=1)
    bmod = np.stack([cut(m[1], i) for m, i in scales + shifts + gates], axis=1)

    swap = (np.arange(C) // D) * D + (np.arange(C) + D // 2) % D

    def down(m): return m.reshape(CH, C, C).transpose(1, 0, 2).reshape(C, HID)

    def cols(v): return list(v.reshape(-1, C))

    w = {
        "sa0": [cut(l0("w_qkv"), 0), cut(l0("w_qkv"), 1), cut(l0("w_qkv"), 2), l0("w_so")],
        "xa0": [l0("w_q"), l0("w_kv"), l0("w_co")],
        "ml0": [l0("w_m1"), down(l0("w_m2"))],
        "sa1": [l1("W_qkv"), l1("W_proj")],
        "xa1": [l1("W_qc"), l1("W_kvc"), l1("W_cproj")],
        "ml1": [l1("W_mlp1"), down(l1("W_mlp2"))],
        "xa2": [l2("Wq"), l2("Wkv"), l2("Wp")],
        "sa3": [cut(l3("qkv_w").T, 0), cut(l3("qkv_w").T, 1), cut(l3("qkv_w").T, 0)[:, swap], cut(l3("qkv_w").T, 1)[:, swap],
                cut(l3("qkv_w").T, 2), l3("sa_out_w").T],
        "xa3": [l3("q_w").T, l3("k_w").T, l3("q_w").T[:, swap], l3("k_w").T[:, swap], l3("v_w").T, l3("ca_out_w").T],
        "ml3": [l3("ffn_w1").T, down(l3("ffn_w2").T)],
    }
    bs = {
        "sa0": cols(l0("b_qkv")) + cols(l0("b_so")), "xa0": cols(l0("b_q")) + cols(l0("b_kv")) + cols(l0("b_co")),
        "ml0": cols(l0("b_m1")) + cols(l0("b_m2")), "sa1": cols(l1("b_qkv")) + cols(l1("b_proj")),
        "xa1": cols(l1("b_qc")) + cols(l1("b_kvc")) + cols(l1("b_cproj")), "ml1": cols(l1("b_mlp1")) + cols(l1("b_mlp2")),
        "xa2": cols(l2("bq")) + cols(l2("bkv")) + cols(l2("bp")), "sa3": [], "xa3": [],
        "ml3": cols(l3("ffn_b1")) + cols(l3("ffn_b2")),
    }
    ctx = a["ctx_1024"]
    arrays = {
        "x": a["x"], "cond_t": a["cond_1024"].T, "ctx_n": ctx, "ctx_t": ctx.transpose(2, 0, 1).reshape(C, B * LC),
        "wmod": wmod, "bmod": bmod, "wts": np.concatenate([m for k in BLOCKS for m in w[k.name]], axis=1),
        "bias": np.stack([v for k in BLOCKS for v in bs[k.name]], axis=1), "consts": shape_constants(),
    }
    arrays = {f"in_{k}": np.ascontiguousarray(v) for k, v in arrays.items()}
    nc = bacc.Bacc("TRN2", target_bir_lowering=False, num_devices=1)
    args = [nc.dram_tensor(k, v.shape, mybir.dt.from_np(v.dtype), kind="ExternalInput").ap() for k, v in arrays.items()]
    args.append(nc.dram_tensor("out_0", (B, L, C), F32, kind="ExternalOutput").ap())
    build(nc, *args)
    r = run_bass_kernel_spmd(nc, [arrays], core_ids=[0])
    return r.results[0]["out_0"]
```

```python
from contextlib import ExitStack

import numpy as np

import concourse.bass as bass
from concourse import mybir

F32 = mybir.dt.float32
BF16 = mybir.dt.bfloat16
ALU = mybir.AluOpType
ACT = mybir.ActivationFunctionType
AX = mybir.AxisListType.X

B, L, C, LC = 8, 128, 128, 120
H = 16
D = C // H
G = 4
J = H // G
SHIFT = 32
HID = 512
CH = HID // C
SCALE = float(D) ** -0.5
S = H // 2
R = 2 * D
PARTS = 3
Q_SLOTS = [(0, 3, 1), (0, 3, 1), (0, 2, 1)]
K_SLOTS = [(0, 1, 3), (1, 1, 3), (2, 1, 2)]
TAKEN = -3.0e38

MODS = ["L0a", "L0c", "L0m", "L1a", "L1m", "L2q", "L2kv", "L31", "L32", "L33"]
GATED = 5
NMOD = len(MODS)
NVEC = 2 * NMOD + GATED


class Blk:
    def __init__(self, kind, name, mod=None, eps=1e-6, windows=1, ctx=None, rope=False, bias=True, gate=None, act=None):
        self.kind, self.name, self.mod, self.eps, self.windows = kind, name, mod, eps, windows
        self.ctx, self.rope, self.bias, self.gate, self.act = ctx, rope, bias, gate, act
        self.attn = kind != "mlp"
        self.keys = LC if ctx is not None else L


BLOCKS = [
    Blk("soft", "sa0", mod=0, windows=2, gate=0),
    Blk("topk", "xa0", mod=1, ctx=0, gate=1),
    Blk("mlp", "ml0", mod=2, gate=2, act=ACT.Silu),
    Blk("soft", "sa1", mod=3, gate=3),
    Blk("soft", "xa1", ctx=1),
    Blk("mlp", "ml1", mod=4, gate=4, act=ACT.Gelu_apprx_tanh),
    Blk("soft", "xa2", mod=5, eps=1e-5, ctx=2),
    Blk("soft", "sa3", mod=7, eps=1e-5, rope=True, bias=False),
    Blk("soft", "xa3", mod=8, eps=1e-5, ctx=0, rope=True, bias=False),
    Blk("mlp", "ml3", mod=9, eps=1e-5, act=ACT.Gelu),
]
NBLK = len(BLOCKS)
BIASED = [n for n, k in enumerate(BLOCKS) if k.bias and k.attn]

WCOL = {}
_at = 0
for _k in BLOCKS:
    for _w, _n in ((("q", C), ("k", C), ("qr", C * _k.rope), ("kr", C * _k.rope), ("v", C), ("o", C)) if _k.attn
                   else (("w1", HID * (2 if _k.act == ACT.Silu else 1)), ("w2", HID))):
        if _n:
            WCOL[_k.name, _w] = _at
            _at += _n
WTOT = _at
WSPLIT = [WCOL["xa0", "q"], WCOL["ml0", "w1"], WCOL["sa1", "q"], WCOL["xa2", "q"], WTOT]

BCOL = {}
_at = 0
for _k in BLOCKS:
    for _w, _n in ((("q", 1), ("k", 1), ("v", 1), ("o", 1)) if _k.attn
                   else (("b1", CH * (2 if _k.act == ACT.Silu else 1)), ("b2", 1))):
        if _k.bias:
            BCOL[_k.name, _w] = _at
            _at += _n
BTOT = _at

CCOL = {"ident": 0, "headmask": 128, "sel": 130, "cos": 146, "sin": 274, "cosc": 402, "sinc": 522}
CTOT = 642


def build(nc, x, cond_t, ctx_n, ctx_t, wmod, bmod, wts, bias, consts, out, scratch):
    with ExitStack() as ctx:
        def sb(name, shape, dt=F32):
            return ctx.enter_context(nc.sbuf_tensor(name, shape, dt))

        def sem(name):
            return ctx.enter_context(nc.semaphore(name))

        def sems(name, n=G):
            return [sem(f"{name}{i}") for i in range(n)]

        bank_a = [ctx.enter_context(nc.psum_tensor(f"bank_a{i}", [128, 512], F32)) for i in range(2)]
        bank_b = [ctx.enter_context(nc.psum_tensor(f"bank_b{i}", [128, 512], F32)) for i in range(2)]
        bank_o = ctx.enter_context(nc.psum_tensor("bank_o", [128, 512], F32))
        bank_p = ctx.enter_context(nc.psum_tensor("bank_p", [128, 512], F32))
        bank_f = ctx.enter_context(nc.psum_tensor("bank_f", [128, 512], F32))
        bank_m = ctx.enter_context(nc.psum_tensor("bank_m", [128, 512], F32))

        x_sb = sb("x_sb", [128, B * C])
        w_sb = sb("w_sb", [128, WTOT])
        b_sb = sb("b_sb", [128, BTOT])
        c_sb = sb("c_sb", [128, CTOT])
        wmod_sb = sb("wmod_sb", [128, NVEC * C])
        bmod_sb = sb("bmod_sb", [128, NVEC])
        cond_sb = sb("cond_sb", [128, B])
        scond_sb = sb("scond_sb", [128, B])
        mods = sb("mods", [128, NVEC * B])
        bprime = sb("bprime", [128, NBLK])
        gbias = sb("gbias", [128, GATED * B])
        ctxn_sb = sb("ctxn_sb", [LC, B * C])
        ctx_sb = [sb(f"ctx_sb{i}", [128, B * LC]) for i in range(3)]
        cstat = sb("cstat", [LC, B * 6])
        cmv = sb("cmv", [LC, B * 2])
        ceps = sb("ceps", [LC, 2 * B])
        crstd = sb("crstd", [LC, 2 * B])
        cnorm = sb("cnorm", [LC, 2 * B * C])
        half_neg = sb("half_neg", [128, 2 * B])
        ident = c_sb[:, 0:128]
        identb = sb("identb", [128, 128], BF16)
        selcol = c_sb[:, CCOL["sel"]:CCOL["sel"] + H]
        sel = sb("sel", [128, H * 128], BF16)
        headmask = [c_sb[:, CCOL["headmask"] + j:CCOL["headmask"] + j + 1] for j in range(2)]

        stat = sb("stat", [128, 2 * 6])
        mv = sb("mv", [128, 2 * 2])
        vareps = sb("vareps", [128, 2])
        rstd = sb("rstd", [128, 2])
        xn = [sb(f"xn{i}", [128, C]) for i in range(2)]
        ht = [sb(f"ht{i}", [128, L]) for i in range(2)]
        cslot = [sb(f"cslot{i}", [128, LC]) for i in range(2)]
        qk = [sb(f"qk{i}", [128, 2 * L]) for i in range(2)]
        ropec = sb("ropec", [128, 2 * L])
        ropes = sb("ropes", [128, 2 * L])
        parts = [sb(f"parts{i}", [128, PARTS * 2 * L], BF16) for i in range(2)]
        pres = [sb(f"pres{i}", [128, 2 * L]) for i in range(2)]
        qst = [sb(f"qst{i}", [128, S * L], BF16) for i in range(2)]
        kst = [sb(f"kst{i}", [128, S * L], BF16) for i in range(2)]
        qbd = [sb(f"qbd{i}", [128, 2 * S * L], BF16) for i in range(2)]
        vpad = [sb(f"vpad{i}", [128, H * 64]) for i in range(2)]
        vwin = [[sb(f"vwin{w}_{i}", [128, H * 64]) for i in range(2)] for w in range(2)]
        nmax = sb("nmax", [128, H])
        mres = sb("mres", [128, H])
        mparts = sb("mparts", [128, 3 * H], BF16)
        mt = sb("mt", [128, L], BF16)
        pt = [sb(f"pt{i}", [128, 512]) for i in range(2)]
        ot = sb("ot", [128, 2 * L])
        rec = sb("rec", [128, H])
        on = sb("on", [128, C])
        ont = sb("ont", [128, L])
        yt = sb("yt", [128, L])
        top = sb("top", [128, H * 16])
        nbias = sb("nbias", [128, H])
        s3 = sb("s3", [128, H * LC])
        ex = sb("ex", [128, H * LC])
        pn = sb("pn", [128, H * LC])
        act = [sb(f"act{i}", [128, HID]) for i in range(2)]
        hid = [sb(f"hid{i}", [128, HID]) for i in range(2)]

        x_in, w_in, small_in, wmod_in, ctx_in = sem("x_in"), sems("w_in", 5), sem("small_in"), sem("wmod_in"), sem("ctx_in")
        silu_c, consts_made, pads_zero, pads_made = sem("silu_c"), sem("consts_made"), sem("pads_zero"), sem("pads_made")
        mods_mm, mods_add, mods_made, bp_mm, bp_made = (
            sem("mods_mm"), sem("mods_add"), sem("mods_made"), sem("bp_mm"), sem("bp_made"))
        gb_made = sem("gb_made")
        c_stat, c_aggr, c_eps, c_rstd, c_norm, c_tr, c_out = (
            sem("c_stat"), sem("c_aggr"), sem("c_eps"), sem("c_rstd"), sem("c_norm"), sem("c_tr"), sem("c_out"))
        st_done, aggr_done, eps_done, rstd_done, xn_done = (
            sem("st_done"), sem("aggr_done"), sem("eps_done"), sem("rstd_done"), sem("xn_done"))
        xnt_done, ht_done, qkp_done, proj_done = sem("xnt_done"), sem("ht_done"), sem("qkp_done"), sem("proj_done")
        ph_done, pr_done, pm_done, parts_done = sem("ph_done"), sem("pr_done"), sem("pm_done"), sem("parts_done")
        parts_out, q_in, k_in = sems("parts_out", 2), sems("q_in", 2), sems("k_in", 2)
        ctx_copied, ropec_done, ropes_done = sem("ctx_copied"), sem("ropec_done"), sem("ropes_done")
        qk_done, v_done, qbd_done = sem("qk_done"), sem("v_done"), sem("qbd_done")
        a_done, a_free = sems("a_done"), sems("a_free")
        m1_done, r1_done, m2_done, mparts_done = sem("m1_done"), sem("r1_done"), sem("m2_done"), sem("mparts_done")
        mpt_done, mt_done = sem("mpt_done"), sem("mt_done")
        t8_done, tmr_done, t16_done, s3_done, mask_done, p_done = (
            sems("t8_done"), sems("tmr_done"), sems("t16_done"), sems("s3_done"), sems("mask_done"), sems("p_done"))
        b_done, pt_done, pv_done = sems("b_done"), sems("pt_done"), sems("pv_done", G - 1)
        o_done, o_free = sem("o_done"), sem("o_free")
        otn_done, rec_done, on_done, ont_done, ontc_done = (
            sem("otn_done"), sem("rec_done"), sem("on_done"), sem("ont_done"), sem("ontc_done"))
        y_done, yt_done, yb_done, xadd_done = sem("y_done"), sem("yt_done"), sem("yb_done"), sem("xadd_done")
        act_done, hid_done = sem("act_done"), sem("hid_done")
        stored = sem("stored")

        def before(n, *kinds):
            return B * sum(k.kind in kinds for k in BLOCKS[:n])

        def all_(n):
            return B * n

        def xadd_(n):
            return all_(n) + 1

        def attn_(n):
            return before(n, "soft", "topk")

        def soft_(n):
            return before(n, "soft")

        def topk_(n):
            return before(n, "topk")

        def mlp_(n):
            return before(n, "mlp")

        def cross_(n):
            return B * sum(k.ctx is not None for k in BLOCKS[:n])

        def rope_(n):
            return B * sum(k.rope for k in BLOCKS[:n])

        class At:

            def __init__(self, eng, n, c, i=None, held=None):
                self.eng, self.n, self.c, self.i, self.held = eng, n, c, i, held
                self.k, self.u = BLOCKS[n], c % 2

            def value(self, scale, add):
                if self.i is None:
                    return scale * self.c + add
                key = (scale, scale * self.c + add)
                if key not in self.held:
                    self.held[key] = self.eng.snap(self.i * (2 * scale) + key[1])
                    self.eng.compute_val(self.held[key])
                return self.held[key]

            def span(self, width, at=0):
                return bass.ds(self.value(width, at), width)

            def one(self, at):
                return bass.ds(self.value(1, at), 1)

            def wait(self, semaphore, base, back=0, carry=None):
                count = self.count(base, back)
                if carry and self.i is not None:
                    self.eng.wait_ge(*carry)
                self.wait_count(semaphore, count)

            def count(self, base, back=0):
                return self.value(1, base + 1 - back)

            def wait_count(self, semaphore, count):
                if self.i is not None or count > 0:
                    self.eng.wait_ge(semaphore, count)

            def wait_dma(self, semaphores, base, dmas, back=0):
                self.wait_count(semaphores[self.u], self.count_dma(base, dmas, back))

            def count_dma(self, base, dmas, back=0):
                unit = 16 * dmas
                return self.value(unit // 2, unit * (base // 2 + 1 - back // 2) - unit // 2 * self.u)

            @property
            def first(self):
                return self.i is None and self.c == 0

        def pipeline(eng, step):
            def fixed(n, c):
                n, c = n + c // B, c % B
                return At(eng, n, c) if 0 <= n < NBLK else None

            near = (-1, 0, 1, 2, 3)
            for c in (-3, -2, -1):
                step(*(fixed(0, c + d) for d in near))
            for n in range(NBLK):
                step(*(fixed(n, d) for d in near))
                with eng.Fori(0, 2) as i:
                    for c in (1, 2):
                        held = {}
                        step(*(At(eng, n, c + d, i, held) for d in near))
                for c in (5, 6, 7):
                    step(*(fixed(n, c + d) for d in near))
            step(fixed(NBLK, -1), None, None, None, None)

        def w(k, what, n=C, at=0):
            c = WCOL[k.name, what] + at
            return w_sb[:, c:c + n]

        def bcol(k, what, at=0):
            c = BCOL[k.name, what] + at
            return b_sb[:, c:c + 1]

        def heads4(ap, n):
            return ap.rearrange("p (j n) -> p j n", n=n)

        def vspots(t, rows):
            base = t[rows, :]
            v = base.rearrange("p (g r) -> p g r", g=G)
            return v

        block = ctx.enter_context(nc.Block())

        @block.sync
        def _(sp):
            sp.dma_start(cond_sb[:], cond_t).then_inc(small_in, 16)
            sp.dma_start(bmod_sb[:], bmod).then_inc(small_in, 16)
            sp.dma_start(b_sb[:], bias).then_inc(small_in, 16)
            sp.dma_start(c_sb[:], consts).then_inc(small_in, 16)
            sp.dma_start(wmod_sb[:], wmod).then_inc(wmod_in, 16)
            sp.dma_start(ctx_sb[0][:], ctx_t).then_inc(ctx_in, 16)
            sp.dma_start(ctxn_sb[:].rearrange("p (b c) -> p b c", b=B), ctx_n.rearrange("b s c -> s b c")).then_inc(ctx_in, 16)
            lo = 0
            for s, hi in zip(w_in[1:], WSPLIT[1:]):
                lo = WSPLIT[w_in.index(s) - 1]
                sp.dma_start(w_sb[:, lo:hi], wts[:, lo:hi]).then_inc(s, 16)
            part_of = [scratch[u].rearrange("p q f t -> f (p q) t") for u in range(2)]

            def parts_to_slots(a):
                if not a.k.attn:
                    return
                u, base = a.u, attn_(a.n)
                made, used = a.count(base), a.count(base, 2)
                out, read = a.count_dma(base, 1), a.count_dma(base, len(Q_SLOTS), 2)
                a.wait_count(parts_done, made)
                a.wait_count(q_in[u], read)
                a.wait_count(k_in[u], read)
                sp.dma_start(part_of[u], parts[u][:].rearrange("f (pq t) -> f pq t", t=L)).then_inc(parts_out[u], 16)
                a.wait_count(parts_out[u], out)
                for i, (tensor, slots, sem_in) in enumerate(((qst[u], Q_SLOTS, q_in[u]), (kst[u], K_SLOTS, k_in[u]))):
                    a.wait_count((qbd_done, b_done[G - 1])[i], used)
                    at = 0
                    for first, n, times in slots:
                        src = scratch[u][first:first + n, i].rearrange("p (r s) t -> p r (s t)", s=S)
                        if times > 1:
                            src = src.broadcast_to([times, R, S * L])
                        sp.dma_start(tensor[at:at + n * times * R, :], src).then_inc(sem_in, 16)
                        at += n * times * R

            pipeline(sp, lambda done, now, nxt, aft, far: parts_to_slots(aft) if aft is not None else None)
            for b in range(B):
                sp.wait_ge(xadd_done, xadd_(NBLK - 1) + b + 1)
                sp.dma_start(out[b, SHIFT:L, :], x_sb[0:L - SHIFT, b * C:(b + 1) * C]).then_inc(stored, 16)
                sp.dma_start(out[b, 0:SHIFT, :], x_sb[L - SHIFT:L, b * C:(b + 1) * C]).then_inc(stored, 16)
            sp.wait_ge(stored, 2 * 16 * B)

        @block.gpsimd
        def _(pool):
            for t in vpad + vwin[0] + vwin[1]:
                nc.gpsimd.memset(t[:], 0.0)
            nc.gpsimd.memset(mt[:], 0.0)
            for t in qk:
                nc.gpsimd.memset(t[:], 0.0)
            nc.gpsimd.memset(half_neg[:], -0.5).then_inc(pads_zero, 1)
            pool.wait_ge(pads_zero, 1)
            for j in range(J):
                for t in vpad:
                    last = nc.gpsimd.memset(t[:].rearrange("p (g r) -> p g r", g=G)[:, :, 64 * j + 32 + j:64 * j + 33 + j], 1.0)
            last.then_inc(pads_zero, 1)
            pool.wait_ge(pads_zero, 2)
            for wd in range(2):
                for j in range(J):
                    for t in vwin[wd]:
                        last = nc.gpsimd.memset(
                            t[64 * wd:64 * wd + 64, :].rearrange("p (g r) -> p g r", g=G)[:, :, 64 * j + 32 + j:64 * j + 33 + j], 1.0)
            last.then_inc(pads_made, 1)
            pool.wait_ge(pads_made, 1)
            pool.wait_ge(c_aggr, 1)
            var = cmv[:].rearrange("p (b t) -> p b t", t=2)[:, :, 1]
            for e, eps in enumerate((1e-6, 1e-5)):
                last = nc.gpsimd.tensor_scalar(ceps[:, e * B:(e + 1) * B], var, eps, None, ALU.add)
            last.then_inc(c_eps, 1)
            pool.wait_ge(c_eps, 1)
            nc.gpsimd.tensor_tensor(crstd[:], ceps[:], half_neg[0:LC, :], ALU.pow).then_inc(c_rstd, 1)

            def rstd_of(a):
                u = a.u
                a.wait(aggr_done, all_(a.n), carry=(pads_made, 1))
                a.wait(xn_done, all_(a.n), 2, carry=(pads_made, 1))
                nc.gpsimd.tensor_scalar(vareps[:, u:u + 1], mv[:, 2 * u + 1:2 * u + 2], a.k.eps, None, ALU.add).then_inc(eps_done, 1)
                a.wait(eps_done, all_(a.n))
                nc.gpsimd.tensor_tensor(rstd[:, u:u + 1], vareps[:, u:u + 1], half_neg[:, 0:1], ALU.pow).then_inc(rstd_done, 1)

            def context_of(a):
                if a.k.ctx is None:
                    return
                if a.k.ctx and a.first:
                    pool.wait_ge(c_out, 10)
                if a.k.ctx == 0 and a.first:
                    pool.wait_ge(ctx_in, 32)
                a.wait(proj_done, all_(a.n), 2)
                nc.gpsimd.tensor_copy(cslot[a.u][:], ctx_sb[a.k.ctx][:, a.span(LC)]).then_inc(ctx_copied, 1)

            def low_part(a):
                if not a.k.attn:
                    return
                u, n = a.u, 2 * L
                a.wait(pm_done, attn_(a.n))
                nc.gpsimd.tensor_tensor(parts[u][:, 2 * n:3 * n], pres[u][:], parts[u][:, n:2 * n], ALU.subtract).then_inc(parts_done, 1)

            def keep_top(a):
                if a.k.kind != "topk":
                    return
                for g in range(G):
                    cols = slice(g * J * LC, (g + 1) * J * LC)
                    a.wait(s3_done[g], topk_(a.n), carry=(pads_made, 1))
                    nc.gpsimd.tensor_scalar(s3[:, cols], s3[:, cols], TAKEN, None, ALU.is_le).then_inc(mask_done[g], 1)
                    a.wait(mask_done[g], topk_(a.n))
                    a.wait(a_free[g], attn_(a.n))
                    a.wait(b_done[g], attn_(a.n), 1)
                    nc.gpsimd.tensor_tensor(pn[:, cols], ex[:, cols], s3[:, cols], ALU.mult).then_inc(p_done[g], 1)

            def step(done, now, nxt, aft, far):
                if far is not None:
                    rstd_of(far)
                if aft is not None:
                    low_part(aft)
                if far is not None:
                    context_of(far)
                if nxt is not None:
                    keep_top(nxt)

            pipeline(pool, step)

        @block.scalar
        def _(sc):
            sc.dma_start(x_sb[0:L - SHIFT, :].rearrange("p (b c) -> p b c", b=B), x[:, SHIFT:L, :].rearrange("b t c -> t b c")).then_inc(x_in, 16)
            sc.dma_start(x_sb[L - SHIFT:L, :].rearrange("p (b c) -> p b c", b=B), x[:, 0:SHIFT, :].rearrange("b t c -> t b c")).then_inc(x_in, 16)
            sc.dma_start(w_sb[:, 0:WSPLIT[0]], wts[:, 0:WSPLIT[0]]).then_inc(w_in[0], 16)
            sc.wait_ge(small_in, 64)
            nc.scalar.activation(scond_sb[:], cond_sb[:], ACT.Silu).then_inc(silu_c, 1)
            for i in range(2):
                sc.wait_ge(c_tr, i + 1)
                nc.scalar.activation(ctx_sb[1][:, i * 4 * LC:(i + 1) * 4 * LC], bank_b[i][:, 0:4 * LC], ACT.Copy).then_inc(c_out, 1)
            sc.wait_ge(mods_made, 1)
            kv = MODS.index("L2kv")
            for b in range(B):
                if b % 4 == 0:
                    sc.wait_ge(c_tr, 3 + b // 4)
                nc.scalar.activation(
                    ctx_sb[2][:, b * LC:(b + 1) * LC], (bank_o, bank_f)[b // 4][:, b % 4 * LC:(b % 4 + 1) * LC], ACT.Identity,
                    bias=mods[:, (NMOD + kv) * B + b:(NMOD + kv) * B + b + 1],
                    scale=mods[:, kv * B + b:kv * B + b + 1]).then_inc(c_out, 1)
            sc.preload_act_table(ACT.Exp)

            def modulate(a):
                a.wait(xnt_done, all_(a.n))
                a.wait(proj_done, all_(a.n), 2)
                if a.k.mod is None:
                    nc.scalar.activation(ht[a.u][:], bank_p[:, 0:L], ACT.Copy).then_inc(ht_done, 1)
                else:
                    nc.scalar.activation(ht[a.u][:], bank_p[:, 0:L], ACT.Identity, bias=mods[:, a.one((NMOD + a.k.mod) * B)],
                                         scale=mods[:, a.one(a.k.mod * B)]).then_inc(ht_done, 1)

            def qk_out(a):
                if not a.k.attn or a.k.rope:
                    return
                u, n, k = a.u, a.k.keys, a.k
                a.wait(qkp_done, attn_(a.n))
                a.wait(parts_done, attn_(a.n), 2)
                if a.first and a.n == 0:
                    sc.wait_ge(pads_made, 1)
                nc.scalar.activation(qk[u][:, 0:L], bank_p[:, 0:L], ACT.Identity, bias=bcol(k, "q"))
                nc.scalar.activation(qk[u][:, L:L + n], bank_p[:, L:L + n], ACT.Identity, bias=bcol(k, "k")).then_inc(qk_done, 1)

            def high_part(a):
                if not a.k.attn:
                    return
                u, base = a.u, attn_(a.n)
                a.wait(qk_done, base)
                a.wait_dma(parts_out, base, 1, 2)
                nc.scalar.activation(parts[u][:, 0:2 * L], qk[u][:], ACT.Copy).then_inc(ph_done, 1)

            def v_out(a):
                if not a.k.attn:
                    return
                u, n, k = a.u, a.k.keys, a.k
                a.wait(proj_done, all_(a.n))
                a.wait(o_done, all_(a.n), 2)
                for wd in range(k.windows):
                    rows = slice(64 * wd, 64 * wd + 64) if k.windows == 2 else slice(0, n)
                    dst = vwin[wd][u] if k.windows == 2 else vpad[u]
                    for j in range(J):
                        last = nc.scalar.activation(
                            dst[rows, :].rearrange("p (g r) -> p g r", g=G)[:, :, 72 * j:72 * j + D],
                            bank_m[rows, 128:256].rearrange("p (g j d) -> p g j d", g=G, j=J)[:, :, j, :], ACT.Copy)
                last.then_inc(v_done, 1)

            def maxima_out(a):
                if a.k.kind != "soft":
                    return
                a.wait(mpt_done, soft_(a.n))
                a.wait(b_done[G - 1], attn_(a.n), 1)
                nc.scalar.activation(mt[0:3 * H, :], bank_m[0:3 * H, 0:L // 2].bitcast(BF16), ACT.Copy).then_inc(mt_done, 1)

            def weights_out(a, g):
                a.wait(b_done[g], attn_(a.n))
                if g == 1:
                    a.wait(o_done, all_(a.n), 1)
                else:
                    a.wait(pv_done[g - 2 if g else 2], attn_(a.n), 0 if g else 1)
                if a.k.kind == "soft":
                    n, q = (128, 64) if a.k.windows == 2 else (a.k.keys, L)
                    nc.scalar.activation(pt[g % 2][0:n, 0:J * q], bank_b[g % 2][0:n, 0:J * q], ACT.Exp, scale=SCALE).then_inc(pt_done[g], 1)
                else:
                    nc.scalar.activation(pt[g % 2][0:LC, :], bank_b[g % 2][0:LC, :], ACT.Copy).then_inc(pt_done[g], 1)

            def top_exp(a):
                if a.k.kind != "topk":
                    return
                for g in range(G):
                    a.wait(tmr_done[g], topk_(a.n))
                    a.wait(p_done[g], topk_(a.n), 1)
                    for j in range(J):
                        h = g * J + j
                        last = nc.scalar.activation(ex[:, h * LC:(h + 1) * LC], bank_a[g % 2][:, j * LC:(j + 1) * LC], ACT.Exp,
                                                    bias=nbias[:, h:h + 1], scale=SCALE)
                    last.then_inc(a_free[g], 1)

            def hidden_out(a):
                if a.k.attn:
                    return
                u, k = a.u, a.k
                a.wait(proj_done, all_(a.n))
                a.wait(o_done, all_(a.n), 2)
                for c in range(CH):
                    last = nc.scalar.activation(act[u][:, c * L:(c + 1) * L], bank_b[u][:, c * L:(c + 1) * L], k.act, bias=bcol(k, "b1", c))
                last.then_inc(act_done, 1)

            def gated(a, dst, src):
                k = a.k
                if k.gate is not None:
                    return nc.scalar.activation(dst, src, ACT.Identity, bias=gbias[:, a.one(k.gate * B)],
                                                scale=mods[:, a.one((2 * NMOD + k.gate) * B)])
                if k.bias:
                    return nc.scalar.activation(dst, src, ACT.Identity, bias=bprime[:, a.n:a.n + 1])
                return nc.scalar.activation(dst, src, ACT.Copy)

            def result_out(a):
                a.wait(o_done, all_(a.n))
                if a.k.attn:
                    a.wait(otn_done, attn_(a.n), 1)
                    nc.scalar.activation(ot[:], bank_o[:, 0:2 * L], ACT.Copy).then_inc(o_free, 1)
                else:
                    a.wait(yb_done, all_(a.n), 1)
                    gated(a, yt[:], bank_o[:, 0:L]).then_inc(o_free, 1)

            def heads_out(a):
                if not a.k.attn:
                    return
                a.wait(ont_done, attn_(a.n))
                nc.scalar.activation(ont[:], bank_f[:, 0:L], ACT.Copy).then_inc(ontc_done, 1)

            def branch_out(a):
                if not a.k.attn:
                    return
                a.wait(y_done, attn_(a.n))
                gated(a, yt[:], bank_f[:, 0:L]).then_inc(yt_done, 1)

            def step(done, now, nxt, aft, far):
                attn = now is not None and now.k.attn
                if aft is not None:
                    modulate(aft)
                if aft is not None:
                    qk_out(aft)
                if attn:
                    maxima_out(now)
                if aft is not None:
                    high_part(aft)
                if attn:
                    weights_out(now, 0)
                if nxt is not None:
                    v_out(nxt)
                if attn:
                    weights_out(now, 1)
                if done is not None:
                    heads_out(done)
                if attn:
                    weights_out(now, 2)
                if done is not None:
                    branch_out(done)
                if attn:
                    weights_out(now, 3)
                if now is not None:
                    result_out(now)
                    if now.first and now.n == 0:
                        sc.wait_ge(gb_made, 1)
                if nxt is not None:
                    top_exp(nxt)
                    hidden_out(nxt)

            pipeline(sc, step)

        @block.vector
        def _(ve):
            ve.wait_ge(small_in, 64)
            nc.vector.tensor_copy(identb[:], ident)
            nc.vector.tensor_copy(sel[:].rearrange("p (h n) -> p h n", h=H), selcol[:, :, None].broadcast_to([128, H, 128])).then_inc(consts_made, 1)
            ve.wait_ge(ctx_in, 32)
            for b in range(B):
                last = nc.vector.bn_stats(cstat[:, 6 * b:6 * b + 6], ctxn_sb[:, b * C:(b + 1) * C])
            last.then_inc(c_stat, 1)
            ve.wait_ge(c_stat, 1)
            for b in range(B):
                last = nc.vector.bn_aggr(cmv[:, 2 * b:2 * b + 2], cstat[:, 6 * b:6 * b + 6])
            last.then_inc(c_aggr, 1)
            ve.wait_ge(mods_mm, 1)
            nc.vector.tensor_tensor(mods[:].rearrange("p (v b) -> p v b", b=B), bank_p[:, 0:NVEC * B].rearrange("p (v b) -> p v b", b=B),
                                    bmod_sb[:, :, None].broadcast_to([128, NVEC, B]), ALU.add).then_inc(mods_add, 1)
            ve.wait_ge(mods_add, 1)
            nc.vector.tensor_scalar(mods[:, 0:NMOD * B], mods[:, 0:NMOD * B], 1.0, None, ALU.add).then_inc(mods_made, 1)
            ve.wait_ge(c_rstd, 1)
            for e in range(2):
                for b in range(B):
                    last = nc.vector.tensor_scalar(
                        cnorm[:, (e * B + b) * C:(e * B + b + 1) * C], ctxn_sb[:, b * C:(b + 1) * C], cmv[:, 2 * b:2 * b + 1],
                        crstd[:, e * B + b:e * B + b + 1], ALU.subtract, ALU.mult)
                last.then_inc(c_norm, 1)
            ve.wait_ge(x_in, 32)
            nc.vector.tensor_copy(rec[:, 0:1], ident[:, 0:1]).then_inc(xadd_done, 1)

            def stats(a):
                u = a.u
                if a.n:
                    a.wait(xadd_done, xadd_(a.n - 1))
                a.wait(rstd_done, all_(a.n), 2)
                nc.vector.bn_stats(stat[:, 6 * u:6 * u + 6], x_sb[:, a.span(C)]).then_inc(st_done, 1)
                a.wait(st_done, all_(a.n), carry=(x_in, 32))
                nc.vector.bn_aggr(mv[:, 2 * u:2 * u + 2], stat[:, 6 * u:6 * u + 6]).then_inc(aggr_done, 1)

            def normalise(a):
                u = a.u
                a.wait(rstd_done, all_(a.n))
                a.wait(xnt_done, all_(a.n), 2)
                nc.vector.tensor_scalar(xn[u][:], x_sb[:, a.span(C)], mv[:, 2 * u:2 * u + 1], rstd[:, u:u + 1],
                                        ALU.subtract, ALU.mult).then_inc(xn_done, 1)

            def rotate(a):
                if not (a.k.attn and a.k.rope):
                    return
                u, n, base = a.u, a.k.keys, rope_(a.n)
                parts = [(0, L, "cos", "sin")]
                parts.append((L, n, "cosc", "sinc") if a.k.ctx is not None else (L, n, "cos", "sin"))
                a.wait(qkp_done, attn_(a.n))
                a.wait(qk_done, attn_(a.n), 1)
                for at, m, c, s in parts:
                    last = nc.vector.tensor_tensor(ropec[:, at:at + m], bank_p[:, at:at + m], c_sb[:, CCOL[c]:CCOL[c] + m], ALU.mult)
                last.then_inc(ropec_done, 1)
                for at, m, c, s in parts:
                    last = nc.vector.tensor_tensor(ropes[:, at:at + m], bank_p[:, 256 + at:256 + at + m], c_sb[:, CCOL[s]:CCOL[s] + m], ALU.mult)
                last.then_inc(ropes_done, 1)
                a.wait(ropec_done, base)
                a.wait(ropes_done, base)
                a.wait(parts_done, attn_(a.n), 2)
                nc.vector.tensor_tensor(qk[u][:, 0:L + n], ropec[:, 0:L + n], ropes[:, 0:L + n], ALU.add).then_inc(qk_done, 1)

            def split_qk(a):
                if not a.k.attn:
                    return
                u, base, n = a.u, attn_(a.n), 2 * L
                high, middle = (parts[u][:, p * n:(p + 1) * n] for p in range(2))
                a.wait(ph_done, base)
                a.wait(parts_done, base, 2)
                nc.vector.tensor_tensor(pres[u][:], qk[u][:], high, ALU.subtract).then_inc(pr_done, 1)
                a.wait(pr_done, base)
                nc.vector.tensor_copy(middle, pres[u][:]).then_inc(pm_done, 1)

            def spread(a):
                if not a.k.attn:
                    return
                u = a.u
                a.wait_dma(q_in, attn_(a.n), len(Q_SLOTS))
                a.wait(b_done[G - 1], attn_(a.n), 2)
                for j in range(2):
                    last = nc.vector.tensor_scalar(qbd[u][:, j * S * L:(j + 1) * S * L], qst[u][:], headmask[j], None, ALU.mult)
                last.then_inc(qbd_done, 1)

            def maximum(a, g):
                n = L // a.k.windows if a.k.ctx is None else LC
                a.wait(a_done[g], attn_(a.n))
                a.wait(mparts_done, soft_(a.n), 1)
                nc.vector.tensor_reduce(nmax[:, g * J:(g + 1) * J], heads4(bank_a[g % 2][:, 0:J * n], n), AX, ALU.max,
                                        negate=True).then_inc(a_free[g], 1)

            def split(a):
                base = soft_(a.n)
                for g in range(G):
                    a.wait(a_free[g], attn_(a.n))
                a.wait(mpt_done, base, 1)
                nc.vector.tensor_copy(mparts[:, 0:H], nmax[:]).then_inc(m1_done, 1)
                a.wait(m1_done, base)
                nc.vector.tensor_tensor(mres[:], nmax[:], mparts[:, 0:H], ALU.subtract).then_inc(r1_done, 1)
                a.wait(r1_done, base)
                nc.vector.tensor_copy(mparts[:, H:2 * H], mres[:]).then_inc(m2_done, 1)
                a.wait(m2_done, base)
                nc.vector.tensor_tensor(mparts[:, 2 * H:3 * H], mres[:], mparts[:, H:2 * H], ALU.subtract).then_inc(mparts_done, 1)

            def take_top(a, g):
                base = topk_(a.n)
                heads = range(g * J, (g + 1) * J)
                a.wait(a_done[g], attn_(a.n), carry=(x_in, 32))
                a.wait(p_done[g], base, 1, carry=(x_in, 32))
                for h in heads:
                    last = nc.vector.max(top[:, 16 * h:16 * h + 8], bank_a[g % 2][:, h % J * LC:(h % J + 1) * LC])
                last.then_inc(t8_done[g], 1)
                a.wait(t8_done[g], base)
                nc.vector.tensor_scalar(nbias[:, g * J:(g + 1) * J], top[:].rearrange("p (h e) -> p h e", e=16)[:, g * J:(g + 1) * J, 0],
                                        -SCALE, None, ALU.mult)
                for h in heads:
                    last = nc.vector.match_replace(s3[:, h * LC:(h + 1) * LC], top[:, 16 * h:16 * h + 8],
                                                   bank_a[g % 2][:, h % J * LC:(h % J + 1) * LC], TAKEN)
                last.then_inc(tmr_done[g], 1)
                a.wait(tmr_done[g], base, carry=(x_in, 32))
                for h in heads:
                    last = nc.vector.max(top[:, 16 * h + 8:16 * h + 16], s3[:, h * LC:(h + 1) * LC])
                last.then_inc(t16_done[g], 1)
                a.wait(t16_done[g], base, carry=(x_in, 32))
                for h in heads:
                    last = nc.vector.match_replace(s3[:, h * LC:(h + 1) * LC], top[:, 16 * h + 8:16 * h + 16],
                                                   s3[:, h * LC:(h + 1) * LC], TAKEN)
                last.then_inc(s3_done[g], 1)

            def row_stage(a, g):
                if a.k.kind == "soft":
                    maximum(a, g)
                elif a.k.kind == "topk":
                    take_top(a, g)

            def divide(a):
                if not a.k.attn:
                    return
                a.wait(otn_done, attn_(a.n))
                f = bank_f[:, 0:4 * 64].rearrange("p (g r) -> p g r", g=G)
                nc.vector.reciprocal(rec[:].rearrange("p (g j) -> p g j", g=G), f[:, :, 32:36]).then_inc(rec_done, 1)
                a.wait(rec_done, attn_(a.n))
                nc.vector.tensor_tensor(
                    on[:].rearrange("p (g j d) -> p g j d", g=G, j=J), f[:, :, 0:32].rearrange("p g (j d) -> p g j d", d=D),
                    rec[:].rearrange("p (g j) -> p g j", g=G)[:, :, :, None].broadcast_to([128, G, J, D]), ALU.mult).then_inc(on_done, 1)

            def add(a):
                a.wait(yb_done, all_(a.n))
                nc.vector.tensor_tensor(x_sb[:, a.span(C)], x_sb[:, a.span(C)], bank_f[:, 0:C], ALU.add).then_inc(xadd_done, 1)

            def hidden_gate(a):
                if a.k.attn or a.k.act != ACT.Silu:
                    return
                u = a.u
                a.wait(act_done, mlp_(a.n))
                for c in range(CH):
                    last = nc.vector.scalar_tensor_tensor(
                        out=hid[u][:, c * L:(c + 1) * L], in0=bank_a[u][:, c * L:(c + 1) * L], scalar=bcol(a.k, "b1", CH + c),
                        in1=act[u][:, c * L:(c + 1) * L], op0=ALU.add, op1=ALU.mult)
                last.then_inc(hid_done, 1)

            def attention_biases():
                ve.wait_ge(bp_mm, 1)
                for i, n in enumerate(BIASED):
                    nc.vector.tensor_tensor(bprime[:, n:n + 1], bank_f[:, i:i + 1], bcol(BLOCKS[n], "o"), ALU.add)
                for n, k in enumerate(BLOCKS):
                    if not k.attn:
                        last = nc.vector.tensor_copy(bprime[:, n:n + 1], bcol(k, "b2"))
                last.then_inc(bp_made, 1)
                ve.wait_ge(bp_made, 1)
                for n, k in enumerate(BLOCKS):
                    if k.gate is not None:
                        gate = mods[:, (2 * NMOD + k.gate) * B:(2 * NMOD + k.gate + 1) * B]
                        last = nc.vector.tensor_scalar(gbias[:, k.gate * B:(k.gate + 1) * B], gate, bprime[:, n:n + 1], None, ALU.mult)
                last.then_inc(gb_made, 1)

            def step(done, now, nxt, aft, far):
                if now is not None and now.first and now.n == 0:
                    attention_biases()
                if far is not None:
                    stats(far)
                if done is not None:
                    divide(done)
                if aft is not None:
                    rotate(aft)
                    split_qk(aft)
                if far is not None:
                    normalise(far)
                if nxt is not None:
                    spread(nxt)
                    for g in range(G):
                        row_stage(nxt, g)
                        if g == (0 if nxt.k.kind == "topk" else 1) and done is not None:
                            add(done)
                    if nxt.k.kind == "soft":
                        split(nxt)
                    hidden_gate(nxt)
                elif done is not None:
                    add(done)

            pipeline(ve, step)

        @block.tensor
        def _(pe):
            pe.wait_ge(wmod_in, 16)
            pe.wait_ge(silu_c, 1)
            for v in range(NVEC):
                m = v % NMOD if v < 2 * NMOD else v - 2 * NMOD
                src = cond_sb if MODS[m].startswith("L3") else scond_sb
                last = nc.tensor.matmul(bank_p[:, v * B:(v + 1) * B], wmod_sb[:, v * C:(v + 1) * C], src[:], start=True, stop=True)
            last.then_inc(mods_mm, 1)
            for i in range(4):
                if i % 2 == 0:
                    pe.wait_ge(c_norm, i // 2 + 1)
                bank = (bank_b[0], bank_b[1], bank_o, bank_f)[i]
                for r in range(4):
                    at = (4 * i + r) * C
                    last = nc.tensor.transpose(bank[:, r * LC:(r + 1) * LC], cnorm[:, at:at + C], c_sb[0:LC, 0:LC])
                last.then_inc(c_tr, 1)
            pe.wait_ge(w_in[0], 16)
            pe.wait_ge(mods_made, 1)
            pe.wait_ge(consts_made, 1)

            def rest_of_setup():
                for s in w_in[1:]:
                    pe.wait_ge(s, 16)
                pe.wait_ge(c_out, 10)
                for i, n in enumerate(BIASED):
                    last = nc.tensor.matmul(bank_f[:, i:i + 1], w(BLOCKS[n], "o"), bcol(BLOCKS[n], "v"), start=True, stop=True)
                last.then_inc(bp_mm, 1)
                pe.wait_ge(bp_made, 1)

            def transpose_x(a):
                a.wait(xn_done, all_(a.n))
                a.wait(ht_done, all_(a.n), 1)
                if a.first:
                    if a.n and BLOCKS[a.n - 1].attn:
                        pe.wait_ge(qk_done, attn_(a.n))
                elif a.k.attn:
                    a.wait(qk_done, attn_(a.n), 1)
                nc.tensor.transpose(bank_p[:, 0:L], xn[a.u][:], ident).then_inc(xnt_done, 1)

            def project_qk(a):
                if not a.k.attn:
                    return
                u, k, n = a.u, a.k, a.k.keys
                a.wait(ht_done, all_(a.n))
                if k.ctx is not None:
                    a.wait(ctx_copied, cross_(a.n))
                src = cslot[u][:, 0:n] if k.ctx is not None else ht[u][:]
                last = nc.tensor.matmul(bank_p[:, 0:L], w(k, "q"), ht[u][:], start=True, stop=True)
                last = nc.tensor.matmul(bank_p[:, L:L + n], w(k, "k"), src, start=True, stop=True)
                if k.rope:
                    nc.tensor.matmul(bank_p[:, 256:256 + L], w(k, "qr"), ht[u][:], start=True, stop=True)
                    last = nc.tensor.matmul(bank_p[:, 384:384 + n], w(k, "kr"), src, start=True, stop=True)
                last.then_inc(qkp_done, 1)

            def project_v(a):
                if not a.k.attn:
                    return
                u, k, n = a.u, a.k, a.k.keys
                src = cslot[u][:, 0:n] if k.ctx is not None else ht[u][:]
                a.wait(v_done, attn_(a.n), 1)
                if a.first:
                    if a.n:
                        pe.wait_ge(mt_done, soft_(a.n))
                elif k.kind == "soft":
                    a.wait(mt_done, soft_(a.n), 1)
                nc.tensor.matmul(bank_m[0:n, 128:256], src, w(k, "v"), start=True, stop=True).then_inc(proj_done, 1)

            def scores_by_row(a, g):
                u, k = a.u, a.k
                nw = k.windows
                n = L // nw if k.ctx is None else LC
                if g == 0:
                    a.wait(qbd_done, attn_(a.n))
                    a.wait_dma(k_in, attn_(a.n), len(K_SLOTS))
                if a.first and g == 0 and a.n and BLOCKS[a.n - 1].act == ACT.Silu:
                    pe.wait_ge(hid_done, mlp_(a.n))
                a.wait(a_free[g - 2], attn_(a.n), 0 if g >= 2 else 1)
                for wd in range(nw):
                    rows = slice(64 * wd, 64 * wd + 64) if nw == 2 else slice(0, L)
                    for j in range(J):
                        s, hj = g * 2 + j // 2, j % 2
                        last = nc.tensor.matmul(
                            bank_a[g % 2][rows, j * n:(j + 1) * n], qbd[u][:, (hj * S + s) * L + rows.start:(hj * S + s) * L + rows.stop],
                            kst[u][:, s * L + wd * n:s * L + wd * n + n], start=True, stop=True)
                last.then_inc(a_done[g], 1)

            def maxima_in(a):
                if a.k.kind != "soft":
                    return
                a.wait(mparts_done, soft_(a.n), carry=(consts_made, 1))
                a.wait(v_done, attn_(a.n), carry=(consts_made, 1))
                nc.tensor.transpose(bank_m[0:3 * H, 0:L // 2].bitcast(BF16), mparts[:], identb[:]).then_inc(mpt_done, 1)

            def scores_by_key(a, g):
                u, k = a.u, a.k
                bank = bank_b[g % 2]
                if a.first and g < 2 and a.n and not BLOCKS[a.n - 1].attn:
                    pe.wait_ge(act_done, mlp_(a.n))
                a.wait(pt_done[g - 2], attn_(a.n), 0 if g >= 2 else 1)
                if k.kind == "topk":
                    a.wait(p_done[g], topk_(a.n))
                    for j in range(J):
                        h = g * J + j
                        last = nc.tensor.transpose(bank[0:LC, j * L:(j + 1) * L], pn[:, h * LC:(h + 1) * LC], ident)
                    last.then_inc(b_done[g], 1)
                    return
                nw = k.windows
                n, q = (L // nw if k.ctx is None else LC), L // nw
                for wd in range(nw):
                    for s in (2 * g, 2 * g + 1):
                        queries = qbd[u][:].rearrange("p (j s t) -> p j s t", j=2, s=S)[:, :, s, wd * q:(wd + 1) * q]
                        at = s % 2 * 2 * q
                        nc.tensor.matmul(bank[n * wd:n * wd + n, at:at + 2 * q], kst[u][:, s * L + n * wd:s * L + n * wd + n], queries,
                                         start=s == 2 * g, stop=False, skip_group_check=True)

            def less_maxima(a, g):
                k = a.k
                if k.kind == "topk":
                    return
                nw = k.windows
                n, q = (L // nw if k.ctx is None else LC), L // nw
                if g == 0:
                    a.wait(mt_done, soft_(a.n), carry=(consts_made, 1))
                for wd in range(nw):
                    for j in range(J):
                        h = g * J + j
                        last = nc.tensor.matmul(bank_b[g % 2][n * wd:n * wd + n, j * q:(j + 1) * q], sel[:, h * 128:h * 128 + n],
                                                mt[:, wd * q:(wd + 1) * q], start=False, stop=True, skip_group_check=True)
                last.then_inc(b_done[g], 1)

            def weigh(a, g):
                u, k = a.u, a.k
                n = k.keys
                q = L // k.windows
                a.wait(pt_done[g], attn_(a.n))
                if g == 0:
                    a.wait(v_done, attn_(a.n))
                    a.wait(o_free, all_(a.n), 1)
                out_rows = slice(64 * (g % 2), 64 * (g % 2) + 64)
                for wd in range(k.windows):
                    at = g // 2 * L + wd * q
                    v = vwin[wd][u] if k.windows == 2 else vpad[u]
                    for j in range(J):
                        h = g * J + j
                        last = nc.tensor.matmul(bank_o[out_rows, at:at + q], v[0:n, h * 64:(h + 1) * 64], pt[g % 2][0:n, j * q:(j + 1) * q],
                                                start=(j == 0), stop=(j == J - 1), skip_group_check=True)
                last.then_inc(pv_done[g] if g < G - 1 else o_done, 1)

            def sums_back(a):
                if not a.k.attn:
                    return
                a.wait(o_free, all_(a.n))
                a.wait(xadd_done, xadd_(a.n), 1)
                for i in range(2):
                    last = nc.tensor.transpose(bank_f[:, i * L:(i + 1) * L], ot[:, i * L:(i + 1) * L], ident)
                last.then_inc(otn_done, 1)

            def heads_back(a):
                if not a.k.attn:
                    return
                a.wait(on_done, attn_(a.n))
                nc.tensor.transpose(bank_f[:, 0:L], on[:], ident).then_inc(ont_done, 1)

            def project_out(a):
                if not a.k.attn:
                    return
                a.wait(ontc_done, attn_(a.n))
                nc.tensor.matmul(bank_f[:, 0:L], w(a.k, "o"), ont[:], start=True, stop=True).then_inc(y_done, 1)

            def branch_back(a):
                if a.k.attn:
                    a.wait(yt_done, attn_(a.n))
                else:
                    a.wait(o_free, all_(a.n))
                    a.wait(xadd_done, xadd_(a.n), 1)
                nc.tensor.transpose(bank_f[:, 0:C], yt[:], ident).then_inc(yb_done, 1)

            def hidden(a):
                if a.k.attn:
                    return
                u, k = a.u, a.k
                a.wait(ht_done, all_(a.n))
                a.wait(act_done, mlp_(a.n), 2)
                if k.act == ACT.Silu:
                    a.wait(hid_done, mlp_(a.n), 2)
                if a.i is None and a.c < 2 and BLOCKS[a.n - 1].attn:
                    pe.wait_ge(pt_done[2 + u], attn_(a.n))
                    pe.wait_ge(a_free[2 + u], attn_(a.n))
                if k.act == ACT.Silu:
                    for c in range(CH):
                        nc.tensor.matmul(bank_a[u][:, c * L:(c + 1) * L], w(k, "w1", C, HID + c * C), ht[u][:], start=True, stop=True)
                for c in range(CH):
                    last = nc.tensor.matmul(bank_b[u][:, c * L:(c + 1) * L], w(k, "w1", C, c * C), ht[u][:], start=True, stop=True)
                last.then_inc(proj_done, 1)

            def down(a):
                u, k = a.u, a.k
                if k.act == ACT.Silu:
                    a.wait(hid_done, mlp_(a.n))
                else:
                    a.wait(act_done, mlp_(a.n))
                src = hid[u] if k.act == ACT.Silu else act[u]
                a.wait(o_free, all_(a.n), 1)
                for c in range(CH):
                    last = nc.tensor.matmul(bank_o[:, 0:L], w(k, "w2", C, c * C), src[:, c * L:(c + 1) * L], start=(c == 0), stop=(c == CH - 1))
                last.then_inc(o_done, 1)

            def step(done, now, nxt, aft, far):
                attn = now is not None and now.k.attn
                rows = nxt is not None and nxt.k.attn
                if aft is not None:
                    transpose_x(aft)
                if now is not None and now.first and now.n == 0:
                    rest_of_setup()
                if attn:
                    scores_by_key(now, 0)
                if done is not None:
                    sums_back(done)
                if attn:
                    scores_by_key(now, 1)
                if aft is not None:
                    project_qk(aft)
                if attn:
                    maxima_in(now)
                    less_maxima(now, 0)
                if nxt is not None:
                    project_v(nxt)
                if attn:
                    less_maxima(now, 1)
                    weigh(now, 0)
                elif now is not None:
                    down(now)
                if done is not None:
                    heads_back(done)
                if attn:
                    scores_by_key(now, 2)
                    less_maxima(now, 2)
                if rows:
                    scores_by_row(nxt, 0)
                if attn:
                    weigh(now, 1)
                if done is not None:
                    project_out(done)
                if rows:
                    scores_by_row(nxt, 1)
                if attn:
                    scores_by_key(now, 3)
                    less_maxima(now, 3)
                early = rows and nxt.k.kind == "soft"
                if early:
                    scores_by_row(nxt, 2)
                if done is not None:
                    branch_back(done)
                if attn:
                    weigh(now, 2)
                if early:
                    scores_by_row(nxt, 3)
                if attn:
                    weigh(now, 3)
                if rows:
                    if not early:
                        scores_by_row(nxt, 2)
                        scores_by_row(nxt, 3)
                elif nxt is not None:
                    hidden(nxt)

            pipeline(pe, step)


FEATURES = np.array([D * (2 * s + r // D) + r % D for r in range(R) for s in range(S)])


def shape_constants():
    c = np.zeros((128, CTOT), np.float32)
    p = np.arange(128)
    c[:, 0:128] = np.eye(128)
    c[p, CCOL["headmask"] + p % R // D] = 1.0
    r = np.arange(3 * H)
    c[r, CCOL["sel"] + r % H] = 1.0
    half = D // 2
    inv = (1.0 / np.float32(10000.0) ** (np.arange(half, dtype=np.float32) / np.float32(half))).astype(np.float32)
    feature = FEATURES % D
    sign = np.where(feature < half, -1.0, 1.0).astype(np.float32)[:, None]
    for cs, sn, pos in (("cos", "sin", (np.arange(L) + SHIFT) % L), ("cosc", "sinc", np.arange(LC))):
        ang = pos.astype(np.float32)[None, :] * inv[feature % half][:, None]
        c[:, CCOL[cs]:CCOL[cs] + len(pos)] = np.cos(ang)
        c[:, CCOL[sn]:CCOL[sn] + len(pos)] = np.sin(ang) * sign
    return c


def kernel(**inputs):
    import concourse.bacc as bacc
    from concourse.bass_utils import run_bass_kernel_spmd

    a = {k: np.asarray(v) for k, v in inputs.items()}

    def l0(s): return a["L0_xcond_" + s]
    def l1(s): return a["L1_xcond_" + s]
    def l2(s): return a["L2_xcond_" + s]
    def l3(s): return a["L3_xcond_" + s]

    def cut(m, i): return m[..., i * C:(i + 1) * C]

    ada, mod, l2q, l2k = (l0("w_ada"), l0("b_ada")), (l1("W_mod"), l1("b_mod")), (l2("Wss_q"), l2("bss_q")), (l2("Wss_kv"), l2("bss_kv"))
    l3n = [(l3(f"ln{i}_w").T, l3(f"ln{i}_b")) for i in (1, 2, 3)]
    scales = [(ada, 1), (ada, 4), (ada, 7), (mod, 1), (mod, 4), (l2q, 0), (l2k, 0)] + [(m, 0) for m in l3n]
    shifts = [(ada, 0), (ada, 3), (ada, 6), (mod, 0), (mod, 3), (l2q, 1), (l2k, 1)] + [(m, 1) for m in l3n]
    gates = [(ada, 2), (ada, 5), (ada, 8), (mod, 2), (mod, 5)]
    wmod = np.concatenate([cut(m[0], i) for m, i in scales + shifts + gates], axis=1)
    bmod = np.stack([cut(m[1], i) for m, i in scales + shifts + gates], axis=1)

    swap = (np.arange(C) // D) * D + (np.arange(C) + D // 2) % D

    def down(m): return m.reshape(CH, C, C).transpose(1, 0, 2).reshape(C, HID)

    def cols(v): return list(v.reshape(-1, C))

    def biases(v, n):
        return [u[FEATURES] if i < n else u for i, u in enumerate(cols(v))]

    def spread(m, n, extra=slice(None)):
        return np.concatenate([cut(m, i)[:, extra][:, FEATURES] if i < n else cut(m, i) for i in range(m.shape[1] // C)], axis=1)

    qkv3 = l3("qkv_w").T
    w = {
        "sa0": [spread(l0("w_qkv"), 2), l0("w_so")],
        "xa0": [spread(l0("w_q"), 1), spread(l0("w_kv"), 1), l0("w_co")],
        "ml0": [l0("w_m1"), down(l0("w_m2"))],
        "sa1": [spread(l1("W_qkv"), 2), l1("W_proj")],
        "xa1": [spread(l1("W_qc"), 1), spread(l1("W_kvc"), 1), l1("W_cproj")],
        "ml1": [l1("W_mlp1"), down(l1("W_mlp2"))],
        "xa2": [spread(l2("Wq"), 1), spread(l2("Wkv"), 1), l2("Wp")],
        "sa3": [spread(qkv3[:, 0:2 * C], 2), spread(qkv3[:, 0:2 * C], 2, swap), cut(qkv3, 2), l3("sa_out_w").T],
        "xa3": [spread(l3("q_w").T, 1), spread(l3("k_w").T, 1), spread(l3("q_w").T, 1, swap), spread(l3("k_w").T, 1, swap),
                l3("v_w").T, l3("ca_out_w").T],
        "ml3": [l3("ffn_w1").T, down(l3("ffn_w2").T)],
    }
    bs = {
        "sa0": biases(l0("b_qkv"), 2) + cols(l0("b_so")), "xa0": biases(l0("b_q"), 1) + biases(l0("b_kv"), 1) + cols(l0("b_co")),
        "ml0": cols(l0("b_m1")) + cols(l0("b_m2")), "sa1": biases(l1("b_qkv"), 2) + cols(l1("b_proj")),
        "xa1": biases(l1("b_qc"), 1) + biases(l1("b_kvc"), 1) + cols(l1("b_cproj")), "ml1": cols(l1("b_mlp1")) + cols(l1("b_mlp2")),
        "xa2": biases(l2("bq"), 1) + biases(l2("bkv"), 1) + cols(l2("bp")), "sa3": [], "xa3": [],
        "ml3": cols(l3("ffn_b1")) + cols(l3("ffn_b2")),
    }
    ctx = a["ctx_1024"]
    arrays = {
        "x": a["x"], "cond_t": a["cond_1024"].T, "ctx_n": ctx, "ctx_t": ctx.transpose(2, 0, 1).reshape(C, B * LC),
        "wmod": wmod, "bmod": bmod, "wts": np.concatenate([m for k in BLOCKS for m in w[k.name]], axis=1),
        "bias": np.stack([v for k in BLOCKS for v in bs[k.name]], axis=1), "consts": shape_constants(),
    }
    arrays = {f"in_{k}": np.ascontiguousarray(v) for k, v in arrays.items()}
    nc = bacc.Bacc("TRN2", target_bir_lowering=False, num_devices=1)
    args = [nc.dram_tensor(k, v.shape, mybir.dt.from_np(v.dtype), kind="ExternalInput").ap() for k, v in arrays.items()]
    args.append(nc.dram_tensor("out_0", (B, L, C), F32, kind="ExternalOutput").ap())
    args.append(nc.dram_tensor("scratch", (2, PARTS, 2, C, L), BF16, kind="Internal").ap())
    build(nc, *args)
    r = run_bass_kernel_spmd(nc, [arrays], core_ids=[0])
    return r.results[0]["out_0"]
```

```python
from contextlib import ExitStack

import numpy as np

import concourse.bass as bass
from concourse import mybir

F32 = mybir.dt.float32
BF16 = mybir.dt.bfloat16
ALU = mybir.AluOpType
ACT = mybir.ActivationFunctionType
AX = mybir.AxisListType.X

B, L, C, LC = 8, 128, 128, 120
H = 16
D = C // H
G = 4
J = H // G
SHIFT = 32
HID = 512
CH = HID // C
SCALE = float(D) ** -0.5
S = H // 2
R = 2 * D
PARTS = 3
Q_SLOTS = [(0, 3, 2), (0, 2, 1)]
K_SLOTS = [(0, 1, 3), (1, 1, 3), (2, 1, 2)]
TAKEN = -3.0e38

MODS = ["L0a", "L0c", "L0m", "L1a", "L1m", "L2q", "L2kv", "L31", "L32", "L33"]
GATED = 5
NMOD = len(MODS)
NVEC = 2 * NMOD + GATED
FIRST = [0, NMOD, 2 * NMOD]
VECS = FIRST + [v for v in range(NVEC) if v not in FIRST]


class Blk:
    def __init__(self, kind, name, mod=None, eps=1e-6, windows=1, ctx=None, rope=False, bias=True, gate=None, act=None):
        self.kind, self.name, self.mod, self.eps, self.windows = kind, name, mod, eps, windows
        self.ctx, self.rope, self.bias, self.gate, self.act = ctx, rope, bias, gate, act
        self.attn = kind != "mlp"
        self.keys = LC if ctx is not None else L


BLOCKS = [
    Blk("soft", "sa0", mod=0, windows=2, gate=0),
    Blk("topk", "xa0", mod=1, ctx=0, gate=1),
    Blk("mlp", "ml0", mod=2, gate=2, act=ACT.Silu),
    Blk("soft", "sa1", mod=3, gate=3),
    Blk("soft", "xa1", ctx=1),
    Blk("mlp", "ml1", mod=4, gate=4, act=ACT.Gelu_apprx_tanh),
    Blk("soft", "xa2", mod=5, eps=1e-5, ctx=2),
    Blk("soft", "sa3", mod=7, eps=1e-5, rope=True, bias=False),
    Blk("soft", "xa3", mod=8, eps=1e-5, ctx=0, rope=True, bias=False),
    Blk("mlp", "ml3", mod=9, eps=1e-5, act=ACT.Gelu),
]
NBLK = len(BLOCKS)
FIRST_MLP = [k.attn for k in BLOCKS].index(False)
BIASED = [n for n, k in enumerate(BLOCKS) if k.bias and k.attn]

WCOL = {}
_at = 0
for _k in BLOCKS:
    for _w, _n in ((("q", C), ("k", C), ("qr", C * _k.rope), ("kr", C * _k.rope), ("v", C), ("o", C)) if _k.attn
                   else (("w1", HID * (2 if _k.act == ACT.Silu else 1)), ("w2", HID))):
        if _n:
            WCOL[_k.name, _w] = _at
            _at += _n
WTOT = _at
WSPLIT = [WCOL["xa0", "q"], WCOL["ml0", "w1"], WCOL["sa1", "q"], WCOL["xa2", "q"], WTOT]

BCOL = {}
_at = 0
for _k in BLOCKS:
    for _w, _n in ((("q", 1), ("k", 1), ("v", 1), ("o", 1)) if _k.attn
                   else (("b1", CH * (2 if _k.act == ACT.Silu else 1)), ("b2", 1))):
        if _k.bias:
            BCOL[_k.name, _w] = _at
            _at += _n
BTOT = _at

CCOL = {"ident": 0, "headmask": 128, "sel": 130, "cos": 146, "sin": 274, "cosc": 402, "sinc": 522}
CTOT = 642


def build(nc, x, cond_t, ctx_n, ctx_t, wmod, bmod, wts, bias, consts, out, scratch):
    with ExitStack() as ctx:
        def sb(name, shape, dt=F32):
            return ctx.enter_context(nc.sbuf_tensor(name, shape, dt))

        def sem(name):
            return ctx.enter_context(nc.semaphore(name))

        def sems(name, n=G):
            return [sem(f"{name}{i}") for i in range(n)]

        bank_a = [ctx.enter_context(nc.psum_tensor(f"bank_a{i}", [128, 512], F32)) for i in range(2)]
        bank_b = [ctx.enter_context(nc.psum_tensor(f"bank_b{i}", [128, 512], F32)) for i in range(2)]
        bank_o = ctx.enter_context(nc.psum_tensor("bank_o", [128, 512], F32))
        bank_p = ctx.enter_context(nc.psum_tensor("bank_p", [128, 512], F32))
        bank_f = ctx.enter_context(nc.psum_tensor("bank_f", [128, 512], F32))
        bank_m = ctx.enter_context(nc.psum_tensor("bank_m", [128, 512], F32))

        x_sb = sb("x_sb", [128, B * C])
        w_sb = sb("w_sb", [128, WTOT])
        b_sb = sb("b_sb", [128, BTOT])
        c_sb = sb("c_sb", [128, CTOT])
        wmod_sb = sb("wmod_sb", [128, NVEC * C])
        bmod_sb = sb("bmod_sb", [128, NVEC])
        cond_sb = sb("cond_sb", [128, B])
        scond_sb = sb("scond_sb", [128, B])
        mods = sb("mods", [128, NVEC * B])
        bprime = sb("bprime", [128, NBLK])
        gbias = sb("gbias", [128, GATED * B])
        ctxn_sb = sb("ctxn_sb", [LC, B * C])
        ctx_sb = [sb(f"ctx_sb{i}", [128, B * LC]) for i in range(3)]
        cstat = sb("cstat", [LC, B * 6])
        cmv = sb("cmv", [LC, B * 2])
        ceps = sb("ceps", [LC, 2 * B])
        crstd = sb("crstd", [LC, 2 * B])
        cnorm = sb("cnorm", [LC, 2 * B * C])
        half_neg = sb("half_neg", [128, 2 * B])
        ident = c_sb[:, 0:128]
        identb = sb("identb", [128, 128], BF16)
        selcol = c_sb[:, CCOL["sel"]:CCOL["sel"] + H]
        sel = sb("sel", [128, H * 128], BF16)
        headmask = [c_sb[:, CCOL["headmask"] + j:CCOL["headmask"] + j + 1] for j in range(2)]

        stat = sb("stat", [128, 2 * 6])
        mv = sb("mv", [128, 2 * 2])
        vareps = sb("vareps", [128, 2])
        rstd = sb("rstd", [128, 2])
        xn = [sb(f"xn{i}", [128, C]) for i in range(2)]
        ht = [sb(f"ht{i}", [128, L]) for i in range(2)]
        cslot = [sb(f"cslot{i}", [128, LC]) for i in range(2)]
        qk = [sb(f"qk{i}", [128, 2 * L]) for i in range(2)]
        ropec = sb("ropec", [128, 2 * L])
        ropes = sb("ropes", [128, 2 * L])
        parts = [sb(f"parts{i}", [128, PARTS * 2 * L], BF16) for i in range(2)]
        pres = [sb(f"pres{i}", [128, 2 * L]) for i in range(2)]
        qst = [sb(f"qst{i}", [128, S * L], BF16) for i in range(2)]
        kst = [sb(f"kst{i}", [128, S * L], BF16) for i in range(2)]
        qbd = [sb(f"qbd{i}", [128, 2 * S * L], BF16) for i in range(2)]
        vpad = [sb(f"vpad{i}", [128, H * 64]) for i in range(2)]
        vwin = [[sb(f"vwin{w}_{i}", [128, H * 64]) for i in range(2)] for w in range(2)]
        nmax = sb("nmax", [128, H])
        mres = sb("mres", [128, H])
        mparts = sb("mparts", [128, 3 * H], BF16)
        mt = sb("mt", [128, L], BF16)
        pt = [sb(f"pt{i}", [128, 512]) for i in range(2)]
        ot = sb("ot", [128, 2 * L])
        rec = sb("rec", [128, H])
        on = sb("on", [128, C])
        ont = sb("ont", [128, L])
        yt = sb("yt", [128, L])
        top = sb("top", [128, H * 16])
        nbias = sb("nbias", [128, H])
        s3 = sb("s3", [128, H * LC])
        ex = sb("ex", [128, H * LC])
        pn = sb("pn", [128, H * LC])
        act = [sb(f"act{i}", [128, HID]) for i in range(2)]
        hid = [sb(f"hid{i}", [128, HID]) for i in range(2)]

        x_in, w_in, small_in, wmod_in, ctx_in = sem("x_in"), sems("w_in", 5), sem("small_in"), sems("wmod_in", 2), sem("ctx_in")
        silu_c, consts_made, pads_zero, pads_made = sem("silu_c"), sem("consts_made"), sem("pads_zero"), sem("pads_made")
        mods_mm, mods_add, mods_made, bp_mm, bp_made = (
            sem("mods_mm"), sem("mods_add"), sem("mods_made"), sem("bp_mm"), sem("bp_made"))
        gb_made = sem("gb_made")
        c_stat, c_aggr, c_eps, c_rstd, c_norm, c_tr, c_out = (
            sem("c_stat"), sem("c_aggr"), sem("c_eps"), sem("c_rstd"), sem("c_norm"), sem("c_tr"), sem("c_out"))
        st_done, aggr_done, eps_done, rstd_done, xn_done = (
            sem("st_done"), sem("aggr_done"), sem("eps_done"), sem("rstd_done"), sem("xn_done"))
        xnt_done, ht_done, qkp_done, proj_done = sem("xnt_done"), sem("ht_done"), sem("qkp_done"), sem("proj_done")
        ph_done, pr_done, pm_done, parts_done = sem("ph_done"), sem("pr_done"), sem("pm_done"), sem("parts_done")
        parts_out, q_in, k_in = sems("parts_out", 2), sems("q_in", 2), sems("k_in", 2)
        ctx_copied, ropec_done, ropes_done = sem("ctx_copied"), sem("ropec_done"), sem("ropes_done")
        qk_done, v_done, qbd_done = sem("qk_done"), sem("v_done"), sem("qbd_done")
        a_done, a_free = sems("a_done"), sems("a_free")
        m1_done, r1_done, m2_done, mparts_done = sem("m1_done"), sem("r1_done"), sem("m2_done"), sem("mparts_done")
        mpt_done, mt_done = sem("mpt_done"), sem("mt_done")
        t8_done, tmr_done, t16_done, s3_done, mask_done, p_done = (
            sems("t8_done"), sems("tmr_done"), sems("t16_done"), sems("s3_done"), sems("mask_done"), sems("p_done"))
        b_done, pt_done, pv_done = sems("b_done"), sems("pt_done"), sems("pv_done", G - 1)
        o_done, o_free = sem("o_done"), sem("o_free")
        otn_done, rec_done, on_done, ont_done, ontc_done = (
            sem("otn_done"), sem("rec_done"), sem("on_done"), sem("ont_done"), sem("ontc_done"))
        y_done, yt_done, yb_done, xadd_done = sem("y_done"), sem("yt_done"), sem("yb_done"), sem("xadd_done")
        act_done, hid_done = sem("act_done"), sem("hid_done")
        stored = sem("stored")

        def before(n, *kinds):
            return B * sum(k.kind in kinds for k in BLOCKS[:n])

        def all_(n):
            return B * n

        def xadd_(n):
            return all_(n) + 1

        def attn_(n):
            return before(n, "soft", "topk")

        def soft_(n):
            return before(n, "soft")

        def topk_(n):
            return before(n, "topk")

        def mlp_(n):
            return before(n, "mlp")

        def cross_(n):
            return B * sum(k.ctx is not None for k in BLOCKS[:n])

        def rope_(n):
            return B * sum(k.rope for k in BLOCKS[:n])

        class At:

            def __init__(self, eng, n, c, i=None, held=None):
                self.eng, self.n, self.c, self.i, self.held = eng, n, c, i, held
                self.k, self.u = BLOCKS[n], c % 2

            def value(self, scale, add):
                if self.i is None:
                    return scale * self.c + add
                key = (scale, scale * self.c + add)
                if key not in self.held:
                    self.held[key] = self.eng.snap(self.i * (2 * scale) + key[1])
                    self.eng.compute_val(self.held[key])
                return self.held[key]

            def span(self, width, at=0):
                return bass.ds(self.value(width, at), width)

            def one(self, at):
                return bass.ds(self.value(1, at), 1)

            def wait(self, semaphore, base, back=0, carry=None):
                count = self.count(base, back)
                if carry and self.i is not None:
                    self.eng.wait_ge(*carry)
                self.wait_count(semaphore, count)

            def count(self, base, back=0):
                return self.value(1, base + 1 - back)

            def wait_count(self, semaphore, count):
                if self.i is not None or count > 0:
                    self.eng.wait_ge(semaphore, count)

            def wait_dma(self, semaphores, base, dmas, back=0):
                self.wait_count(semaphores[self.u], self.count_dma(base, dmas, back))

            def count_dma(self, base, dmas, back=0):
                unit = 16 * dmas
                return self.value(unit // 2, unit * (base // 2 + 1 - back // 2) - unit // 2 * self.u)

            @property
            def first(self):
                return self.i is None and self.c == 0

        def pipeline(eng, step, extra=None):
            def fixed(n, c):
                n, c = n + c // B, c % B
                return At(eng, n, c) if 0 <= n < NBLK else None

            near = (-1, 0, 1, 2, 3)

            def one(n, c):
                step(*(fixed(n, c + d) for d in near))
                if extra:
                    extra(n, c)

            for c in (-3, -2, -1):
                one(0, c)
            for n in range(NBLK):
                one(n, 0)
                with eng.Fori(0, 2) as i:
                    for c in (1, 2):
                        held = {}
                        step(*(At(eng, n, c + d, i, held) for d in near))
                for c in (5, 6, 7):
                    one(n, c)
            step(fixed(NBLK, -1), None, None, None, None)

        def w(k, what, n=C, at=0):
            c = WCOL[k.name, what] + at
            return w_sb[:, c:c + n]

        def bcol(k, what, at=0):
            c = BCOL[k.name, what] + at
            return b_sb[:, c:c + 1]

        def heads4(ap, n):
            return ap.rearrange("p (j n) -> p j n", n=n)

        def part(t, i):
            return t[:].rearrange("f (q p t) -> f q p t", q=2, p=PARTS)[:, :, i, :]

        def both(t):
            return t[:].rearrange("f (q t) -> f q t", q=2)

        block = ctx.enter_context(nc.Block())

        @block.sync
        def _(sp):
            sp.dma_start(cond_sb[:], cond_t).then_inc(small_in, 16)
            sp.dma_start(bmod_sb[:], bmod).then_inc(small_in, 16)
            sp.dma_start(b_sb[:], bias).then_inc(small_in, 16)
            sp.dma_start(c_sb[:], consts).then_inc(small_in, 16)
            cut = len(FIRST) * C
            sp.dma_start(wmod_sb[:, 0:cut], wmod[:, 0:cut]).then_inc(wmod_in[0], 16)
            sp.dma_start(wmod_sb[:, cut:], wmod[:, cut:]).then_inc(wmod_in[1], 16)
            sp.dma_start(ctx_sb[0][:], ctx_t).then_inc(ctx_in, 16)
            sp.dma_start(ctxn_sb[:].rearrange("p (b c) -> p b c", b=B), ctx_n.rearrange("b s c -> s b c")).then_inc(ctx_in, 16)
            lo = 0
            for s, hi in zip(w_in[1:], WSPLIT[1:]):
                lo = WSPLIT[w_in.index(s) - 1]
                sp.dma_start(w_sb[:, lo:hi], wts[:, lo:hi]).then_inc(s, 16)
            part_of = [scratch[u].rearrange("q p f t -> f (q p) t") for u in range(2)]

            def parts_to_slots(a):
                if not a.k.attn:
                    return
                u, base = a.u, attn_(a.n)
                made, used = a.count(base), a.count(base, 2)
                out = a.count_dma(base, 1)
                q_read, k_read = a.count_dma(base, len(Q_SLOTS), 2), a.count_dma(base, len(K_SLOTS), 2)
                a.wait_count(parts_done, made)
                a.wait_count(q_in[u], q_read)
                a.wait_count(k_in[u], k_read)
                sp.dma_start(part_of[u], parts[u][:].rearrange("f (qp t) -> f qp t", t=L)).then_inc(parts_out[u], 16)
                a.wait_count(parts_out[u], out)
                for i, (tensor, slots, sem_in) in enumerate(((qst[u], Q_SLOTS, q_in[u]), (kst[u], K_SLOTS, k_in[u]))):
                    a.wait_count((qbd_done, b_done[G - 1])[i], used)
                    at = 0
                    for first, n, times in slots:
                        src = scratch[u][i, first:first + n].rearrange("p (r s) t -> (p r) (s t)", s=S)
                        if times > 1:
                            src = src[None].broadcast_to([times, n * R, S * L])
                        sp.dma_start(tensor[at:at + n * times * R, :], src).then_inc(sem_in, 16)
                        at += n * times * R

            pipeline(sp, lambda done, now, nxt, aft, far: parts_to_slots(aft) if aft is not None else None)
            for b in range(B):
                sp.wait_ge(xadd_done, xadd_(NBLK - 1) + b + 1)
                sp.dma_start(out[b, SHIFT:L, :], x_sb[0:L - SHIFT, b * C:(b + 1) * C]).then_inc(stored, 16)
                sp.dma_start(out[b, 0:SHIFT, :], x_sb[L - SHIFT:L, b * C:(b + 1) * C]).then_inc(stored, 16)
            sp.wait_ge(stored, 2 * 16 * B)

        @block.gpsimd
        def _(pool):
            for t in vpad + vwin[0] + vwin[1]:
                nc.gpsimd.memset(t[:], 0.0)
            nc.gpsimd.memset(mt[:], 0.0)
            for t in qk:
                nc.gpsimd.memset(t[:], 0.0)
            nc.gpsimd.memset(half_neg[:], -0.5).then_inc(pads_zero, 1)
            pool.wait_ge(pads_zero, 1)
            for j in range(J):
                for t in vpad:
                    last = nc.gpsimd.memset(t[:].rearrange("p (g r) -> p g r", g=G)[:, :, 64 * j + 32 + j:64 * j + 33 + j], 1.0)
            last.then_inc(pads_zero, 1)
            pool.wait_ge(pads_zero, 2)
            for wd in range(2):
                for j in range(J):
                    for t in vwin[wd]:
                        last = nc.gpsimd.memset(
                            t[64 * wd:64 * wd + 64, :].rearrange("p (g r) -> p g r", g=G)[:, :, 64 * j + 32 + j:64 * j + 33 + j], 1.0)
            last.then_inc(pads_made, 1)
            pool.wait_ge(pads_made, 1)
            def context(quarter):
                if quarter == 0:
                    pool.wait_ge(c_aggr, 1)
                    var = cmv[:].rearrange("p (b t) -> p b t", t=2)[:, :, 1]
                    for e, eps in enumerate((1e-6, 1e-5)):
                        last = nc.gpsimd.tensor_scalar(ceps[:, e * B:(e + 1) * B], var, eps, None, ALU.add)
                    last.then_inc(c_eps, 1)
                    pool.wait_ge(c_eps, 1)
                    nc.gpsimd.tensor_tensor(crstd[:], ceps[:], half_neg[0:LC, :], ALU.pow).then_inc(c_rstd, 1)
                    pool.wait_ge(c_rstd, 1)
                for i in range(4 * quarter, 4 * quarter + 4):
                    b = i % B
                    last = nc.gpsimd.tensor_scalar(cnorm[:, i * C:(i + 1) * C], ctxn_sb[:, b * C:(b + 1) * C], cmv[:, 2 * b:2 * b + 1],
                                                   crstd[:, i:i + 1], ALU.subtract, ALU.mult)
                last.then_inc(c_norm, 1)

            def rstd_of(a):
                u = a.u
                a.wait(aggr_done, all_(a.n), carry=(pads_made, 1))
                a.wait(xn_done, all_(a.n), 2, carry=(pads_made, 1))
                nc.gpsimd.tensor_scalar(vareps[:, u:u + 1], mv[:, 2 * u + 1:2 * u + 2], a.k.eps, None, ALU.add).then_inc(eps_done, 1)
                a.wait(eps_done, all_(a.n))
                nc.gpsimd.tensor_tensor(rstd[:, u:u + 1], vareps[:, u:u + 1], half_neg[:, 0:1], ALU.pow).then_inc(rstd_done, 1)

            def context_of(a):
                if a.k.ctx is None:
                    return
                if a.k.ctx and a.first:
                    pool.wait_ge(c_out, 10)
                if a.k.ctx == 0 and a.first:
                    pool.wait_ge(ctx_in, 32)
                a.wait(proj_done, all_(a.n), 2)
                nc.gpsimd.tensor_copy(cslot[a.u][:], ctx_sb[a.k.ctx][:, a.span(LC)]).then_inc(ctx_copied, 1)

            def low_part(a):
                if not a.k.attn:
                    return
                u = a.u
                a.wait(pm_done, attn_(a.n))
                nc.gpsimd.tensor_tensor(part(parts[u], 2), both(pres[u]), part(parts[u], 1), ALU.subtract).then_inc(parts_done, 1)

            def keep_top(a):
                if a.k.kind != "topk":
                    return
                for g in range(G):
                    cols = slice(g * J * LC, (g + 1) * J * LC)
                    a.wait(s3_done[g], topk_(a.n), carry=(pads_made, 1))
                    nc.gpsimd.tensor_scalar(s3[:, cols], s3[:, cols], TAKEN, None, ALU.is_le).then_inc(mask_done[g], 1)
                    a.wait(mask_done[g], topk_(a.n))
                    a.wait(a_free[g], attn_(a.n))
                    a.wait(b_done[g], attn_(a.n), 1)
                    nc.gpsimd.tensor_tensor(pn[:, cols], ex[:, cols], s3[:, cols], ALU.mult).then_inc(p_done[g], 1)

            def step(done, now, nxt, aft, far):
                rope = aft is not None and aft.k.rope
                if aft is not None and not rope:
                    low_part(aft)
                if far is not None:
                    rstd_of(far)
                if rope:
                    low_part(aft)
                if far is not None:
                    context_of(far)
                if nxt is not None:
                    keep_top(nxt)

            pipeline(pool, step, lambda n, c: context((0, 5, 6, 7).index(c)) if n == 0 and c >= 0 else None)

        @block.scalar
        def _(sc):
            sc.dma_start(x_sb[0:L - SHIFT, :].rearrange("p (b c) -> p b c", b=B), x[:, SHIFT:L, :].rearrange("b t c -> t b c")).then_inc(x_in, 16)
            sc.dma_start(x_sb[L - SHIFT:L, :].rearrange("p (b c) -> p b c", b=B), x[:, 0:SHIFT, :].rearrange("b t c -> t b c")).then_inc(x_in, 16)
            sc.dma_start(w_sb[:, 0:WSPLIT[0]], wts[:, 0:WSPLIT[0]]).then_inc(w_in[0], 16)
            sc.wait_ge(small_in, 64)
            nc.scalar.activation(scond_sb[:], cond_sb[:], ACT.Silu).then_inc(silu_c, 1)
            sc.wait_ge(mods_made, 1)
            sc.preload_act_table(ACT.Exp)

            def context():
                for i in range(2):
                    sc.wait_ge(c_tr, i + 1)
                    nc.scalar.activation(ctx_sb[1][:, i * 4 * LC:(i + 1) * 4 * LC], bank_m[:, 0:4 * LC], ACT.Copy).then_inc(c_out, 1)
                kv = MODS.index("L2kv")
                for b in range(B):
                    if b % 4 == 0:
                        sc.wait_ge(c_tr, 3 + b // 4)
                    nc.scalar.activation(
                        ctx_sb[2][:, b * LC:(b + 1) * LC], bank_m[:, b % 4 * LC:(b % 4 + 1) * LC], ACT.Identity,
                        bias=mods[:, (NMOD + kv) * B + b:(NMOD + kv) * B + b + 1],
                        scale=mods[:, kv * B + b:kv * B + b + 1]).then_inc(c_out, 1)

            def modulate(a):
                a.wait(xnt_done, all_(a.n))
                a.wait(proj_done, all_(a.n), 2)
                if a.k.mod is None:
                    nc.scalar.activation(ht[a.u][:], bank_p[:, 0:L], ACT.Copy).then_inc(ht_done, 1)
                else:
                    nc.scalar.activation(ht[a.u][:], bank_p[:, 0:L], ACT.Identity, bias=mods[:, a.one((NMOD + a.k.mod) * B)],
                                         scale=mods[:, a.one(a.k.mod * B)]).then_inc(ht_done, 1)

            def qk_out(a):
                if not a.k.attn or a.k.rope:
                    return
                u, n, k = a.u, a.k.keys, a.k
                a.wait(qkp_done, attn_(a.n))
                a.wait(parts_done, attn_(a.n), 2)
                if a.first and a.n == 0:
                    sc.wait_ge(pads_made, 1)
                nc.scalar.activation(qk[u][:, 0:L], bank_p[:, 0:L], ACT.Identity, bias=bcol(k, "q"))
                nc.scalar.activation(qk[u][:, L:L + n], bank_p[:, L:L + n], ACT.Identity, bias=bcol(k, "k")).then_inc(qk_done, 1)

            def high_part(a):
                if not a.k.attn:
                    return
                u, base = a.u, attn_(a.n)
                a.wait(qk_done, base)
                a.wait_dma(parts_out, base, 1, 2)
                nc.scalar.activation(part(parts[u], 0), both(qk[u]), ACT.Copy).then_inc(ph_done, 1)

            def v_out(a):
                if not a.k.attn:
                    return
                u, n, k = a.u, a.k.keys, a.k
                a.wait(proj_done, all_(a.n))
                a.wait(o_done, all_(a.n), 2)
                for wd in range(k.windows):
                    rows = slice(64 * wd, 64 * wd + 64) if k.windows == 2 else slice(0, n)
                    dst = vwin[wd][u] if k.windows == 2 else vpad[u]
                    for j in range(J):
                        last = nc.scalar.activation(
                            dst[rows, :].rearrange("p (g r) -> p g r", g=G)[:, :, 72 * j:72 * j + D],
                            bank_m[rows, 128:256].rearrange("p (g j d) -> p g j d", g=G, j=J)[:, :, j, :], ACT.Copy)
                last.then_inc(v_done, 1)

            def maxima_out(a):
                if a.k.kind != "soft":
                    return
                a.wait(mpt_done, soft_(a.n))
                a.wait(b_done[G - 1], attn_(a.n), 1)
                nc.scalar.activation(mt[0:3 * H, :], bank_m[0:3 * H, 0:L // 2].bitcast(BF16), ACT.Copy).then_inc(mt_done, 1)

            def weights_out(a, g):
                a.wait(b_done[g], attn_(a.n))
                if g == 1:
                    a.wait(o_done, all_(a.n), 1)
                else:
                    a.wait(pv_done[g - 2 if g else 2], attn_(a.n), 0 if g else 1)
                if a.k.kind == "soft":
                    n, q = (128, 64) if a.k.windows == 2 else (a.k.keys, L)
                    nc.scalar.activation(pt[g % 2][0:n, 0:J * q], bank_b[g % 2][0:n, 0:J * q], ACT.Exp, scale=SCALE).then_inc(pt_done[g], 1)
                else:
                    nc.scalar.activation(pt[g % 2][0:LC, :], bank_b[g % 2][0:LC, :], ACT.Copy).then_inc(pt_done[g], 1)

            def top_exp(a, g):
                a.wait(tmr_done[g], topk_(a.n))
                a.wait(p_done[g], topk_(a.n), 1)
                for j in range(J):
                    h = g * J + j
                    last = nc.scalar.activation(ex[:, h * LC:(h + 1) * LC], bank_a[g % 2][:, j * LC:(j + 1) * LC], ACT.Exp,
                                                bias=nbias[:, h:h + 1], scale=SCALE)
                last.then_inc(a_free[g], 1)

            def hidden_out(a):
                if a.k.attn:
                    return
                u, k = a.u, a.k
                a.wait(proj_done, all_(a.n))
                a.wait(o_done, all_(a.n), 2)
                for c in range(CH):
                    last = nc.scalar.activation(act[u][:, c * L:(c + 1) * L], bank_b[u][:, c * L:(c + 1) * L], k.act, bias=bcol(k, "b1", c))
                last.then_inc(act_done, 1)

            def gated(a, dst, src):
                k = a.k
                if k.gate is not None:
                    return nc.scalar.activation(dst, src, ACT.Identity, bias=gbias[:, a.one(k.gate * B)],
                                                scale=mods[:, a.one((2 * NMOD + k.gate) * B)])
                if k.bias:
                    return nc.scalar.activation(dst, src, ACT.Identity, bias=bprime[:, a.n:a.n + 1])
                return nc.scalar.activation(dst, src, ACT.Copy)

            def result_out(a):
                a.wait(o_done, all_(a.n))
                if a.k.attn:
                    a.wait(otn_done, attn_(a.n), 1)
                    nc.scalar.activation(ot[:], bank_o[:, 0:2 * L], ACT.Copy).then_inc(o_free, 1)
                else:
                    a.wait(yb_done, all_(a.n), 1)
                    gated(a, yt[:], bank_o[:, 0:L]).then_inc(o_free, 1)

            def heads_out(a):
                if not a.k.attn:
                    return
                a.wait(ont_done, attn_(a.n))
                nc.scalar.activation(ont[:], bank_f[:, 0:L], ACT.Copy).then_inc(ontc_done, 1)

            def branch_out(a):
                if not a.k.attn:
                    return
                a.wait(y_done, attn_(a.n))
                gated(a, yt[:], bank_f[:, 0:L]).then_inc(yt_done, 1)

            def step(done, now, nxt, aft, far):
                attn = now is not None and now.k.attn
                top = nxt is not None and nxt.k.kind == "topk"
                rope = aft is not None and aft.k.rope
                if attn:
                    maxima_out(now)
                if attn:
                    weights_out(now, 0)
                if rope:
                    high_part(aft)
                if nxt is not None:
                    v_out(nxt)
                if attn:
                    weights_out(now, 1)
                if top:
                    top_exp(nxt, 0)
                if done is not None:
                    heads_out(done)
                if attn:
                    weights_out(now, 2)
                if done is not None:
                    branch_out(done)
                rows = nxt is not None and nxt.k.attn
                if rows and far is not None:
                    modulate(far)
                if top:
                    top_exp(nxt, 1)
                if attn:
                    weights_out(now, 3)
                if rows and far is not None:
                    qk_out(far)
                    if not far.k.rope:
                        high_part(far)
                if now is not None:
                    result_out(now)
                    if now.first and now.n == 0:
                        sc.wait_ge(mods_made, 2)
                        sc.wait_ge(gb_made, 1)
                if top:
                    top_exp(nxt, 2)
                    top_exp(nxt, 3)
                if nxt is not None:
                    hidden_out(nxt)
                if far is not None and not rows:
                    modulate(far)
                    qk_out(far)
                    if not far.k.rope:
                        high_part(far)

            pipeline(sc, step, lambda n, c: context() if (n, c) == (FIRST_MLP, 0) else None)

        @block.vector
        def _(ve):
            ve.wait_ge(small_in, 64)
            nc.vector.tensor_copy(identb[:], ident)
            nc.vector.tensor_copy(sel[:].rearrange("p (h n) -> p h n", h=H), selcol[:, :, None].broadcast_to([128, H, 128])).then_inc(consts_made, 1)
            ve.wait_ge(ctx_in, 32)
            for b in range(B):
                last = nc.vector.bn_stats(cstat[:, 6 * b:6 * b + 6], ctxn_sb[:, b * C:(b + 1) * C])
            last.then_inc(c_stat, 1)
            ve.wait_ge(c_stat, 1)
            for b in range(B):
                last = nc.vector.bn_aggr(cmv[:, 2 * b:2 * b + 2], cstat[:, 6 * b:6 * b + 6])
            last.then_inc(c_aggr, 1)

            def add_biases(bank, lo, hi):
                return nc.vector.tensor_tensor(
                    mods[:, lo * B:hi * B].rearrange("p (v b) -> p v b", b=B), bank[:, lo * B:hi * B].rearrange("p (v b) -> p v b", b=B),
                    bmod_sb[:, lo:hi, None].broadcast_to([128, hi - lo, B]), ALU.add)

            ve.wait_ge(mods_mm, 1)
            for v in FIRST:
                last = add_biases(bank_p, v, v + 1)
            last.then_inc(mods_add, 1)
            ve.wait_ge(mods_add, 1)
            nc.vector.tensor_scalar(mods[:, 0:B], mods[:, 0:B], 1.0, None, ALU.add).then_inc(mods_made, 1)
            ve.wait_ge(x_in, 32)
            nc.vector.tensor_copy(rec[:, 0:1], ident[:, 0:1]).then_inc(xadd_done, 1)

            def other_modulations():
                ve.wait_ge(mods_mm, 2)
                for lo, hi in ((1, NMOD), (NMOD + 1, 2 * NMOD), (2 * NMOD + 1, NVEC)):
                    last = add_biases(bank_o, lo, hi)
                last.then_inc(mods_add, 1)
                ve.wait_ge(mods_add, 2)
                nc.vector.tensor_scalar(mods[:, B:NMOD * B], mods[:, B:NMOD * B], 1.0, None, ALU.add).then_inc(mods_made, 1)

            def stats(a):
                u = a.u
                if a.n:
                    a.wait(xadd_done, xadd_(a.n - 1))
                a.wait(rstd_done, all_(a.n), 2)
                nc.vector.bn_stats(stat[:, 6 * u:6 * u + 6], x_sb[:, a.span(C)]).then_inc(st_done, 1)
                a.wait(st_done, all_(a.n), carry=(x_in, 32))
                nc.vector.bn_aggr(mv[:, 2 * u:2 * u + 2], stat[:, 6 * u:6 * u + 6]).then_inc(aggr_done, 1)

            def normalise(a):
                u = a.u
                a.wait(rstd_done, all_(a.n))
                a.wait(xnt_done, all_(a.n), 2)
                nc.vector.tensor_scalar(xn[u][:], x_sb[:, a.span(C)], mv[:, 2 * u:2 * u + 1], rstd[:, u:u + 1],
                                        ALU.subtract, ALU.mult).then_inc(xn_done, 1)

            def rotate(a):
                if not (a.k.attn and a.k.rope):
                    return
                n = a.k.keys
                parts = [(0, L, "cos", "sin")]
                parts.append((L, n, "cosc", "sinc") if a.k.ctx is not None else (L, n, "cos", "sin"))
                a.wait(qkp_done, attn_(a.n))
                a.wait(qk_done, attn_(a.n), 1)
                for at, m, c, s in parts:
                    last = nc.vector.tensor_tensor(ropec[:, at:at + m], bank_p[:, at:at + m], c_sb[:, CCOL[c]:CCOL[c] + m], ALU.mult)
                last.then_inc(ropec_done, 1)
                for at, m, c, s in parts:
                    last = nc.vector.tensor_tensor(ropes[:, at:at + m], bank_p[:, 256 + at:256 + at + m], c_sb[:, CCOL[s]:CCOL[s] + m], ALU.mult)
                last.then_inc(ropes_done, 1)

            def rotate_sum(a):
                if not (a.k.attn and a.k.rope):
                    return
                n, base = L + a.k.keys, rope_(a.n)
                a.wait(ropec_done, base)
                a.wait(ropes_done, base)
                a.wait(parts_done, attn_(a.n), 2)
                nc.vector.tensor_tensor(qk[a.u][:, 0:n], ropec[:, 0:n], ropes[:, 0:n], ALU.add).then_inc(qk_done, 1)

            def split_qk(a):
                if not a.k.attn:
                    return
                u, base = a.u, attn_(a.n)
                a.wait(ph_done, base)
                a.wait(parts_done, base, 2)
                nc.vector.tensor_tensor(both(pres[u]), both(qk[u]), part(parts[u], 0), ALU.subtract).then_inc(pr_done, 1)
                a.wait(pr_done, base)
                nc.vector.tensor_copy(part(parts[u], 1), both(pres[u])).then_inc(pm_done, 1)

            def spread(a):
                if not a.k.attn:
                    return
                u = a.u
                a.wait_dma(q_in, attn_(a.n), len(Q_SLOTS))
                a.wait(b_done[G - 1], attn_(a.n), 2)
                for j in range(2):
                    last = nc.vector.tensor_scalar(qbd[u][:, j * S * L:(j + 1) * S * L], qst[u][:], headmask[j], None, ALU.mult)
                last.then_inc(qbd_done, 1)

            def maximum(a, g):
                n = L // a.k.windows if a.k.ctx is None else LC
                a.wait(a_done[g], attn_(a.n))
                a.wait(mparts_done, soft_(a.n), 1)
                nc.vector.tensor_reduce(nmax[:, g * J:(g + 1) * J], heads4(bank_a[g % 2][:, 0:J * n], n), AX, ALU.max,
                                        negate=True).then_inc(a_free[g], 1)

            def split(a):
                base = soft_(a.n)
                for g in range(G):
                    a.wait(a_free[g], attn_(a.n))
                a.wait(mpt_done, base, 1)
                nc.vector.tensor_copy(mparts[:, 0:H], nmax[:]).then_inc(m1_done, 1)
                a.wait(m1_done, base)
                nc.vector.tensor_tensor(mres[:], nmax[:], mparts[:, 0:H], ALU.subtract).then_inc(r1_done, 1)
                a.wait(r1_done, base)
                nc.vector.tensor_copy(mparts[:, H:2 * H], mres[:]).then_inc(m2_done, 1)
                a.wait(m2_done, base)
                nc.vector.tensor_tensor(mparts[:, 2 * H:3 * H], mres[:], mparts[:, H:2 * H], ALU.subtract).then_inc(mparts_done, 1)

            def take_top(a, g):
                base = topk_(a.n)
                heads = range(g * J, (g + 1) * J)
                a.wait(a_done[g], attn_(a.n), carry=(x_in, 32))
                a.wait(p_done[g], base, 1, carry=(x_in, 32))
                for h in heads:
                    last = nc.vector.max(top[:, 16 * h:16 * h + 8], bank_a[g % 2][:, h % J * LC:(h % J + 1) * LC])
                last.then_inc(t8_done[g], 1)
                a.wait(t8_done[g], base)
                nc.vector.tensor_scalar(nbias[:, g * J:(g + 1) * J], top[:].rearrange("p (h e) -> p h e", e=16)[:, g * J:(g + 1) * J, 0],
                                        -SCALE, None, ALU.mult)
                for h in heads:
                    last = nc.vector.match_replace(s3[:, h * LC:(h + 1) * LC], top[:, 16 * h:16 * h + 8],
                                                   bank_a[g % 2][:, h % J * LC:(h % J + 1) * LC], TAKEN)
                last.then_inc(tmr_done[g], 1)
                a.wait(tmr_done[g], base, carry=(x_in, 32))
                for h in heads:
                    last = nc.vector.max(top[:, 16 * h + 8:16 * h + 16], s3[:, h * LC:(h + 1) * LC])
                last.then_inc(t16_done[g], 1)
                a.wait(t16_done[g], base, carry=(x_in, 32))
                for h in heads:
                    last = nc.vector.match_replace(s3[:, h * LC:(h + 1) * LC], top[:, 16 * h + 8:16 * h + 16],
                                                   s3[:, h * LC:(h + 1) * LC], TAKEN)
                last.then_inc(s3_done[g], 1)

            def row_stage(a, g):
                if a.k.kind == "soft":
                    maximum(a, g)
                elif a.k.kind == "topk":
                    take_top(a, g)

            def divide(a):
                if not a.k.attn:
                    return
                a.wait(otn_done, attn_(a.n))
                f = bank_f[:, 0:4 * 64].rearrange("p (g r) -> p g r", g=G)
                nc.vector.reciprocal(rec[:].rearrange("p (g j) -> p g j", g=G), f[:, :, 32:36]).then_inc(rec_done, 1)
                a.wait(rec_done, attn_(a.n))
                nc.vector.tensor_tensor(
                    on[:].rearrange("p (g j d) -> p g j d", g=G, j=J), f[:, :, 0:32].rearrange("p g (j d) -> p g j d", d=D),
                    rec[:].rearrange("p (g j) -> p g j", g=G)[:, :, :, None].broadcast_to([128, G, J, D]), ALU.mult).then_inc(on_done, 1)

            def add(a):
                a.wait(yb_done, all_(a.n))
                nc.vector.tensor_tensor(x_sb[:, a.span(C)], x_sb[:, a.span(C)], bank_f[:, 0:C], ALU.add).then_inc(xadd_done, 1)

            def hidden_gate(a):
                if a.k.attn or a.k.act != ACT.Silu:
                    return
                u = a.u
                a.wait(act_done, mlp_(a.n))
                for c in range(CH):
                    last = nc.vector.scalar_tensor_tensor(
                        out=hid[u][:, c * L:(c + 1) * L], in0=bank_a[u][:, c * L:(c + 1) * L], scalar=bcol(a.k, "b1", CH + c),
                        in1=act[u][:, c * L:(c + 1) * L], op0=ALU.add, op1=ALU.mult)
                last.then_inc(hid_done, 1)

            def attention_biases():
                ve.wait_ge(bp_mm, 1)
                for i, n in enumerate(BIASED):
                    nc.vector.tensor_tensor(bprime[:, n:n + 1], bank_f[:, i:i + 1], bcol(BLOCKS[n], "o"), ALU.add)
                for n, k in enumerate(BLOCKS):
                    if not k.attn:
                        last = nc.vector.tensor_copy(bprime[:, n:n + 1], bcol(k, "b2"))
                last.then_inc(bp_made, 1)
                ve.wait_ge(bp_made, 1)
                for n, k in enumerate(BLOCKS):
                    if k.gate is not None:
                        gate = mods[:, (2 * NMOD + k.gate) * B:(2 * NMOD + k.gate + 1) * B]
                        last = nc.vector.tensor_scalar(gbias[:, k.gate * B:(k.gate + 1) * B], gate, bprime[:, n:n + 1], None, ALU.mult)
                last.then_inc(gb_made, 1)

            def step(done, now, nxt, aft, far):
                if now is not None and now.first and now.n == 0:
                    attention_biases()
                rope = aft is not None and aft.k.rope
                if aft is not None:
                    if rope:
                        rotate(aft)
                    else:
                        split_qk(aft)
                if far is not None:
                    stats(far)
                if rope:
                    rotate_sum(aft)
                if done is not None:
                    divide(done)
                if nxt is not None:
                    spread(nxt)
                if rope:
                    split_qk(aft)
                if nxt is not None:
                    row_stage(nxt, 0)
                if far is not None:
                    normalise(far)
                if nxt is not None:
                    row_stage(nxt, 1)
                soft = nxt is not None and nxt.k.kind == "soft"
                if done is not None and not soft:
                    add(done)
                if nxt is not None:
                    row_stage(nxt, 2)
                    row_stage(nxt, 3)
                    hidden_gate(nxt)
                if soft:
                    split(nxt)
                    if done is not None:
                        add(done)

            pipeline(ve, step, lambda n, c: other_modulations() if (n, c) == (0, -2) else None)

        @block.tensor
        def _(pe):
            def modulations(vecs, bank):
                for v in vecs:
                    m = v % NMOD if v < 2 * NMOD else v - 2 * NMOD
                    src = cond_sb if MODS[m].startswith("L3") else scond_sb
                    at = VECS.index(v) * C
                    last = nc.tensor.matmul(bank[:, v * B:(v + 1) * B], wmod_sb[:, at:at + C], src[:], start=True, stop=True)
                last.then_inc(mods_mm, 1)

            pe.wait_ge(wmod_in[0], 16)
            pe.wait_ge(silu_c, 1)
            modulations(FIRST, bank_p)
            pe.wait_ge(w_in[0], 16)
            pe.wait_ge(mods_made, 1)
            pe.wait_ge(consts_made, 1)

            def other_modulations():
                pe.wait_ge(wmod_in[1], 16)
                modulations(VECS[len(FIRST):], bank_o)

            def context():
                n = FIRST_MLP
                pe.wait_ge(v_done, attn_(n))
                pe.wait_ge(mt_done, soft_(n))
                for i in range(4):
                    pe.wait_ge(c_norm, i + 1)
                    if i:
                        pe.wait_ge(c_out, (0, 1, 2, 6)[i])
                    for r in range(4):
                        at = (4 * i + r) * C
                        last = nc.tensor.transpose(bank_m[:, r * LC:(r + 1) * LC], cnorm[:, at:at + C], c_sb[0:LC, 0:LC])
                    last.then_inc(c_tr, 1)

            def rest_of_setup():
                for s in w_in[1:]:
                    pe.wait_ge(s, 16)
                pe.wait_ge(mods_made, 2)
                for i, n in enumerate(BIASED):
                    last = nc.tensor.matmul(bank_f[:, i:i + 1], w(BLOCKS[n], "o"), bcol(BLOCKS[n], "v"), start=True, stop=True)
                last.then_inc(bp_mm, 1)
                pe.wait_ge(bp_made, 1)

            def transpose_x(a):
                a.wait(xn_done, all_(a.n))
                a.wait(ht_done, all_(a.n), 1)
                if a.first:
                    if a.n and BLOCKS[a.n - 1].attn:
                        pe.wait_ge(qk_done, attn_(a.n))
                elif a.k.attn:
                    a.wait(qk_done, attn_(a.n), 1)
                nc.tensor.transpose(bank_p[:, 0:L], xn[a.u][:], ident).then_inc(xnt_done, 1)

            def project_qk(a):
                if not a.k.attn:
                    return
                u, k, n = a.u, a.k, a.k.keys
                a.wait(ht_done, all_(a.n))
                if k.ctx is not None:
                    a.wait(ctx_copied, cross_(a.n))
                src = cslot[u][:, 0:n] if k.ctx is not None else ht[u][:]
                last = nc.tensor.matmul(bank_p[:, 0:L], w(k, "q"), ht[u][:], start=True, stop=True)
                last = nc.tensor.matmul(bank_p[:, L:L + n], w(k, "k"), src, start=True, stop=True)
                if k.rope:
                    nc.tensor.matmul(bank_p[:, 256:256 + L], w(k, "qr"), ht[u][:], start=True, stop=True)
                    last = nc.tensor.matmul(bank_p[:, 384:384 + n], w(k, "kr"), src, start=True, stop=True)
                last.then_inc(qkp_done, 1)

            def project_v(a):
                if not a.k.attn:
                    return
                u, k, n = a.u, a.k, a.k.keys
                src = cslot[u][:, 0:n] if k.ctx is not None else ht[u][:]
                a.wait(v_done, attn_(a.n), 1)
                if a.first:
                    if a.n == FIRST_MLP + 1:
                        pe.wait_ge(c_out, 10)
                    if a.n:
                        pe.wait_ge(mt_done, soft_(a.n))
                elif k.kind == "soft":
                    a.wait(mt_done, soft_(a.n), 1)
                nc.tensor.matmul(bank_m[0:n, 128:256], src, w(k, "v"), start=True, stop=True).then_inc(proj_done, 1)

            def scores_by_row(a, g):
                u, k = a.u, a.k
                nw = k.windows
                n = L // nw if k.ctx is None else LC
                if g == 0:
                    a.wait(qbd_done, attn_(a.n))
                    a.wait_dma(k_in, attn_(a.n), len(K_SLOTS))
                if a.first and g == 0 and a.n and BLOCKS[a.n - 1].act == ACT.Silu:
                    pe.wait_ge(hid_done, mlp_(a.n))
                a.wait(a_free[g - 2], attn_(a.n), 0 if g >= 2 else 1)
                for wd in range(nw):
                    rows = slice(64 * wd, 64 * wd + 64) if nw == 2 else slice(0, L)
                    for j in range(J):
                        s, hj = g * 2 + j // 2, j % 2
                        last = nc.tensor.matmul(
                            bank_a[g % 2][rows, j * n:(j + 1) * n], qbd[u][:, (hj * S + s) * L + rows.start:(hj * S + s) * L + rows.stop],
                            kst[u][:, s * L + wd * n:s * L + wd * n + n], start=True, stop=True)
                last.then_inc(a_done[g], 1)

            def maxima_in(a):
                if a.k.kind != "soft":
                    return
                a.wait(mparts_done, soft_(a.n), carry=(consts_made, 1))
                a.wait(v_done, attn_(a.n), carry=(consts_made, 1))
                nc.tensor.transpose(bank_m[0:3 * H, 0:L // 2].bitcast(BF16), mparts[:], identb[:]).then_inc(mpt_done, 1)

            def scores_by_key(a, g):
                u, k = a.u, a.k
                bank = bank_b[g % 2]
                if a.first and g < 2 and a.n and not BLOCKS[a.n - 1].attn:
                    pe.wait_ge(act_done, mlp_(a.n))
                a.wait(pt_done[g - 2], attn_(a.n), 0 if g >= 2 else 1)
                if k.kind == "topk":
                    a.wait(p_done[g], topk_(a.n))
                    for j in range(J):
                        h = g * J + j
                        last = nc.tensor.transpose(bank[0:LC, j * L:(j + 1) * L], pn[:, h * LC:(h + 1) * LC], ident)
                    last.then_inc(b_done[g], 1)
                    return
                nw = k.windows
                n, q = (L // nw if k.ctx is None else LC), L // nw
                for wd in range(nw):
                    for s in (2 * g, 2 * g + 1):
                        queries = qbd[u][:].rearrange("p (j s t) -> p j s t", j=2, s=S)[:, :, s, wd * q:(wd + 1) * q]
                        at = s % 2 * 2 * q
                        nc.tensor.matmul(bank[n * wd:n * wd + n, at:at + 2 * q], kst[u][:, s * L + n * wd:s * L + n * wd + n], queries,
                                         start=s == 2 * g, stop=False, skip_group_check=True)

            def less_maxima(a, g):
                k = a.k
                if k.kind == "topk":
                    return
                nw = k.windows
                n, q = (L // nw if k.ctx is None else LC), L // nw
                if g == 0:
                    a.wait(mt_done, soft_(a.n), carry=(consts_made, 1))
                for wd in range(nw):
                    for j in range(J):
                        h = g * J + j
                        last = nc.tensor.matmul(bank_b[g % 2][n * wd:n * wd + n, j * q:(j + 1) * q], sel[:, h * 128:h * 128 + n],
                                                mt[:, wd * q:(wd + 1) * q], start=False, stop=True, skip_group_check=True)
                last.then_inc(b_done[g], 1)

            def weigh(a, g):
                u, k = a.u, a.k
                n = k.keys
                q = L // k.windows
                a.wait(pt_done[g], attn_(a.n))
                if g == 0:
                    a.wait(v_done, attn_(a.n))
                    a.wait(o_free, all_(a.n), 1)
                out_rows = slice(64 * (g % 2), 64 * (g % 2) + 64)
                for wd in range(k.windows):
                    at = g // 2 * L + wd * q
                    v = vwin[wd][u] if k.windows == 2 else vpad[u]
                    for j in range(J):
                        h = g * J + j
                        last = nc.tensor.matmul(bank_o[out_rows, at:at + q], v[0:n, h * 64:(h + 1) * 64], pt[g % 2][0:n, j * q:(j + 1) * q],
                                                start=(j == 0), stop=(j == J - 1), skip_group_check=True)
                last.then_inc(pv_done[g] if g < G - 1 else o_done, 1)

            def sums_back(a):
                if not a.k.attn:
                    return
                a.wait(o_free, all_(a.n))
                a.wait(xadd_done, xadd_(a.n), 1)
                for i in range(2):
                    last = nc.tensor.transpose(bank_f[:, i * L:(i + 1) * L], ot[:, i * L:(i + 1) * L], ident)
                last.then_inc(otn_done, 1)

            def heads_back(a):
                if not a.k.attn:
                    return
                a.wait(on_done, attn_(a.n))
                nc.tensor.transpose(bank_f[:, 0:L], on[:], ident).then_inc(ont_done, 1)

            def project_out(a):
                if not a.k.attn:
                    return
                a.wait(ontc_done, attn_(a.n))
                nc.tensor.matmul(bank_f[:, 0:L], w(a.k, "o"), ont[:], start=True, stop=True).then_inc(y_done, 1)

            def branch_back(a):
                if a.k.attn:
                    a.wait(yt_done, attn_(a.n))
                else:
                    a.wait(o_free, all_(a.n))
                    a.wait(xadd_done, xadd_(a.n), 1)
                nc.tensor.transpose(bank_f[:, 0:C], yt[:], ident).then_inc(yb_done, 1)

            def hidden(a):
                if a.k.attn:
                    return
                u, k = a.u, a.k
                a.wait(ht_done, all_(a.n))
                a.wait(act_done, mlp_(a.n), 2)
                if k.act == ACT.Silu:
                    a.wait(hid_done, mlp_(a.n), 2)
                if a.i is None and a.c < 2 and BLOCKS[a.n - 1].attn:
                    pe.wait_ge(pt_done[2 + u], attn_(a.n))
                    pe.wait_ge(a_free[2 + u], attn_(a.n))
                if k.act == ACT.Silu:
                    for c in range(CH):
                        nc.tensor.matmul(bank_a[u][:, c * L:(c + 1) * L], w(k, "w1", C, HID + c * C), ht[u][:], start=True, stop=True)
                for c in range(CH):
                    last = nc.tensor.matmul(bank_b[u][:, c * L:(c + 1) * L], w(k, "w1", C, c * C), ht[u][:], start=True, stop=True)
                last.then_inc(proj_done, 1)

            def down(a):
                u, k = a.u, a.k
                if k.act == ACT.Silu:
                    a.wait(hid_done, mlp_(a.n))
                else:
                    a.wait(act_done, mlp_(a.n))
                src = hid[u] if k.act == ACT.Silu else act[u]
                a.wait(o_free, all_(a.n), 1)
                for c in range(CH):
                    last = nc.tensor.matmul(bank_o[:, 0:L], w(k, "w2", C, c * C), src[:, c * L:(c + 1) * L], start=(c == 0), stop=(c == CH - 1))
                last.then_inc(o_done, 1)

            def step(done, now, nxt, aft, far):
                attn = now is not None and now.k.attn
                rows = nxt is not None and nxt.k.attn
                top = rows and nxt.k.kind == "topk"
                soft = rows and not top
                if now is not None and now.first and now.n == 0:
                    rest_of_setup()
                if attn and not top:
                    scores_by_key(now, 0)
                    maxima_in(now)
                if done is not None:
                    sums_back(done)
                if attn and not top:
                    scores_by_key(now, 1)
                if top:
                    scores_by_row(nxt, 0)
                    scores_by_row(nxt, 1)
                    if attn:
                        scores_by_key(now, 0)
                        scores_by_key(now, 1)
                        maxima_in(now)
                if attn:
                    less_maxima(now, 0)
                if nxt is not None:
                    project_v(nxt)
                if attn:
                    less_maxima(now, 1)
                if attn:
                    weigh(now, 0)
                elif now is not None:
                    down(now)
                if soft:
                    scores_by_row(nxt, 0)
                if done is not None:
                    heads_back(done)
                if soft:
                    scores_by_row(nxt, 1)
                if attn:
                    scores_by_key(now, 2)
                    less_maxima(now, 2)
                if attn:
                    weigh(now, 1)
                if soft:
                    scores_by_row(nxt, 2)
                if done is not None:
                    project_out(done)
                if rows and far is not None:
                    transpose_x(far)
                if attn:
                    scores_by_key(now, 3)
                if soft:
                    scores_by_row(nxt, 3)
                if attn:
                    less_maxima(now, 3)
                if top:
                    scores_by_row(nxt, 2)
                if done is not None:
                    branch_back(done)
                if rows and far is not None:
                    project_qk(far)
                if attn:
                    weigh(now, 2)
                if top:
                    scores_by_row(nxt, 3)
                if attn:
                    weigh(now, 3)
                if nxt is not None and not rows:
                    hidden(nxt)
                if far is not None and not rows:
                    transpose_x(far)
                    project_qk(far)

            def extra(n, c):
                if (n, c) == (0, -2):
                    other_modulations()
                if (n, c) == (FIRST_MLP, 0):
                    context()

            pipeline(pe, step, extra)


FEATURES = np.array([D * (2 * s + r // D) + r % D for r in range(R) for s in range(S)])


def shape_constants():
    c = np.zeros((128, CTOT), np.float32)
    p = np.arange(128)
    c[:, 0:128] = np.eye(128)
    c[p, CCOL["headmask"] + p % R // D] = 1.0
    r = np.arange(3 * H)
    c[r, CCOL["sel"] + r % H] = 1.0
    half = D // 2
    inv = (1.0 / np.float32(10000.0) ** (np.arange(half, dtype=np.float32) / np.float32(half))).astype(np.float32)
    feature = FEATURES % D
    sign = np.where(feature < half, -1.0, 1.0).astype(np.float32)[:, None]
    for cs, sn, pos in (("cos", "sin", (np.arange(L) + SHIFT) % L), ("cosc", "sinc", np.arange(LC))):
        ang = pos.astype(np.float32)[None, :] * inv[feature % half][:, None]
        c[:, CCOL[cs]:CCOL[cs] + len(pos)] = np.cos(ang)
        c[:, CCOL[sn]:CCOL[sn] + len(pos)] = np.sin(ang) * sign
    return c


def kernel(**inputs):
    import concourse.bacc as bacc
    from concourse.bass_utils import run_bass_kernel_spmd

    a = {k: np.asarray(v) for k, v in inputs.items()}

    def l0(s): return a["L0_xcond_" + s]
    def l1(s): return a["L1_xcond_" + s]
    def l2(s): return a["L2_xcond_" + s]
    def l3(s): return a["L3_xcond_" + s]

    def cut(m, i): return m[..., i * C:(i + 1) * C]

    ada, mod, l2q, l2k = (l0("w_ada"), l0("b_ada")), (l1("W_mod"), l1("b_mod")), (l2("Wss_q"), l2("bss_q")), (l2("Wss_kv"), l2("bss_kv"))
    l3n = [(l3(f"ln{i}_w").T, l3(f"ln{i}_b")) for i in (1, 2, 3)]
    scales = [(ada, 1), (ada, 4), (ada, 7), (mod, 1), (mod, 4), (l2q, 0), (l2k, 0)] + [(m, 0) for m in l3n]
    shifts = [(ada, 0), (ada, 3), (ada, 6), (mod, 0), (mod, 3), (l2q, 1), (l2k, 1)] + [(m, 1) for m in l3n]
    gates = [(ada, 2), (ada, 5), (ada, 8), (mod, 2), (mod, 5)]
    vectors = scales + shifts + gates
    wmod = np.concatenate([cut(vectors[v][0][0], vectors[v][1]) for v in VECS], axis=1)
    bmod = np.stack([cut(m[1], i) for m, i in scales + shifts + gates], axis=1)

    swap = (np.arange(C) // D) * D + (np.arange(C) + D // 2) % D

    def down(m): return m.reshape(CH, C, C).transpose(1, 0, 2).reshape(C, HID)

    def cols(v): return list(v.reshape(-1, C))

    def biases(v, n):
        return [u[FEATURES] if i < n else u for i, u in enumerate(cols(v))]

    def spread(m, n, extra=slice(None)):
        return np.concatenate([cut(m, i)[:, extra][:, FEATURES] if i < n else cut(m, i) for i in range(m.shape[1] // C)], axis=1)

    qkv3 = l3("qkv_w").T
    w = {
        "sa0": [spread(l0("w_qkv"), 2), l0("w_so")],
        "xa0": [spread(l0("w_q"), 1), spread(l0("w_kv"), 1), l0("w_co")],
        "ml0": [l0("w_m1"), down(l0("w_m2"))],
        "sa1": [spread(l1("W_qkv"), 2), l1("W_proj")],
        "xa1": [spread(l1("W_qc"), 1), spread(l1("W_kvc"), 1), l1("W_cproj")],
        "ml1": [l1("W_mlp1"), down(l1("W_mlp2"))],
        "xa2": [spread(l2("Wq"), 1), spread(l2("Wkv"), 1), l2("Wp")],
        "sa3": [spread(qkv3[:, 0:2 * C], 2), spread(qkv3[:, 0:2 * C], 2, swap), cut(qkv3, 2), l3("sa_out_w").T],
        "xa3": [spread(l3("q_w").T, 1), spread(l3("k_w").T, 1), spread(l3("q_w").T, 1, swap), spread(l3("k_w").T, 1, swap),
                l3("v_w").T, l3("ca_out_w").T],
        "ml3": [l3("ffn_w1").T, down(l3("ffn_w2").T)],
    }
    bs = {
        "sa0": biases(l0("b_qkv"), 2) + cols(l0("b_so")), "xa0": biases(l0("b_q"), 1) + biases(l0("b_kv"), 1) + cols(l0("b_co")),
        "ml0": cols(l0("b_m1")) + cols(l0("b_m2")), "sa1": biases(l1("b_qkv"), 2) + cols(l1("b_proj")),
        "xa1": biases(l1("b_qc"), 1) + biases(l1("b_kvc"), 1) + cols(l1("b_cproj")), "ml1": cols(l1("b_mlp1")) + cols(l1("b_mlp2")),
        "xa2": biases(l2("bq"), 1) + biases(l2("bkv"), 1) + cols(l2("bp")), "sa3": [], "xa3": [],
        "ml3": cols(l3("ffn_b1")) + cols(l3("ffn_b2")),
    }
    ctx = a["ctx_1024"]
    arrays = {
        "x": a["x"], "cond_t": a["cond_1024"].T, "ctx_n": ctx, "ctx_t": ctx.transpose(2, 0, 1).reshape(C, B * LC),
        "wmod": wmod, "bmod": bmod, "wts": np.concatenate([m for k in BLOCKS for m in w[k.name]], axis=1),
        "bias": np.stack([v for k in BLOCKS for v in bs[k.name]], axis=1), "consts": shape_constants(),
    }
    arrays = {f"in_{k}": np.ascontiguousarray(v) for k, v in arrays.items()}
    nc = bacc.Bacc("TRN2", target_bir_lowering=False, num_devices=1)
    args = [nc.dram_tensor(k, v.shape, mybir.dt.from_np(v.dtype), kind="ExternalInput").ap() for k, v in arrays.items()]
    args.append(nc.dram_tensor("out_0", (B, L, C), F32, kind="ExternalOutput").ap())
    args.append(nc.dram_tensor("scratch", (2, 2, PARTS, C, L), BF16, kind="Internal").ap())
    build(nc, *args)
    r = run_bass_kernel_spmd(nc, [arrays], core_ids=[0])
    return r.results[0]["out_0"]
```
